# Optimizing a Trainium2 kernel written in Bass

```python
import numpy as np
import jax
import jax.numpy as jnp

def _softmax(x, axis=-1):
    return jax.nn.softmax(x, axis=axis)

def _gelu(x):
    return jax.nn.gelu(x, approximate=True)

def _silu(x):
    return jax.nn.silu(x)

def _sigmoid(x):
    return jax.nn.sigmoid(x)

def _layernorm(x, axis=-1, eps=1e-05):
    m = jnp.mean(x, axis=axis, keepdims=True)
    v = jnp.var(x, axis=axis, keepdims=True)
    return (x - m) / jnp.sqrt(v + eps)

def _scatter_add(tgt, idx, src, axis=0):
    return tgt.at[idx].add(src)

def _segment_sum(src, seg, n):
    return jax.ops.segment_sum(src, seg, n)
kernel_name = 'mk_perceiver_d1_seqx_r8_e86992'

def setup_inputs(seed: int=0):
    np.random.seed(seed)
    _w = jnp.asarray

    def _rec_inputs():
        import jax
        import jax.numpy as jnp
        _rk = jax.random.key(seed)
        x = -4.161e-06 + 1 * jax.random.normal(jax.random.fold_in(_rk, 1), (1, 64, 256), jnp.float32)
        _lenS = 64 - jax.random.randint(jax.random.fold_in(_rk, 7), (1,), 0, max(1, 64 // 4) + 1, jnp.int32)
        _lenS2 = 6272 - jax.random.randint(jax.random.fold_in(_rk, 8), (1,), 0, max(1, 6272 // 4) + 1, jnp.int32)
        _ctx_2048P = jax.random.normal(jax.random.fold_in(_rk, 11), (1, 16, 256), jnp.float32)
        _ctx_2048c = jax.random.dirichlet(jax.random.fold_in(_rk, 511), 0.3 * jnp.ones((16,), jnp.float32), (1, 6272))
        _ctx_2048t = jnp.einsum('bsk,bkd->bsd', _ctx_2048c, _ctx_2048P)
        _ctx_2048t = _ctx_2048t * jax.lax.rsqrt(jnp.mean(jnp.square(_ctx_2048t)) + 1e-12) * 0.953939
        ctx_2048 = -0.000192764 + 0.999654 * (_ctx_2048t + 0.3 * jax.random.normal(jax.random.fold_in(_rk, 611), (1, 6272, 256), jnp.float32))
        return (x, ctx_2048)
    x, ctx_2048 = _rec_inputs()

    def _L0_xattn_setup():
        import jax, jax.numpy as jnp
        import numpy as np
        FP8_MAX = 448.0
        EPS = 1e-05

        def _fp8_roundtrip(x):
            return x.astype(jnp.float8_e4m3fn).astype(jnp.float32)

        def _div_clamp_fp8(x, scale):
            y = jnp.clip(x.astype(jnp.float32) / scale, -FP8_MAX, FP8_MAX)
            y = y.astype(jnp.bfloat16).astype(jnp.float32)
            return _fp8_roundtrip(y)

        def _ln(x, w, b):
            mu = jnp.mean(x, axis=-1, keepdims=True)
            var = jnp.mean(jnp.square(x - mu), axis=-1, keepdims=True)
            return (x - mu) * jax.lax.rsqrt(var + EPS) * w + b

        def _fp8_linear_pertensor(x, wq, w_scale, in_scale):
            xq = _div_clamp_fp8(x, in_scale)
            return jnp.einsum('bsi,oi->bso', xq * in_scale, wq) * w_scale

        def _gqa(q, k, v):
            scale = 1.0 / np.sqrt(q.shape[-1])
            scores = jnp.einsum('bsghd,btgd->bghst', q, k) * scale
            p = jax.nn.softmax(scores, axis=-1)
            return jnp.einsum('bghst,btgd->bsghd', p, v)
        key = jax.random.key(seed)
        ks = jax.random.split(key, 8)
        B, S, SC, H, NH, G, D = (2, 256, 64, 256, 16, 8, 128)

        def qw(k, out_f, in_f):
            w = jax.random.normal(k, (out_f, in_f), jnp.float32) * 0.02
            sc = jnp.max(jnp.abs(w)) / FP8_MAX
            return (_fp8_roundtrip(w / sc), sc.astype(jnp.float32))
        wq, wq_s = qw(ks[0], NH * D, H)
        wqx, wqx_s = qw(ks[1], NH * D, H)
        wk, wk_s = qw(ks[2], G * D, H)
        wv, wv_s = qw(ks[3], G * D, H)
        wproj, wp_s = qw(ks[4], H, 2 * NH * D)
        return {'hidden_states': jax.random.normal(ks[5], (B, S, H), jnp.float32), 'cond': jax.random.normal(ks[6], (B, SC, H), jnp.float32), 'ln_w': jnp.ones((H,), jnp.float32), 'ln_b': jnp.zeros((H,), jnp.float32), 'wq': wq, 'wq_scale': wq_s, 'q_in_scale': jnp.full((H,), 0.05, jnp.float32), 'wqx': wqx, 'wqx_scale': wqx_s, 'qx_in_scale': jnp.full((H,), 0.05, jnp.float32), 'wk': wk, 'wk_scale': wk_s, 'k_in_scale': jnp.full((H,), 0.05, jnp.float32), 'wv': wv, 'wv_scale': wv_s, 'v_in_scale': jnp.full((H,), 0.05, jnp.float32), 'w_kv_x': jax.random.normal(ks[7], (2 * G * D, H), jnp.float32) * 0.02, 'qln_w': jnp.ones((D,), jnp.float32), 'qln_b': jnp.zeros((D,), jnp.float32), 'kln_w': jnp.ones((D,), jnp.float32), 'kln_b': jnp.zeros((D,), jnp.float32), 'qxln_w': jnp.ones((D,), jnp.float32), 'qxln_b': jnp.zeros((D,), jnp.float32), 'kxln_w': jnp.ones((D,), jnp.float32), 'kxln_b': jnp.zeros((D,), jnp.float32), 'wproj': wproj, 'proj_w_scale': wp_s, 'proj_in_scale': jnp.asarray(0.05, jnp.float32), 'proj_smooth': jnp.full((2 * NH * D,), 0.05, jnp.float32)}
    _L0_xattn_all = _L0_xattn_setup()
    _L0_xattn_in = {k: v for k, v in _L0_xattn_all.items() if k in ('ln_w', 'ln_b', 'wq', 'wq_scale', 'q_in_scale', 'wqx', 'wqx_scale', 'qx_in_scale', 'wk', 'wk_scale', 'k_in_scale', 'wv', 'wv_scale', 'v_in_scale', 'w_kv_x', 'qln_w', 'qln_b', 'kln_w', 'kln_b', 'qxln_w', 'qxln_b', 'kxln_w', 'kxln_b', 'wproj', 'proj_w_scale', 'proj_in_scale', 'proj_smooth')}
    del _L0_xattn_all

    def _L0_attn_setup():
        import jax, jax.numpy as jnp
        import numpy as np
        HIDDEN = 256
        NKH, NVH, HD, K = (16, 32, 128, 4)
        KDIM = NKH * HD
        VDIM = NVH * HD
        CONV = 2 * KDIM + VDIM
        EXP = NVH // NKH

        def _l2norm(a):
            n = jnp.sqrt(jnp.sum(a * a, axis=-1, keepdims=True))
            return a / jnp.maximum(n, 1e-12)

        def _reference_tuple_inner(x, W_qkv, W_z, W_b, W_a, conv_w, dt_bias, A_log, norm_w, W_out):
            B, T, _ = x.shape
            qkv = jnp.einsum('bth,ch->btc', x, W_qkv)
            z = jnp.einsum('bth,vh->btv', x, W_z)
            b_raw = jnp.einsum('bth,nh->btn', x, W_b)
            a_raw = jnp.einsum('bth,nh->btn', x, W_a)
            qkv_t = jnp.swapaxes(qkv, 1, 2)
            padded = jnp.concatenate([jnp.zeros((B, CONV, K - 1), x.dtype), qkv_t], axis=2)
            w = conv_w[:, 0, :]
            conv = sum((w[None, :, j:j + 1] * padded[:, :, j:j + T] for j in range(K)))
            conv = jax.nn.silu(conv)
            new_conv_buf = padded[..., T:]
            qkvc = jnp.swapaxes(conv, 1, 2)
            q = qkvc[..., :KDIM].reshape(B, T, NKH, HD)
            kk = qkvc[..., KDIM:2 * KDIM].reshape(B, T, NKH, HD)
            v = qkvc[..., 2 * KDIM:].reshape(B, T, NVH, HD)
            q = jnp.repeat(q, EXP, axis=2)
            kk = jnp.repeat(kk, EXP, axis=2)
            q = _l2norm(q)
            kk = _l2norm(kk)
            beta = jax.nn.sigmoid(b_raw)
            g = -jnp.exp(A_log) * jax.nn.softplus(a_raw + dt_bias)
            decay = jnp.exp(g)
            state0 = jnp.zeros((B, NVH, HD, HD), x.dtype)
            tm = lambda a: jnp.moveaxis(a, 1, 0)

            def step(state, inp):
                q_t, k_t, v_t, b_t, d_t = inp
                state = state * d_t[..., None, None]
                Sk = jnp.einsum('bhi,bhij->bhj', k_t, state)
                delta = (v_t - Sk) * b_t[..., None]
                state = state + jnp.einsum('bhi,bhj->bhij', k_t, delta)
                o = jnp.einsum('bhi,bhij->bhj', q_t, state)
                return (state, o)
            state, o = jax.lax.scan(step, state0, (tm(q), tm(kk), tm(v), tm(beta), tm(decay)))
            o = jnp.moveaxis(o, 0, 1)
            zz = z.reshape(B, T, NVH, HD)
            y = o * jax.nn.silu(zz)
            y = y * jax.lax.rsqrt(jnp.mean(y * y, axis=-1, keepdims=True) + 1e-06) * norm_w
            out = jnp.einsum('btv,ov->bto', y.reshape(B, T, VDIM), W_out)
            return (out, state, new_conv_buf)
        key = jax.random.key(seed)
        ks = jax.random.split(key, 8)
        s = 0.02
        B, T = (2, 256)
        return {'x': jax.random.normal(ks[0], (B, T, HIDDEN), jnp.float32), 'W_qkv': jax.random.normal(ks[1], (CONV, HIDDEN), jnp.float32) * s, 'W_z': jax.random.normal(ks[2], (VDIM, HIDDEN), jnp.float32) * s, 'W_b': jax.random.normal(ks[3], (NVH, HIDDEN), jnp.float32) * s, 'W_a': jax.random.normal(ks[4], (NVH, HIDDEN), jnp.float32) * s, 'conv_w': jax.random.normal(ks[5], (CONV, 1, K), jnp.float32) * 0.1, 'dt_bias': jnp.ones((NVH,), jnp.float32), 'A_log': jnp.zeros((NVH,), jnp.float32), 'norm_w': jnp.ones((HD,), jnp.float32), 'W_out': jax.random.normal(ks[6], (HIDDEN, VDIM), jnp.float32) * s}
    _L0_attn_all = _L0_attn_setup()
    _L0_attn_in = {k: v for k, v in _L0_attn_all.items() if k in ('W_qkv', 'W_z', 'W_b', 'W_a', 'conv_w', 'dt_bias', 'A_log', 'norm_w', 'W_out')}
    del _L0_attn_all

    def _L0_ffn_setup():
        import jax, jax.numpy as jnp
        import numpy as np
        H, I, E, K = (256, 512, 8, 2)
        B, S = (1, 256)

        def _silu_mul(gu):
            d = gu.shape[-1] // 2
            return jax.nn.silu(gu[..., :d]) * gu[..., d:]
        key = jax.random.key(seed)
        ks = jax.random.split(key, 6)
        w_scale = 0.02
        return {'x': jax.random.normal(ks[0], (B, S, H), jnp.float32), 'gate_w': jax.random.normal(ks[1], (H, E), jnp.float32) * w_scale, 'base_gate_up': jax.random.normal(ks[2], (H, 2 * I), jnp.float32) * w_scale, 'base_down': jax.random.normal(ks[3], (I, H), jnp.float32) * w_scale, 'expert_gate_up': jax.random.normal(ks[4], (E, H, 2 * I), jnp.float32) * w_scale, 'expert_down': jax.random.normal(ks[5], (E, I, H), jnp.float32) * w_scale}
    _L0_ffn_all = _L0_ffn_setup()
    _L0_ffn_in = {k: v for k, v in _L0_ffn_all.items() if k in ('gate_w', 'base_gate_up', 'base_down', 'expert_gate_up', 'expert_down')}
    del _L0_ffn_all
    return {'x': x, 'ctx_2048': ctx_2048, 'L0_xattn_ln_w': _L0_xattn_in['ln_w'], 'L0_xattn_ln_b': _L0_xattn_in['ln_b'], 'L0_xattn_wq': _L0_xattn_in['wq'], 'L0_xattn_wq_scale': _L0_xattn_in['wq_scale'], 'L0_xattn_q_in_scale': _L0_xattn_in['q_in_scale'], 'L0_xattn_wqx': _L0_xattn_in['wqx'], 'L0_xattn_wqx_scale': _L0_xattn_in['wqx_scale'], 'L0_xattn_qx_in_scale': _L0_xattn_in['qx_in_scale'], 'L0_xattn_wk': _L0_xattn_in['wk'], 'L0_xattn_wk_scale': _L0_xattn_in['wk_scale'], 'L0_xattn_k_in_scale': _L0_xattn_in['k_in_scale'], 'L0_xattn_wv': _L0_xattn_in['wv'], 'L0_xattn_wv_scale': _L0_xattn_in['wv_scale'], 'L0_xattn_v_in_scale': _L0_xattn_in['v_in_scale'], 'L0_xattn_w_kv_x': _L0_xattn_in['w_kv_x'], 'L0_xattn_qln_w': _L0_xattn_in['qln_w'], 'L0_xattn_qln_b': _L0_xattn_in['qln_b'], 'L0_xattn_kln_w': _L0_xattn_in['kln_w'], 'L0_xattn_kln_b': _L0_xattn_in['kln_b'], 'L0_xattn_qxln_w': _L0_xattn_in['qxln_w'], 'L0_xattn_qxln_b': _L0_xattn_in['qxln_b'], 'L0_xattn_kxln_w': _L0_xattn_in['kxln_w'], 'L0_xattn_kxln_b': _L0_xattn_in['kxln_b'], 'L0_xattn_wproj': _L0_xattn_in['wproj'], 'L0_xattn_proj_w_scale': _L0_xattn_in['proj_w_scale'], 'L0_xattn_proj_in_scale': _L0_xattn_in['proj_in_scale'], 'L0_xattn_proj_smooth': _L0_xattn_in['proj_smooth'], 'L0_attn_W_qkv': _L0_attn_in['W_qkv'], 'L0_attn_W_z': _L0_attn_in['W_z'], 'L0_attn_W_b': _L0_attn_in['W_b'], 'L0_attn_W_a': _L0_attn_in['W_a'], 'L0_attn_conv_w': _L0_attn_in['conv_w'], 'L0_attn_dt_bias': _L0_attn_in['dt_bias'], 'L0_attn_A_log': _L0_attn_in['A_log'], 'L0_attn_norm_w': _L0_attn_in['norm_w'], 'L0_attn_W_out': _L0_attn_in['W_out'], 'L0_ffn_gate_w': _L0_ffn_in['gate_w'], 'L0_ffn_base_gate_up': _L0_ffn_in['base_gate_up'], 'L0_ffn_base_down': _L0_ffn_in['base_down'], 'L0_ffn_expert_gate_up': _L0_ffn_in['expert_gate_up'], 'L0_ffn_expert_down': _L0_ffn_in['expert_down']}

def reference(x, ctx_2048, L0_xattn_ln_w, L0_xattn_ln_b, L0_xattn_wq, L0_xattn_wq_scale, L0_xattn_q_in_scale, L0_xattn_wqx, L0_xattn_wqx_scale, L0_xattn_qx_in_scale, L0_xattn_wk, L0_xattn_wk_scale, L0_xattn_k_in_scale, L0_xattn_wv, L0_xattn_wv_scale, L0_xattn_v_in_scale, L0_xattn_w_kv_x, L0_xattn_qln_w, L0_xattn_qln_b, L0_xattn_kln_w, L0_xattn_kln_b, L0_xattn_qxln_w, L0_xattn_qxln_b, L0_xattn_kxln_w, L0_xattn_kxln_b, L0_xattn_wproj, L0_xattn_proj_w_scale, L0_xattn_proj_in_scale, L0_xattn_proj_smooth, L0_attn_W_qkv, L0_attn_W_z, L0_attn_W_b, L0_attn_W_a, L0_attn_conv_w, L0_attn_dt_bias, L0_attn_A_log, L0_attn_norm_w, L0_attn_W_out, L0_ffn_gate_w, L0_ffn_base_gate_up, L0_ffn_base_down, L0_ffn_expert_gate_up, L0_ffn_expert_down):
    import jax
    import jax.numpy as jnp

    def _L0_xattn_ref(hidden_states, cond, ln_w, ln_b, wq, wq_scale, q_in_scale, wqx, wqx_scale, qx_in_scale, wk, wk_scale, k_in_scale, wv, wv_scale, v_in_scale, w_kv_x, qln_w, qln_b, kln_w, kln_b, qxln_w, qxln_b, kxln_w, kxln_b, wproj, proj_w_scale, proj_in_scale, proj_smooth):
        import jax, jax.numpy as jnp
        import numpy as np
        FP8_MAX = 448.0
        EPS = 1e-05

        def _fp8_roundtrip(x):
            return x.astype(jnp.float8_e4m3fn).astype(jnp.float32)

        def _div_clamp_fp8(x, scale):
            y = jnp.clip(x.astype(jnp.float32) / scale, -FP8_MAX, FP8_MAX)
            y = y.astype(jnp.bfloat16).astype(jnp.float32)
            return _fp8_roundtrip(y)

        def _ln(x, w, b):
            mu = jnp.mean(x, axis=-1, keepdims=True)
            var = jnp.mean(jnp.square(x - mu), axis=-1, keepdims=True)
            return (x - mu) * jax.lax.rsqrt(var + EPS) * w + b

        def _fp8_linear_pertensor(x, wq, w_scale, in_scale):
            xq = _div_clamp_fp8(x, in_scale)
            return jnp.einsum('bsi,oi->bso', xq * in_scale, wq) * w_scale

        def _gqa(q, k, v):
            scale = 1.0 / np.sqrt(q.shape[-1])
            scores = jnp.einsum('bsghd,btgd->bghst', q, k) * scale
            p = jax.nn.softmax(scores, axis=-1)
            return jnp.einsum('bghst,btgd->bsghd', p, v)
        b, s, _ = hidden_states.shape
        sc = cond.shape[1]
        d = qln_w.shape[0]
        nh = wq.shape[0] // d
        g = wk.shape[0] // d
        hpg = nh // g
        ln_out = _ln(hidden_states, ln_w, ln_b)
        q = _fp8_linear_pertensor(ln_out, wq, wq_scale, q_in_scale).reshape(b, s, g, hpg, d)
        q = _ln(q, qln_w, qln_b)
        k = _fp8_linear_pertensor(ln_out, wk, wk_scale, k_in_scale).reshape(b, s, g, d)
        k = _ln(k, kln_w, kln_b)
        v = _fp8_linear_pertensor(ln_out, wv, wv_scale, v_in_scale).reshape(b, s, g, d)
        core = _gqa(q, k, v).reshape(b, s, nh * d)
        qx = _fp8_linear_pertensor(ln_out, wqx, wqx_scale, qx_in_scale).reshape(b, s, g, hpg, d)
        qx = _ln(qx, qxln_w, qxln_b)
        kvx = jnp.einsum('bsi,oi->bso', cond, w_kv_x)
        kx, vx = jnp.split(kvx, 2, axis=-1)
        kx = _ln(kx.reshape(b, sc, g, d), kxln_w, kxln_b)
        vx = vx.reshape(b, sc, g, d)
        xout = _gqa(qx, kx, vx).reshape(b, s, nh * d)
        cat = jnp.concatenate([core, xout], axis=-1)
        catq = _div_clamp_fp8(cat, proj_smooth)
        return jnp.einsum('bsi,oi->bso', catq, wproj) * (proj_in_scale * proj_w_scale)

    def _L0_attn_ref(x, W_qkv, W_z, W_b, W_a, conv_w, dt_bias, A_log, norm_w, W_out):
        import jax, jax.numpy as jnp
        import numpy as np
        HIDDEN = 256
        NKH, NVH, HD, K = (16, 32, 128, 4)
        KDIM = NKH * HD
        VDIM = NVH * HD
        CONV = 2 * KDIM + VDIM
        EXP = NVH // NKH

        def _l2norm(a):
            n = jnp.sqrt(jnp.sum(a * a, axis=-1, keepdims=True))
            return a / jnp.maximum(n, 1e-12)

        def _reference_tuple_inner(x, W_qkv, W_z, W_b, W_a, conv_w, dt_bias, A_log, norm_w, W_out):
            B, T, _ = x.shape
            qkv = jnp.einsum('bth,ch->btc', x, W_qkv)
            z = jnp.einsum('bth,vh->btv', x, W_z)
            b_raw = jnp.einsum('bth,nh->btn', x, W_b)
            a_raw = jnp.einsum('bth,nh->btn', x, W_a)
            qkv_t = jnp.swapaxes(qkv, 1, 2)
            padded = jnp.concatenate([jnp.zeros((B, CONV, K - 1), x.dtype), qkv_t], axis=2)
            w = conv_w[:, 0, :]
            conv = sum((w[None, :, j:j + 1] * padded[:, :, j:j + T] for j in range(K)))
            conv = jax.nn.silu(conv)
            new_conv_buf = padded[..., T:]
            qkvc = jnp.swapaxes(conv, 1, 2)
            q = qkvc[..., :KDIM].reshape(B, T, NKH, HD)
            kk = qkvc[..., KDIM:2 * KDIM].reshape(B, T, NKH, HD)
            v = qkvc[..., 2 * KDIM:].reshape(B, T, NVH, HD)
            q = jnp.repeat(q, EXP, axis=2)
            kk = jnp.repeat(kk, EXP, axis=2)
            q = _l2norm(q)
            kk = _l2norm(kk)
            beta = jax.nn.sigmoid(b_raw)
            g = -jnp.exp(A_log) * jax.nn.softplus(a_raw + dt_bias)
            decay = jnp.exp(g)
            state0 = jnp.zeros((B, NVH, HD, HD), x.dtype)
            tm = lambda a: jnp.moveaxis(a, 1, 0)

            def step(state, inp):
                q_t, k_t, v_t, b_t, d_t = inp
                state = state * d_t[..., None, None]
                Sk = jnp.einsum('bhi,bhij->bhj', k_t, state)
                delta = (v_t - Sk) * b_t[..., None]
                state = state + jnp.einsum('bhi,bhj->bhij', k_t, delta)
                o = jnp.einsum('bhi,bhij->bhj', q_t, state)
                return (state, o)
            state, o = jax.lax.scan(step, state0, (tm(q), tm(kk), tm(v), tm(beta), tm(decay)))
            o = jnp.moveaxis(o, 0, 1)
            zz = z.reshape(B, T, NVH, HD)
            y = o * jax.nn.silu(zz)
            y = y * jax.lax.rsqrt(jnp.mean(y * y, axis=-1, keepdims=True) + 1e-06) * norm_w
            out = jnp.einsum('btv,ov->bto', y.reshape(B, T, VDIM), W_out)
            return (out, state, new_conv_buf)
        return _reference_tuple_inner(x, W_qkv, W_z, W_b, W_a, conv_w, dt_bias, A_log, norm_w, W_out)[0]

    def _L0_ffn_ref(x, gate_w, base_gate_up, base_down, expert_gate_up, expert_down):
        import jax, jax.numpy as jnp
        import numpy as np
        H, I, E, K = (256, 512, 8, 2)
        B, S = (1, 256)

        def _silu_mul(gu):
            d = gu.shape[-1] // 2
            return jax.nn.silu(gu[..., :d]) * gu[..., d:]
        base_y = _silu_mul(x @ base_gate_up) @ base_down
        b, s, h = x.shape
        xf = x.reshape(-1, h)
        n = xf.shape[0]
        n_exp = gate_w.shape[1]
        probs = jax.nn.softmax((xf @ gate_w).astype(jnp.float32), axis=-1)
        w, idx = jax.lax.top_k(probs, K)
        w = (w / w.sum(axis=-1, keepdims=True)).astype(x.dtype)
        comb = jnp.zeros((n, n_exp), x.dtype).at[jnp.arange(n)[:, None], idx].add(w)
        out = jnp.zeros_like(xf)
        for e in range(n_exp):
            y = _silu_mul(xf @ expert_gate_up[e]) @ expert_down[e]
            out = out + comb[:, e:e + 1] * y
        return out.reshape(b, s, h) + base_y
    x = x + _L0_xattn_ref(_layernorm(x, axis=-1), ctx_2048, L0_xattn_ln_w, L0_xattn_ln_b, L0_xattn_wq, L0_xattn_wq_scale, L0_xattn_q_in_scale, L0_xattn_wqx, L0_xattn_wqx_scale, L0_xattn_qx_in_scale, L0_xattn_wk, L0_xattn_wk_scale, L0_xattn_k_in_scale, L0_xattn_wv, L0_xattn_wv_scale, L0_xattn_v_in_scale, L0_xattn_w_kv_x, L0_xattn_qln_w, L0_xattn_qln_b, L0_xattn_kln_w, L0_xattn_kln_b, L0_xattn_qxln_w, L0_xattn_qxln_b, L0_xattn_kxln_w, L0_xattn_kxln_b, L0_xattn_wproj, L0_xattn_proj_w_scale, L0_xattn_proj_in_scale, L0_xattn_proj_smooth)
    x = x + _L0_attn_ref(_layernorm(x, axis=-1), L0_attn_W_qkv, L0_attn_W_z, L0_attn_W_b, L0_attn_W_a, L0_attn_conv_w, L0_attn_dt_bias, L0_attn_A_log, L0_attn_norm_w, L0_attn_W_out)
    x = x + _L0_ffn_ref(_layernorm(x, axis=-1), L0_ffn_gate_w, L0_ffn_base_gate_up, L0_ffn_base_down, L0_ffn_expert_gate_up, L0_ffn_expert_down)
    return x

_drawn_inputs = setup_inputs


def setup_inputs(seed=0):
    import zlib

    import numpy as np

    out = dict(_drawn_inputs(seed))
    spreads = {'L0_xattn_ln_w': (1.0, 0.2),
     'L0_xattn_ln_b': (0.0, 0.1),
     'L0_xattn_q_in_scale': (0.05000000074505806, 0.6),
     'L0_xattn_qx_in_scale': (0.05000000074505806, 0.6),
     'L0_xattn_k_in_scale': (0.05000000074505806, 0.6),
     'L0_xattn_v_in_scale': (0.05000000074505806, 0.6),
     'L0_xattn_qln_w': (1.0, 0.6),
     'L0_xattn_qln_b': (0.0, 0.8),
     'L0_xattn_kln_w': (1.0, 0.6),
     'L0_xattn_kln_b': (0.0, 2.0),
     'L0_xattn_qxln_w': (1.0, 0.6),
     'L0_xattn_qxln_b': (0.0, 0.8),
     'L0_xattn_kxln_w': (1.0, 0.6),
     'L0_xattn_kxln_b': (0.0, 0.8),
     'L0_xattn_proj_smooth': (0.05000000074505806, 0.2),
     'L0_attn_dt_bias': (1.0, 0.6),
     'L0_attn_A_log': (0.0, 0.699),
     'L0_attn_norm_w': (1.0, 0.2)}
    factors = {'L0_attn_W_a': 3.07,
     'L0_ffn_gate_w': 4.091,
     'L0_ffn_expert_gate_up': 3.508,
     'L0_ffn_expert_down': 3.508,
     'L0_ffn_base_gate_up': 3.368,
     'L0_ffn_base_down': 3.399}
    for name, (base, spread) in spreads.items():
        noise = np.random.default_rng([zlib.crc32(name.encode()), seed]).standard_normal(out[name].shape)
        drawn = base * np.exp(spread * noise) if base else spread * noise
        out[name] = jnp.asarray(drawn.astype(out[name].dtype))
    for name, factor in factors.items():
        out[name] = (out[name] * factor).astype(out[name].dtype)
    return out
```

```python
from contextlib import ExitStack

import numpy as np
import concourse.bass as bass
from concourse import mybir

ALU = mybir.AluOpType
ACT = mybir.ActivationFunctionType
F32 = mybir.dt.float32
F32R = mybir.dt.float32r
BF16 = mybir.dt.bfloat16
U16 = mybir.dt.uint16
I32 = mybir.dt.int32
X = mybir.AxisListType.X

S = 64
H = 256
HC = H // 128
D = 128
G = 8
NH = 16
ROWS = (NH // G) * S
GR = G * ROWS
SC = 6272
CH = 7
NCH = SC // 128 // CH
BUF = [0, 1, 0, 1, 0, 1, 2]
USES = [3, 3, 1]
NV = 32
NK = 16
EXPERTS = 8
INNER = 512
EPS = 1e-5
FP8_MAX = 448.0


def prev_use(i):
    return {0: 3, 1: 3, 6: 7}.get(i, 2)


def buf_use(j, i):
    return j * USES[BUF[i]] + BUF[:i].count(BUF[i])


class Tally:

    def __init__(self, sem):
        self.sem, self.n = sem, 0

    def by(self, ins):
        ins.then_inc(self.sem, 1)
        self.n += 1
        return self.n

    def settle(self, eng, ins):
        self.by(ins)
        eng.wait_ge(self.sem, self.n)


SMALL = {}
_at = 0
for _name, _n in (("ln_w", 2), ("ln_b", 2), ("qx_in", 2), ("q_in", 2), ("k_in", 2), ("v_in", 2),
                  ("qxln_w", 1), ("qxln_b", 1), ("qln_w", 1), ("qln_b", 1), ("kln_w", 1), ("kln_b", 1),
                  ("kxln_w", 1), ("kxln_b", 1), ("smooth", 32), ("norm_w", 1), ("wqx_s", 1), ("wq_s", 1),
                  ("wk_s", 1), ("wv_s", 1), ("pw_s", 1), ("pin_s", 1), ("conv", 256), ("dt_bias", 32),
                  ("A_log", 32), ("W_ba", 128), ("gate", 16)):
    SMALL[_name] = (_at, _n)
    _at += _n
NSMALL = _at


def build(nc, t, upto=9):
    ctx = ExitStack()
    phase1 = ExitStack()
    split_weights = ExitStack()

    def sb(name, shape, dt=F32, at=ctx):
        return at.enter_context(nc.sbuf_tensor(name, shape, dt))

    def sem(name):
        return ctx.enter_context(nc.semaphore(name))

    with ctx:
        wide = sb("wide", [128, 16384])
        k_hi = sb("k_hi", [128, HC, 1024], F32R, split_weights)
        k_lo = sb("k_lo", [128, HC, 1024], F32R, split_weights)
        q_hi = sb("q_hi", [128, HC, 1024], F32R, split_weights)
        q_lo = sb("q_lo", [128, HC, 1024], F32R, split_weights)
        split_weights.close()
        mid = sb("mid", [128, 8192])
        ident = sb("ident", [128, 128])
        ones = sb("ones", [128, 128])
        small = sb("small", [128, NSMALL])
        x_res = sb("x_res", [S, H])
        stat = sb("stat", [128, 64])
        rstd1 = sb("rstd1", [128, 8])
        cst = sb("cst", [128, 8])

        eps8 = sb("eps8", [128, 8])

        scores = sb("scores", [128, CH, GR], F32, phase1)
        neg_max = sb("neg_max", [128, GR], F32, phase1)
        alpha = sb("alpha", [128, GR], F32, phase1)
        run_max = sb("run_max", [128, GR], F32, phase1)
        c_col = sb("c_col", [128, G], F32, phase1)
        mx = sb("mx", [128, G], F32, phase1)
        p_sum = sb("p_sum", [128, GR], F32, phase1)
        o_acc = sb("o_acc", [128, HC, GR], F32, phase1)
        p_f = sb("p_f", [128, 2, 512], F32, phase1)
        p_hi = sb("p_hi", [128, 2, 512], F32R, phase1)
        p_lo = sb("p_lo", [128, 2, 512], F32R, phase1)
        ct_raw = sb("ct_raw", [128, 3, 256], F32, phase1)
        ct_hi = sb("ct_hi", [128, 3, 256], F32R, phase1)
        ct_lo = sb("ct_lo", [128, 3, 256], F32R, phase1)
        cn_raw = sb("cn_raw", [128, 3, 256], F32, phase1)
        cn_hi = sb("cn_hi", [128, 3, 256], F32R, phase1)
        cn_lo = sb("cn_lo", [128, 3, 256], F32R, phase1)
        ksq = sb("ksq", [128, 2, 512], F32, phase1)
        ss = sb("ss", [128, 8], F32, phase1)
        cat_t = sb("cat_t", [128, 2048], F32, phase1)
        wv_x = scores[:, 0:2, :]
        phase1.close()
        ph2 = {}
        second_memory(ph2, sb)
        ph2["stat"] = stat

        pk = ctx.enter_context(nc.psum_tensor("pk", [128, 2, 512], F32))
        ps = ctx.enter_context(nc.psum_tensor("ps", [128, 2, 512], F32))
        po = ctx.enter_context(nc.psum_tensor("po", [128, 4, 512], F32))
        bank = [po[:, 0, :], po[:, 1, :], po[:, 2, :], po[:, 3, :], pk[:, 0, :], pk[:, 1, :], ps[:, 0, :], ps[:, 1, :]]

        def sm(name, rows=128, k=None):
            a, n = SMALL[name]
            return small[0:rows, a:a + n] if k is None else small[0:rows, a + k:a + k + 1]

        names = """x_in small_in w_qx w_q w_k w_v kxT_in kxd_in const_ready pow_ask pow_done dve_step pool_step xT_done
            xq_ready lin_done lin_evac heads_ready headT_done qkT_ready qmean_done qc_ready cbc_done qk_done
            q_split k_split s_self p_self pT_self pT_evac core_done cat_core ct_split cn_split ksq_mm ksq_act
            ssum rstd_ready s_mm evac_v evac_a max_done rt_done mx_ready mb_done c_ready mx_raw mx_full
            alpha_diff max_ready alpha_ready p_shift p_exp p_hi_ready p_lo_ready pv_rh psum_add merged
            psum_scaled wv_in den_done on_ready xo_done wproj_in catq_ready proj_done x1_ready stored""".split()
        s = {n: sem(n) for n in names}
        ct_in = [sem(f"ct_in{b}") for b in range(3)]
        cn_in = [sem(f"cn_in{b}") for b in range(3)]
        s.update({n: sem(n) for n in SECOND})

        wqx = wide[:, 0:4096].rearrange("p (h n) -> p h n", h=HC)
        wq = wide[:, 4096:8192].rearrange("p (h n) -> p h n", h=HC)
        wk = wide[:, 8192:10240].rearrange("p (h n) -> p h n", h=HC)
        wv = wide[:, 10240:12288].rearrange("p (h n) -> p h n", h=HC)
        kxT = wide[:, 12288:14336].rearrange("p (h n) -> p h n", h=HC)
        kxd = wide[:, 14336:16384].rearrange("p (g n) -> p g n", g=G)
        heads = scores[0:S, 0:5, :].rearrange("p a b -> p (a b)")
        vrow = scores[0:S, 5, :]
        hst = scores[0:S, 6, 0:240]
        hm = scores[0:S, 6, 256:296]
        hv = scores[0:S, 6, 296:336]
        ht = scores[0:S, 6, 336:376]
        hr = scores[0:S, 6, 376:416]
        xn = scores[0:S, 6, 512:768]
        qxT = o_acc[:, 0, :]
        qkw = o_acc[:, 1, :]
        qT = p_sum[:, :]
        kT = p_f[:, 0, :]
        pself = p_f[:, 1, :]
        pTs = run_max[0:S, :]
        xT = ct_raw[:, 0, 0:128]
        xy = ct_raw[:, 1, 0:128]
        xm = ct_raw[:, 2, 0:128]
        xb16 = cn_raw[:, 0, 0:64].bitcast(BF16)
        xe16 = cn_raw[:, 0, 64:128].bitcast(BF16)
        xq = [cn_raw[:, 1, 0:128], cn_raw[:, 1, 128:256], cn_raw[:, 2, 0:128], cn_raw[:, 2, 128:256]]
        mean_w = ct_raw[:, 1, 128:256]

        block = ctx.enter_context(nc.Block())

        @block.sync
        def _(sp):
            sp.dma_start(x_res[:, :], t["x"]).then_inc(s["x_in"], 16)
            sp.dma_start(small[:, :], t["small"]).then_inc(s["small_in"], 16)
            sp.dma_start(wqx, t["wqx"]).then_inc(s["w_qx"], 16)
            sp.dma_start(wq, t["wq"]).then_inc(s["w_q"], 16)
            sp.dma_start(wk, t["wk"]).then_inc(s["w_k"], 16)
            sp.dma_start(kxd, t["kxd"]).then_inc(s["kxd_in"], 16)
            sp.dma_start(kxT, t["kxT"]).then_inc(s["kxT_in"], 16)
            sp.dma_start(wv, t["wv"]).then_inc(s["w_v"], 16)

            def load_t(j, i):
                if isinstance(j, int) and j == 0:
                    if i in (0, 1, 6):
                        pass
                    else:
                        sp.wait_ge(s["ct_split"], i - 1)
                else:
                    sp.wait_ge(s["ct_split"], j * CH + i - prev_use(i) + 1)
                sp.dma_start(ct_raw[:, BUF[i], :], t["ctT"][j * CH + i]).then_inc(ct_in[BUF[i]], 16)

            def load_n(j, i):
                if isinstance(j, int) and j == 0:
                    if i not in (0, 1, 6):
                        sp.wait_ge(s["cn_split"], i - 1)
                else:
                    sp.wait_ge(s["cn_split"], j * CH + i - prev_use(i) + 1)
                sp.dma_start(cn_raw[:, BUF[i], :], t["cn"][j * CH + i]).then_inc(cn_in[BUF[i]], 16)

            sp.wait_ge(s["core_done"], 1)
            sp.wait_ge(s["lin_done"], 12)
            for i in range(CH):
                load_t(0, i)
            sp.wait_ge(s["q_split"], 1)
            sp.dma_start(wide[:, :], t["W_qkv"], max_dma_last_dim=8192).then_inc(s["wqkv_in"], 16)
            with sp.Fori(1, 2) as j:
                for i in range(CH):
                    load_t(j, i)
                    load_n(0, i)
            with sp.Fori(2, NCH) as j:
                for i in range(CH):
                    load_t(j, i)
                    load_n(j - 1, i)
            sp.wait_ge(s["s_mm"], 2 * CH * NCH)
            sp.dma_start(mid[:, :], t["wprojT"], max_dma_last_dim=8192).then_inc(s["wproj_in"], 16)
            for i in range(CH):
                load_n(NCH - 1, i)
                if i == 2:
                    sp.wait_ge(s["psum_add"], 2 * (CH * (NCH - 1) + 2))
                    sp.wait_ge(s["p_lo_ready"], 2 * (CH * (NCH - 1) + 2))
                    sp.dma_start(wv_x, t["wvxT"]).then_inc(s["wv_in"], 16)
            if upto > 1:
                second_loads(sp, s, t, ph2, wide, mid)
            sp.wait_ge(s["x1_ready" if upto == 1 else "out_ready"], 1)
            sp.dma_start(t["out"], x_res[:, :]).then_inc(s["stored"], 16)
            sp.wait_ge(s["stored"], 16)

        @block.gpsimd
        def _(pool):
            step = Tally(s["pool_step"])
            asked = Tally(s["pow_ask"])

            def inv_root(out, in_, rows, width):
                asked.n += 1
                pool.wait_ge(s["pow_ask"], asked.n)
                pool.tensor_tensor(out, in_, cst[0:rows, 0:1].broadcast_to([rows, width]) if width > 1
                                   else cst[0:rows, 0:1], ALU.pow).then_inc(s["pow_done"], 1)

            pool.memset(cst[:, :], -0.5).then_inc(s["pool_step"], 1)
            pool.memset(eps8[:, :], 128.0 * EPS)
            pool.memset(ones[:, :], 1.0).then_inc(s["pool_step"], 1)
            pool.memset(ident[:, :], 0.0).then_inc(s["pool_step"], 1)
            pool.wait_ge(s["pool_step"], 3)
            pool.affine_select(out=ident[:, :], in_=ident[:, :], compare_op=ALU.not_equal, fill=1.0, base=0,
                               pattern=[[-1, 128]], channel_multiplier=1).then_inc(s["const_ready"], 1)
            inv_root(stat[0:S, 8:9], stat[0:S, 7:8], S, 1)
            inv_root(stat[0:S, 8:9], stat[0:S, 7:8], S, 1)
            inv_root(hr, hv, S, 40)

            def root(j, i):
                pool.wait_ge(s["ssum"], 2 * (j * CH + i + 1))
                if not (isinstance(j, int) and j == 0 and i == 0):
                    pool.wait_ge(s["evac_v"], j * CH + i)
                    pool.wait_ge(s["evac_a"], j * CH + i)
                pool.tensor_tensor(ss[:, :], ss[:, :], eps8[:, :], ALU.add).then_inc(s["ss_eps"], 1)
                pool.wait_ge(s["ss_eps"], j * CH + i + 1)
                pool.tensor_tensor(rstd1[:, :], ss[:, :], cst[:, :], ALU.pow).then_inc(s["rstd_ready"], 1)

            def shift(j, i):
                if i == 0:
                    pool.wait_ge(s["max_ready"], j + 1)
                for h in range(2):
                    if not (isinstance(j, int) and j == 0 and i == 0):
                        pool.wait_ge(s["psum_add"], 2 * (j * CH + i) + h - 1)
                        pool.wait_ge(s["p_lo_ready"], 2 * (j * CH + i) + h - 1)
                    pool.tensor_tensor(p_f[:, h, :], scores[:, i, 512 * h:512 * h + 512],
                                       neg_max[:, 512 * h:512 * h + 512], ALU.add).then_inc(s["p_shift"], 1)

            def add_p(j, i, h, probs):
                pool.wait_ge(s["p_exp"], 2 * (j * CH + i) + h + 1)
                if i == 0:
                    pool.wait_ge(s["psum_scaled"], j + 1)
                else:
                    pool.wait_ge(s["psum_add"], 2 * (j * CH + i) - 1 + h)
                cols = p_sum[:, 512 * h:512 * h + 512]
                pool.tensor_tensor(cols, cols, probs, ALU.add).then_inc(s["psum_add"], 1)

            for i in range(CH):
                root(0, i)

            def pool_chunk(j, k):
                for i in range(CH):
                    shift(k, i)
                    if i == 0:
                        root(j, i)
                        add_p(k, i, 0, p_f[:, 0, :])
                    else:
                        add_p(k, i, 0, p_f[:, 0, :])
                        root(j, i)
                    add_p(k, i, 1, p_f[:, 1, :])

            pool_chunk(1, 0)
            with pool.Fori(2, NCH) as j:
                pool_chunk(j, j - 1)
            for i in range(CH):
                for h in range(2):
                    add_p(NCH - 1, i, h, scores[:, i, 512 * h:512 * h + 512])
            if upto > 1:
                second_pool(pool, s, ph2, inv_root, ident, cst, small)

        @block.scalar
        def _(act):
            ends = [("wqx_s", 4), ("wq_s", 4), ("wk_s", 2), ("wv_s", 2)]
            act.wait_ge(s["small_in"], 16)
            n = 0
            for name, count in ends:
                for _ in range(count):
                    act.wait_ge(s["lin_done"], n + 1)
                    dst = heads[:, 512 * n:512 * n + 512] if n < 10 else vrow[:, 512 * (n - 10):512 * (n - 9)]
                    act.activation(dst, bank[n % 8][0:S, :], ACT.Identity, scale=sm(name, S)).then_inc(s["lin_evac"], 1)
                    n += 1
            act.wait_ge(s["s_self"], 2)
            act.activation(pself, pself, ACT.Exp, scale=float(D) ** -0.5).then_inc(s["p_self"], 1)

            def high(j, i, half, raw, hi, landed, used):
                b = BUF[i]
                act.wait_ge(landed[b], 16 * (buf_use(j, i) + 1))
                if not (isinstance(j, int) and j == 0 and i in (0, 1, 6)):
                    act.wait_ge(used, 2 * (j * CH + i - prev_use(i) + 1))
                act.activation(hi[:, b, :], raw[:, b, :], ACT.Identity).then_inc(half, 1)

            def high_t(j, i):
                high(j, i, s["ct_half"], ct_raw, ct_hi, ct_in, s["s_mm"])

            def high_n(j, i):
                high(j, i, s["cn_half"], cn_raw, cn_hi, cn_in, s["pv_rh"])

            def square(j, i):
                for n in range(2):
                    act.wait_ge(s["ksq_mm"], 2 * (j * CH + i) + n + 1)
                    if not (isinstance(j, int) and j == 0 and i == 0):
                        act.wait_ge(s["ssum"], 2 * (j * CH + i) + n - 1)
                    act.activation(ksq[:, n, :], pk[:, n, :], ACT.Square).then_inc(s["ksq_act"], 1)

            def probs(j, i, h, p):
                act.wait_ge(s["p_shift"], 2 * (j * CH + i) + h + 1)
                act.activation(p, p, ACT.Exp).then_inc(s["p_exp"], 1)
                act.wait_ge(s["p_exp"], 2 * (j * CH + i) + h + 1)
                if not (isinstance(j, int) and j == 0 and i == 0):
                    act.wait_ge(s["pv_rh"], 2 * (j * CH + i) + h - 1)
                act.copy(p_hi[:, h, :], p).then_inc(s["p_hi_ready"], 1)

            def evacuate(j, i):
                act.wait_ge(s["rstd_ready"], j * CH + i + 1)
                if not (isinstance(j, int) and j == 0):
                    act.wait_ge(s["p_shift"], 2 * (j * CH + i + 1 - CH))
                act.wait_ge(s["s_mm"], 2 * (j * CH + i) + 2)
                for g in range(4, G):
                    ins = act.activation(scores[:, i, ROWS * g:ROWS * g + ROWS], ps[:, 1, ROWS * (g - 4):ROWS * (g - 3)],
                                         ACT.Identity, scale=rstd1[:, g:g + 1])
                ins.then_inc(s["evac_a"], 1)

            def rescale(j):
                act.wait_ge(s["alpha_diff"], j + 1)
                act.activation(alpha[:, :], alpha[:, :], ACT.Exp).then_inc(s["alpha_ready"], 1)

            high_t(0, 0)
            for i in range(CH):
                square(0, i)
                high_t((i + 1) // CH, (i + 1) % CH)
                evacuate(0, i)
            rescale(0)

            def act_chunk(j, k, last=False):
                for i in range(CH):
                    high_n(k, i)
                    probs(k, i, 0, p_f[:, 0, :])
                    square(j, i)
                    probs(k, i, 1, p_f[:, 1, :])
                    if i < CH - 1:
                        high_t(j, i + 1)
                    elif not last:
                        high_t(j + 1, 0)
                    evacuate(j, i)
                rescale(j)

            act_chunk(1, 0)
            with act.Fori(2, NCH - 1) as j:
                act_chunk(j, j - 1)
            act_chunk(NCH - 1, NCH - 2, last=True)
            for i in range(CH):
                high_n(NCH - 1, i)
                for h in range(2):
                    probs(NCH - 1, i, h, scores[:, i, 512 * h:512 * h + 512])
            if upto > 1:
                second_scalar(act, s, ph2, bank, small)

        @block.vector
        def _(dve):
            v = Tally(s["dve_step"])
            asked = Tally(s["pow_ask"])
            normed = Tally(s["normed"])

            def ask_root(ins):
                asked.by(ins)
                dve.wait_ge(s["pow_done"], asked.n)

            def layernorm_rows(dst, src):
                v.settle(dve, dve.bn_stats(stat[0:S, 0:6], src))
                v.settle(dve, dve.bn_aggr(stat[0:S, 6:8], stat[0:S, 0:6]))
                ask_root(dve.tensor_scalar(stat[0:S, 7:8], stat[0:S, 7:8], EPS, None, ALU.add))
                dve.tensor_scalar(dst, src, stat[0:S, 6:7], stat[0:S, 8:9], ALU.subtract, ALU.mult)\
                   .then_inc(s["normed"], 1)
                normed.n += 1
                dve.wait_ge(s["normed"], normed.n)

            def fp8_round(out, y, b16, e16, mag, ready=None):
                v.settle(dve, dve.tensor_scalar(b16, y, FP8_MAX, -FP8_MAX, ALU.min, ALU.max))
                v.settle(dve, dve.tensor_scalar(e16.bitcast(U16), b16.bitcast(U16), 0x7F80, None, ALU.bitwise_and))
                v.settle(dve, dve.tensor_scalar(mag, e16, 2.0 ** -6, 1.5 * 2.0 ** 20, ALU.max, ALU.mult))
                v.settle(dve, dve.tensor_tensor(out, b16, mag, ALU.add))
                ins = dve.tensor_tensor(out, out, mag, ALU.subtract)
                if ready is None:
                    v.settle(dve, ins)
                else:
                    ins.then_inc(ready, 1)

            dve.wait_ge(s["x_in"], 16)
            dve.wait_ge(s["const_ready"], 1)
            layernorm_rows(xn, x_res[:, :])
            layernorm_rows(xn, xn)
            dve.wait_ge(s["small_in"], 16)
            dve.wait_ge(s["xT_done"], 1)
            xT2 = xT.rearrange("p (h t) -> p h t", h=HC)
            for c in range(HC):
                v.settle(dve, dve.tensor_scalar(xT2[:, c, :], bank[0][:, c * S:c * S + S], sm("ln_w", k=c),
                                                sm("ln_b", k=c), ALU.mult, ALU.add))
            inv_in = stat[:, 16:24]
            a = SMALL["qx_in"][0]
            v.settle(dve, dve.reciprocal(inv_in, small[:, a:a + 8]))
            for n in range(4):
                for c in range(HC):
                    v.settle(dve, dve.tensor_scalar(xy[:, c * S:c * S + S], xT2[:, c, :],
                                                    inv_in[:, 2 * n + c:2 * n + c + 1], None, ALU.mult))
                fp8_round(xq[n], xy, xb16, xe16, xm)
                for c in range(HC):
                    col = xq[n][:, c * S:c * S + S]
                    dve.tensor_scalar(col, col, small[:, a + 2 * n + c:a + 2 * n + c + 1], None, ALU.mult)\
                       .then_inc(s["xq_ready"], 1)
            dve.wait_ge(s["kxT_in"], 16)
            km = stat[:, 24:40]
            kx4 = kxT.rearrange("p h (g d) -> p (h g) d", g=G)
            v.settle(dve, dve.tensor_reduce(km, kx4, X, ALU.add))
            v.settle(dve, dve.tensor_scalar(km, km, 1.0 / D, None, ALU.mult))
            v.settle(dve, dve.tensor_tensor(kx4, kx4, km.unsqueeze(2).broadcast_to([128, 16, D]), ALU.subtract))
            v.settle(dve, dve.tensor_copy(k_hi[:, :, :], kxT))
            dve.tensor_tensor(k_lo[:, :, :], kxT, k_hi[:, :, :].bitcast(F32), ALU.subtract).then_inc(s["k_split"], 1)

            dve.wait_ge(s["lin_evac"], 10)
            for h in range(40):
                v.by(dve.bn_stats(hst[:, 6 * h:6 * h + 6], heads[:, D * h:D * h + D]))
            dve.wait_ge(s["dve_step"], v.n)
            st = hst.rearrange("p (h k) -> p h k", k=6)
            v.by(dve.tensor_tensor(hm, st[:, :, 1], st[:, :, 4], ALU.add))
            v.by(dve.tensor_tensor(ht, st[:, :, 1], st[:, :, 4], ALU.subtract))
            v.settle(dve, dve.tensor_tensor(hv, st[:, :, 2], st[:, :, 5], ALU.add))
            v.by(dve.tensor_scalar(hm, hm, 0.5, None, ALU.mult))
            v.by(dve.tensor_scalar(hv, hv, 1.0 / D, EPS, ALU.mult, ALU.add))
            v.settle(dve, dve.scalar_tensor_tensor(ht, ht, 0.25, ht, ALU.mult, ALU.mult))
            ask_root(dve.tensor_tensor(hv, hv, ht, ALU.add))
            for h in range(40):
                hh = heads[:, D * h:D * h + D]
                dve.tensor_scalar(hh, hh, hm[:, h:h + 1], hr[:, h:h + 1], ALU.subtract, ALU.mult)\
                   .then_inc(s["heads_ready"], 1)
            dve.wait_ge(s["headT_done"], 1)
            for n in range(2):
                v.by(dve.tensor_scalar(qxT[:, 512 * n:512 * n + 512], bank[n], sm("qxln_w"), sm("qxln_b"), ALU.mult, ALU.add))
            dve.wait_ge(s["headT_done"], 2)
            for n in range(2):
                v.by(dve.tensor_scalar(qT[:, 512 * n:512 * n + 512], bank[2 + n], sm("qln_w"), sm("qln_b"), ALU.mult, ALU.add))
            dve.wait_ge(s["headT_done"], 3)
            v.settle(dve, dve.tensor_scalar(kT, bank[4], sm("kln_w"), sm("kln_b"), ALU.mult, ALU.add))
            v.by(dve.tensor_scalar(mean_w, ones[:, :], 1.0 / D, None, ALU.mult))
            dve.tensor_scalar(qkw, qxT, sm("kxln_w"), None, ALU.mult).then_inc(s["qkT_ready"], 1)
            dve.wait_ge(s["qkT_ready"], 1)
            dve.wait_ge(s["qmean_done"], 1)
            for n in range(2):
                dve.tensor_tensor(qkw[:, 512 * n:512 * n + 512], qkw[:, 512 * n:512 * n + 512], bank[5 + n],
                                  ALU.subtract).then_inc(s["qc_ready"], 1)
            dve.wait_ge(s["s_self"], 1)
            sg = bank[7].rearrange("p (g t) -> p g t", g=G)
            v.settle(dve, dve.tensor_reduce(stat[:, 40:48], sg, X, ALU.max))
            pg = pself.rearrange("p (g t) -> p g t", g=G)
            dve.tensor_tensor(pg, sg, stat[:, 40:48].unsqueeze(2).broadcast_to([128, G, S]), ALU.subtract)\
               .then_inc(s["s_self"], 1)
            dve.wait_ge(s["cbc_done"], 1)
            dve.tensor_scalar(c_col[:, :], bank[0][:, 0:G], float(D) ** -0.5, None, ALU.mult).then_inc(s["c_ready"], 1)
            dve.wait_ge(s["p_self"], 1)
            v.settle(dve, dve.tensor_reduce(stat[:, 48:56], pg, X, ALU.add))
            v.settle(dve, dve.reciprocal(stat[:, 48:56], stat[:, 48:56]))
            dve.tensor_tensor(pg, pg, stat[:, 48:56].unsqueeze(2).broadcast_to([128, G, S]), ALU.mult)\
               .then_inc(s["p_self"], 1)
            dve.wait_ge(s["qk_done"], 1)
            qp = po.rearrange("p (c b) n -> p c (b n)", c=HC)
            v.settle(dve, dve.tensor_copy(q_hi[:, :, :], qp))
            dve.tensor_tensor(q_lo[:, :, :], qp, q_hi[:, :, :].bitcast(F32), ALU.subtract).then_inc(s["q_split"], 1)
            dve.wait_ge(s["pT_self"], 1)
            dve.tensor_copy(pTs.rearrange("p (b n) -> p b n", b=2), pk[0:S, :, :]).then_inc(s["pT_evac"], 1)
            dve.wait_ge(s["core_done"], 1)
            dve.tensor_copy(cat_t[:, 0:1024].rearrange("p (b n) -> p b n", b=2), ps[:, :, :]).then_inc(s["cat_core"], 1)
            v.by(dve.memset(neg_max[:, :], 1e30))
            v.by(dve.memset(o_acc[:, :, :], 0.0))
            v.settle(dve, dve.memset(p_sum[:, :], 0.0))
            dve.wait_ge(s["lin_done"], 12)

            def low_t(j, i):
                b = BUF[i]
                dve.wait_ge(s["ct_half"], j * CH + i + 1)
                dve.tensor_tensor(ct_lo[:, b, :], ct_raw[:, b, :], ct_hi[:, b, :].bitcast(F32),
                                  ALU.subtract).then_inc(s["ct_split"], 1)

            def low_n(j, i):
                b = BUF[i]
                dve.wait_ge(s["cn_half"], j * CH + i + 1)
                dve.tensor_tensor(cn_lo[:, b, :], cn_raw[:, b, :], cn_hi[:, b, :].bitcast(F32),
                                  ALU.subtract).then_inc(s["cn_split"], 1)

            def low_p(j, i, h, probs):
                dve.wait_ge(s["p_hi_ready"], 2 * (j * CH + i) + h + 1)
                dve.tensor_tensor(p_lo[:, h, :], probs, p_hi[:, h, :].bitcast(F32),
                                  ALU.subtract).then_inc(s["p_lo_ready"], 1)

            def sums(j, i):
                for n in range(2):
                    dve.wait_ge(s["ksq_act"], 2 * (j * CH + i) + n + 1)
                    if not (isinstance(j, int) and j == 0 and i == 0):
                        dve.wait_ge(s["rstd_ready"], j * CH + i)
                    dve.tensor_reduce(ss[:, 4 * n:4 * n + 4], ksq[:, n, :].rearrange("p (g d) -> p g d", g=4),
                                      X, ALU.add).then_inc(s["ssum"], 1)

            def evacuate(j, i):
                dve.wait_ge(s["rstd_ready"], j * CH + i + 1)
                if not (isinstance(j, int) and j == 0):
                    dve.wait_ge(s["p_shift"], 2 * (j * CH + i + 1 - CH))
                dve.wait_ge(s["s_mm"], 2 * (j * CH + i) + 1)
                for g in range(4):
                    ins = dve.tensor_scalar(scores[:, i, ROWS * g:ROWS * g + ROWS], ps[:, 0, ROWS * g:ROWS * g + ROWS],
                                            rstd1[:, g:g + 1], None, ALU.mult)
                ins.then_inc(s["evac_v"], 1)

            def row_max(j, i):
                dve.wait_ge(s["evac_v"], j * CH + i + 1)
                dve.wait_ge(s["evac_a"], j * CH + i + 1)
                if i > 1:
                    dve.wait_ge(s["max_done"], j * (CH - 1) + i - 1)
                dve.tensor_tensor(run_max[:, :], scores[:, 0, :] if i == 1 else run_max[:, :], scores[:, i, :],
                                  ALU.max).then_inc(s["max_done"], 1)

            def scale_out(k):
                dve.wait_ge(s["alpha_ready"], k + 1)
                dve.wait_ge(s["merged"], HC * k)
                for c in range(HC):
                    dve.scalar_tensor_tensor(out=o_acc[:, c, :], in0=alpha[:, :], scalar=1.0, in1=o_acc[:, c, :],
                                             op0=ALU.min, op1=ALU.mult).then_inc(s["o_scaled"], 1)

            def merge(k):
                dve.wait_ge(s["pv_rh"], 2 * CH * (k + 1))
                if not (isinstance(k, int) and k == 0):
                    dve.wait_ge(s["o_scaled"], HC * k)
                for c in range(HC):
                    dve.tensor_tensor(o_acc[:, c, :], o_acc[:, c, :],
                                      po[:, 2 * c:2 * c + 2, :].rearrange("p b n -> p (b n)"),
                                      ALU.add).then_inc(s["merged"], 1)

            def maxima(j, k):
                dve.wait_ge(s["rt_done"], j + 1)
                dve.tensor_reduce(mx[:, :], pk.rearrange("p b (g r) -> p (b g) r", g=4), X, ALU.max)\
                   .then_inc(s["mx_raw"], 1)
                dve.wait_ge(s["mx_raw"], j + 1)
                dve.tensor_tensor(mx[:, :], mx[:, :], c_col[:, :], ALU.add).then_inc(s["mx_full"], 1)
                dve.wait_ge(s["mx_full"], j + 1)
                dve.tensor_tensor(mx[:, :], c_col[:, :], mx[:, :], ALU.subtract).then_inc(s["mx_ready"], 1)
                new = ps.rearrange("p b n -> p (b n)")
                if k is not None:
                    dve.wait_ge(s["psum_add"], 2 * CH * (k + 1))
                    dve.wait_ge(s["psum_scaled"], k + 1)
                    if not (isinstance(k, int) and k == 0):
                        dve.wait_ge(s["o_scaled"], HC * k)
                dve.wait_ge(s["mb_done"], j + 1)
                dve.tensor_tensor(alpha[:, :], new, neg_max[:, :], ALU.subtract).then_inc(s["alpha_diff"], 1)
                dve.wait_ge(s["alpha_diff"], j + 1)
                dve.tensor_tensor(neg_max[:, :], neg_max[:, :], new, ALU.min).then_inc(s["max_ready"], 1)
                if k is not None:
                    merge(k)
                dve.wait_ge(s["alpha_ready"], j + 1)
                dve.scalar_tensor_tensor(out=p_sum[:, :], in0=alpha[:, :], scalar=1.0, in1=p_sum[:, :],
                                         op0=ALU.min, op1=ALU.mult).then_inc(s["psum_scaled"], 1)

            low_t(0, 0)
            for i in range(CH):
                sums(0, i)
                low_t((i + 1) // CH, (i + 1) % CH)
                evacuate(0, i)
                if i:
                    row_max(0, i)
            maxima(0, None)

            def dve_chunk(j, k, last=False):
                for i in range(CH):
                    low_n(k, i)
                    low_p(k, i, 0, p_f[:, 0, :])
                    sums(j, i)
                    low_p(k, i, 1, p_f[:, 1, :])
                    if i < CH - 1:
                        low_t(j, i + 1)
                    elif not last:
                        low_t(j + 1, 0)
                    evacuate(j, i)
                    if i:
                        row_max(j, i)
                    elif not (isinstance(k, int) and k == 0):
                        scale_out(k)
                maxima(j, k)

            dve_chunk(1, 0)
            with dve.Fori(2, NCH - 1) as j:
                dve_chunk(j, j - 1)
            dve_chunk(NCH - 1, NCH - 2, last=True)

            def shift_last(i):
                for h in range(2):
                    q = scores[:, i, 512 * h:512 * h + 512]
                    dve.tensor_tensor(q, q, neg_max[:, 512 * h:512 * h + 512], ALU.add).then_inc(s["p_shift"], 1)

            dve.wait_ge(s["max_ready"], NCH)
            shift_last(0)
            for i in range(CH):
                if i < CH - 1:
                    shift_last(i + 1)
                low_n(NCH - 1, i)
                for h in range(2):
                    low_p(NCH - 1, i, h, scores[:, i, 512 * h:512 * h + 512])
                if i == 0:
                    scale_out(NCH - 1)
            merge(NCH - 1)
            dve.wait_ge(s["merged"], HC * NCH)
            dve.wait_ge(s["den_done"], 1)
            v.settle(dve, dve.reciprocal(neg_max[:, :], pk.rearrange("p b n -> p (b n)")))
            for c in range(HC):
                dve.tensor_tensor(o_acc[:, c, :], o_acc[:, c, :], neg_max[:, :], ALU.mult).then_inc(s["on_ready"], 1)
            dve.wait_ge(s["xo_done"], 1)
            v.by(dve.tensor_copy(cat_t[:, 1024:2048].rearrange("p (b n) -> p b n", b=2), ps[:, :, :]))
            v.settle(dve, dve.reciprocal(stat[:, 0:32], sm("smooth")))
            cat3 = cat_t[:, :].rearrange("p (h t) -> p h t", h=32)
            v.settle(dve, dve.tensor_tensor(cat3, cat3, stat[:, 0:32].unsqueeze(2).broadcast_to([128, 32, S]), ALU.mult))
            fp8_round(cat_t[:, :], cat_t[:, :], scores[:, 3, :].bitcast(BF16), scores[:, 4, :].bitcast(BF16),
                      scores[:, 5:7, :].rearrange("p a b -> p (a b)"), s["catq_ready"])
            v.settle(dve, dve.tensor_scalar(stat[0:S, 40:41], sm("pw_s", S), sm("pin_s", S), None, ALU.mult))
            dve.wait_ge(s["proj_done"], 1)
            dve.scalar_tensor_tensor(out=x_res[:, :], in0=bank[0][0:S, 0:H], scalar=stat[0:S, 40:41],
                                     in1=x_res[:, :], op0=ALU.mult, op1=ALU.add).then_inc(s["x1_ready"], 1)
            dve.wait_ge(s["x1_ready"], 1)
            if upto > 1:
                second_vector(dve, s, ph2, v, layernorm_rows, bank, small, x_res, ident)

        @block.tensor
        def _(pe):
            pe.wait_ge(s["const_ready"], 1)
            pe.wait_ge(s["normed"], 2)
            for c in range(HC):
                ins = pe.transpose(bank[0][:, c * S:c * S + S], xn[:, 128 * c:128 * c + 128], ident[0:S, 0:S])
            ins.then_inc(s["xT_done"], 1)
            n = 0
            for k, (w, key, count) in enumerate(((wqx, "w_qx", 4), (wq, "w_q", 4), (wk, "w_k", 2), (wv, "w_v", 2))):
                pe.wait_ge(s["xq_ready"], HC * (k + 1))
                pe.wait_ge(s[key], 16)
                for b in range(count):
                    if n >= 8:
                        pe.wait_ge(s["lin_evac"], n - 7)
                    for c in range(HC):
                        ins = pe.matmul(bank[n % 8][0:S, :], xq[k][:, c * S:c * S + S], w[:, c, 512 * b:512 * b + 512],
                                        start=(c == 0), stop=(c == HC - 1))
                    ins.then_inc(s["lin_done"], 1)
                    n += 1
            pe.wait_ge(s["lin_evac"], 12)
            for h in range(40):
                pe.wait_ge(s["heads_ready"], h + 1)
                ins = pe.transpose(bank[h // 8][:, S * (h % 8):S * (h % 8) + S], heads[:, D * h:D * h + D], ident[0:S, 0:S])
                if h in (15, 31, 39):
                    ins.then_inc(s["headT_done"], 1)
            pe.wait_ge(s["qkT_ready"], 1)
            for b in range(2):
                ins = pe.matmul(bank[5 + b], mean_w, qkw[:, 512 * b:512 * b + 512], start=True, stop=True)
            ins.then_inc(s["qmean_done"], 1)
            for g in range(G):
                ins = pe.matmul(bank[7][:, S * g:S * g + S], qT[:, ROWS * g:ROWS * g + ROWS], kT[:, S * g:S * g + S],
                                start=True, stop=True)
            ins.then_inc(s["s_self"], 1)
            for g in range(G):
                ins = pe.matmul(bank[0][:, g:g + 1], qxT[:, ROWS * g:ROWS * g + ROWS], sm("kxln_b"), start=True, stop=True)
            ins.then_inc(s["cbc_done"], 1)
            pe.wait_ge(s["c_ready"], 1)
            pe.wait_ge(s["qc_ready"], 2)
            pe.wait_ge(s["kxd_in"], 16)
            for c in range(HC):
                for g in range(G):
                    ins = pe.matmul(po[:, 2 * c + g // 4, ROWS * (g % 4):ROWS * (g % 4) + ROWS],
                                    kxd[:, g, 128 * c:128 * c + 128], qkw[:, ROWS * g:ROWS * g + ROWS],
                                    start=True, stop=True)
            ins.then_inc(s["qk_done"], 1)
            pe.wait_ge(s["p_self"], 2)
            for g in range(G):
                ins = pe.transpose(pk[0:S, g // 4, ROWS * (g % 4):ROWS * (g % 4) + ROWS], pself[:, S * g:S * g + S], ident[:, :])
            ins.then_inc(s["pT_self"], 1)
            pe.wait_ge(s["pT_evac"], 1)
            for g in range(G):
                ins = pe.matmul(ps[:, g // 4, ROWS * (g % 4):ROWS * (g % 4) + ROWS], vrow[:, D * g:D * g + D],
                                pTs[:, ROWS * g:ROWS * g + ROWS], start=True, stop=True)
            ins.then_inc(s["core_done"], 1)
            pe.wait_ge(s["q_split"], 1)
            pe.wait_ge(s["k_split"], 1)
            pe.wait_ge(s["cat_core"], 1)

            def product(out, lo_hi, w_hi, w_lo, b, n):
                hi, lo = lo_hi
                k = 0
                for c in range(HC):
                    st = hi[:, b, 128 * c:128 * c + 128]
                    for w in (w_hi, w_lo):
                        pe.matmul(out, st, w[:, c, 512 * n:512 * n + 512], start=(k == 0), stop=False)
                        k += 1
                for c in range(HC):
                    ins = pe.matmul(out, lo[:, b, 128 * c:128 * c + 128], w_hi[:, c, 512 * n:512 * n + 512],
                                    start=False, stop=(c == HC - 1))
                return ins

            def keys_scores(j, i):
                b = BUF[i]
                pe.wait_ge(s["ct_split"], j * CH + i + 1)
                for n in range(2):
                    if not (isinstance(j, int) and j == 0 and i == 0):
                        pe.wait_ge(s["ksq_act"], 2 * (j * CH + i) + n - 1)
                        if i == 0:
                            pe.wait_ge(s["mx_raw"], j)
                    product(pk[:, n, :], (ct_hi, ct_lo), k_hi, k_lo, b, n).then_inc(s["ksq_mm"], 1)
                for n in range(2):
                    if not (isinstance(j, int) and j == 0 and i == 0):
                        pe.wait_ge(s["evac_a" if n else "evac_v"], j * CH + i)
                        if i == 0:
                            pe.wait_ge(s["max_ready"], j)
                    product(ps[:, n, :], (ct_hi, ct_lo), q_hi, q_lo, b, n).then_inc(s["s_mm"], 1)

            def weighted(j, i):
                b = BUF[i]
                pe.wait_ge(s["cn_split"], j * CH + i + 1)
                if i == 0 and not (isinstance(j, int) and j == 0):
                    pe.wait_ge(s["merged"], HC * j)
                for h in range(2):
                    pe.wait_ge(s["p_lo_ready"], 2 * (j * CH + i) + h + 1)
                    for c in range(HC):
                        out = po[:, 2 * c + h, :]
                        st = cn_hi[:, b, 128 * c:128 * c + 128]
                        pe.matmul(out, st, p_hi[:, h, :], start=(i == 0), stop=False)
                        pe.matmul(out, st, p_lo[:, h, :], start=False, stop=False)
                        ins = pe.matmul(out, cn_lo[:, b, 128 * c:128 * c + 128], p_hi[:, h, :],
                                        start=False, stop=(i == CH - 1))
                    ins.then_inc(s["pv_rh"], 1)

            def turn_max(j):
                pe.wait_ge(s["max_done"], (CH - 1) * (j + 1))
                pe.wait_ge(s["ksq_act"], 2 * CH * (j + 1))
                for g in range(G):
                    ins = pe.transpose(pk[:, g // 4, ROWS * (g % 4):ROWS * (g % 4) + ROWS],
                                       run_max[:, ROWS * g:ROWS * g + ROWS], ident[:, :])
                ins.then_inc(s["rt_done"], 1)

            def spread_max(j):
                pe.wait_ge(s["mx_ready"], j + 1)
                pe.wait_ge(s["evac_v"], CH * (j + 1))
                pe.wait_ge(s["evac_a"], CH * (j + 1))
                for g in range(G):
                    ins = pe.transpose(ps[:, g // 4, ROWS * (g % 4):ROWS * (g % 4) + ROWS],
                                       mx[:, g:g + 1].broadcast_to([128, 128]), ident[:, :])
                ins.then_inc(s["mb_done"], 1)

            for i in range(CH):
                keys_scores(0, i)
            turn_max(0)
            spread_max(0)

            def pe_chunk(j, k):
                for i in range(CH):
                    keys_scores(j, i)
                    weighted(k, i)
                turn_max(j)
                spread_max(j)

            pe_chunk(1, 0)
            with pe.Fori(2, NCH) as j:
                pe_chunk(j, j - 1)
            for i in range(CH):
                weighted(NCH - 1, i)
            pe.wait_ge(s["psum_add"], 2 * CH * NCH)
            for b in range(2):
                ins = pe.matmul(pk[:, b, :], ones[:, :], p_sum[:, 512 * b:512 * b + 512], start=True, stop=True)
            ins.then_inc(s["den_done"], 1)
            pe.wait_ge(s["on_ready"], HC)
            pe.wait_ge(s["wv_in"], 16)
            for g in range(G):
                for c in range(HC):
                    ins = pe.matmul(ps[:, g // 4, ROWS * (g % 4):ROWS * (g % 4) + ROWS],
                                    wv_x[:, c, D * g:D * g + D], o_acc[:, c, ROWS * g:ROWS * g + ROWS],
                                    start=(c == 0), stop=(c == HC - 1))
            ins.then_inc(s["xo_done"], 1)
            pe.wait_ge(s["catq_ready"], 1)
            pe.wait_ge(s["wproj_in"], 16)
            for k in range(32):
                ins = pe.matmul(bank[0][0:S, 0:H], cat_t[:, S * k:S * k + S], mid[:, H * k:H * k + H],
                                start=(k == 0), stop=(k == 31))
            ins.then_inc(s["proj_done"], 1)
            if upto > 1:
                second_tensor(pe, s, ph2, bank, small, ident, ones, wide, mid)


def second_memory(m, sb):
    area = sb("area", [128, 27000])

    def at(a, n, rows=128):
        return area[0:rows, a:a + n]

    m["raw"] = at(0, 4288).rearrange("p (c t) -> p c t", t=S + 3)
    m["u"] = at(0, 4096, S)
    m["cv"] = at(4288, 4096)
    m["y"] = at(4288, 2048, S)
    m["yt"] = at(6336, 2048, S)
    m["gt"] = at(8384, 2048, S)
    m["bv"] = at(8384, 4096, S)
    m["o"] = at(8384, 2048)
    m["o2"] = at(10432, 2048)
    m["zs"] = at(12480, 2048)
    m["sq"] = at(14528, 2048)
    m["z"] = at(14528, 2048, S)
    m["tap"] = at(16576, 2048).rearrange("p (b k n) -> p b k n", b=2, k=2)
    m["lm"] = [at(16576, 2048, S), at(18624, 2048, S)]
    m["gam"] = at(18624, 2048, S)
    m["a_t"] = at(20672, 2048, S)
    m["l"] = at(22720, 2048, S)
    m["tap2"] = at(24768, 1024).rearrange("p (b n) -> p b n", b=2)
    b = 25792
    for name, n, rows in (("xn", 256, S), ("h_t", 128, 128), ("tri", 64, S), ("strict", 64, S), ("far", 64, S),
                          ("g", 32, S), ("beta", 32, S), ("t1", 32, S), ("t2", 32, S), ("t3", 32, S), ("cg", 32, S),
                          ("ea", 32, S)):
        m[name] = at(b, n, rows)
        b += n
    m["mask"] = at(b, 384, S)
    m["rn"] = at(b + 384, 16)
    m["down"] = at(0, 8192)
    m["hx"] = at(8384, 2304)
    m["comb_bc"] = at(10688, 512)
    m["comb_d"] = at(11200, 512, S)
    m["route"] = at(11712, 128, S)
    m["base_up"] = at(16576, 2048)
    m["base_down"] = at(18624, 1024)


SECOND = """wqkv_in normed ct_half cn_half ss_eps o_scaled out_ready wz_in wout_in up_in down_in base_in hT_done
    hT_ready ba_done gates_a gates_b gates_c ea_done sp_done g_ready cg_done cg_ready gt_ready cgb_done
    qkv_mm qkv_in pad_ready tap_ready conv_ready silu_ready z_mm z_silu sq_ready sq_mm norm_in norm_pow
    norm_diag norm_bc normed_qk vT_done bv_ready gam_diff gam_ready l_masked kk_done at_ready l_ready
    lm_ready masks_ready cy_mm cy_in d_mm y_new u_mm u_in o_mm o_ready o_sq o_ms ms_in ms_pow ms_diag
    ms_bc yn_ready out_mm x2_ready x3T_done x3T_ready logit_done r_exp comb_ready combb_done combb_ready
    up_mm gate_silu hid_part hid_ready down_mm""".split()
EXPERT_ORDER = [EXPERTS] + list(range(EXPERTS))


def second_loads(sp, s, t, m, wide, mid):
    sp.wait_ge(s["proj_done"], 1)
    sp.dma_start(mid[:, :], t["W_z"], max_dma_last_dim=8192).then_inc(s["wz_in"], 16)
    sp.wait_ge(s["qkv_mm"], 8)
    sp.dma_start(wide[:, :], t["up"], max_dma_last_dim=8192).then_inc(s["up_in"], 16)
    sp.wait_ge(s["z_mm"], 4)
    sp.dma_start(mid[:, :], t["W_out"], max_dma_last_dim=8192).then_inc(s["wout_in"], 16)
    sp.wait_ge(s["o_mm"], 4)
    sp.dma_start(m["base_up"], t["base_up"]).then_inc(s["base_in"], 16)
    sp.dma_start(m["base_down"], t["base_down"]).then_inc(s["base_in"], 16)
    sp.dma_start(m["down"], t["down"], max_dma_last_dim=8192).then_inc(s["down_in"], 16)


def second_pool(pool, s, m, inv_root, ident, cst, small):
    pool.wait_ge(s["x1_ready"], 1)
    pool.memset(m["tri"], 1.0).then_inc(s["pool_step"], 1)
    pool.memset(m["strict"], 1.0).then_inc(s["pool_step"], 1)
    pool.memset(m["raw"][:, :, 0:3], 0.0).then_inc(s["pad_ready"], 1)
    pool.wait_ge(s["pool_step"], 5)
    pool.affine_select(out=m["tri"], in_=m["tri"], compare_op=ALU.is_ge, fill=0.0, base=0,
                       pattern=[[1, S]], channel_multiplier=-1).then_inc(s["pool_step"], 1)
    pool.affine_select(out=m["strict"], in_=m["strict"], compare_op=ALU.is_gt, fill=0.0, base=0,
                       pattern=[[-1, S]], channel_multiplier=1).then_inc(s["pool_step"], 1)
    pool.iota(m["far"].bitcast(I32), [[1, S]], base=0, channel_multiplier=0).then_inc(s["pool_step"], 1)
    pool.iota(m["mask"][:, 0:S].bitcast(I32), [[0, S]], base=0, channel_multiplier=1).then_inc(s["pool_step"], 1)
    inv_root(m["stat"][0:S, 8:9], m["stat"][0:S, 7:8], S, 1)
    w = small[:, SMALL["conv"][0]:SMALL["conv"][0] + 256].rearrange("p (c j) -> p c j", j=4)
    for n in range(8):
        c = slice(8 * n, 8 * n + 8)
        pool.wait_ge(s["qkv_in"], n + 1)
        if n >= 2:
            pool.wait_ge(s["conv_ready"], n - 1)
        for k in range(2):
            pool.tensor_tensor(m["tap"][:, n % 2, k, :].rearrange("p (c t) -> p c t", t=S), m["raw"][:, c, k:k + S],
                               w[:, c, k:k + 1].broadcast_to([128, 8, S]), ALU.mult).then_inc(s["pool_step"], 1)
        pool.wait_ge(s["pool_step"], 9 + 2 * n + 2)
        pool.tensor_tensor(m["tap"][:, n % 2, 0, :], m["tap"][:, n % 2, 0, :], m["tap"][:, n % 2, 1, :],
                           ALU.add).then_inc(s["tap_ready"], 1)
    pool.wait_ge(s["norm_in"], 1)
    pool.tensor_tensor(m["rn"], m["rn"], cst[:, 0:1].broadcast_to([128, 16]), ALU.pow).then_inc(s["norm_pow"], 1)
    for q in range(4):
        pool.wait_ge(s["gam_ready"], q + 1)
        pool.tensor_tensor(by_head(m["l"], q), by_head(m["gam"], q), over_heads(m["strict"]),
                           ALU.mult).then_inc(s["l_masked"], 1)
    for lv in range(6):
        for q in range(4):
            pool.wait_ge(s["l_ready"], 4)
            pool.wait_ge(s["masks_ready"], 6)
            if lv == 1:
                pool.wait_ge(s["at_ready"], 4)
            if lv >= 2:
                pool.wait_ge(s["cy_mm"], 4 * (lv - 2) + q + 1)
                pool.wait_ge(s["y_new"], 8)
            pool.tensor_tensor(by_head(m["lm"][lv % 2], q), by_head(m["l"], q), over_heads(m["mask"][:, S * lv:S * lv + S]),
                               ALU.mult).then_inc(s["lm_ready"], 1)
    pool.wait_ge(s["ms_in"], 1)
    pool.tensor_tensor(m["rn"], m["rn"], cst[:, 0:1].broadcast_to([128, 16]), ALU.pow).then_inc(s["ms_pow"], 1)
    inv_root(m["stat"][0:S, 8:9], m["stat"][0:S, 7:8], S, 1)
    pool.wait_ge(s["combb_ready"], 1)
    for n, e in enumerate(EXPERT_ORDER):
        if e == EXPERTS:
            continue
        pool.wait_ge(s["hid_part"], n + 1)
        hx = m["hx"][:, 256 * n:256 * n + 256].rearrange("p (k t) -> p k t", t=S)
        pool.tensor_tensor(hx, hx, m["comb_bc"][:, S * e:S * e + S].unsqueeze(1).broadcast_to([128, 4, S]),
                           ALU.mult).then_inc(s["hid_ready"], 1)


def by_head(a, q):
    return a[:, 512 * q:512 * q + 512].rearrange("p (h t) -> p h t", t=S)


def over_heads(a):
    return a.unsqueeze(1).broadcast_to([a.shape[0], 8, a.shape[1]])


def over_tokens(a, q):
    return a[:, 8 * q:8 * q + 8].unsqueeze(2).broadcast_to([a.shape[0], 8, S])


def second_scalar(act, s, m, bank, small):
    act.wait_ge(s["ba_done"], 1)
    act.activation(m["t1"], bank[6][0:S, 0:32], ACT.Exp, scale=-1.0).then_inc(s["gates_a"], 1)
    a = SMALL["A_log"][0]
    act.activation(m["ea"], small[0:S, a:a + 32], ACT.Exp).then_inc(s["ea_done"], 1)
    act.wait_ge(s["gates_b"], 1)
    act.activation(m["t3"], m["t3"], ACT.Exp, scale=-1.0).then_inc(s["gates_c"], 1)
    act.wait_ge(s["gates_c"], 1)
    act.activation(m["t3"], m["t3"], ACT.Ln, bias=m["stat"][0:S, 15:16]).then_inc(s["sp_done"], 1)
    act.wait_ge(s["pad_ready"], 1)

    def silu(n):
        c = m["cv"][:, 512 * n:512 * n + 512]
        act.wait_ge(s["conv_ready"], n + 1)
        act.activation(c, c, ACT.Silu).then_inc(s["silu_ready"], 1)

    for n in range(8):
        act.wait_ge(s["qkv_mm"], n + 1)
        act.copy(m["raw"][:, 8 * n:8 * n + 8, 3:S + 3], bank[n % 4].rearrange("p (c t) -> p c t", t=S))\
           .then_inc(s["qkv_in"], 1)
        if n >= 2:
            silu(n - 2)
    silu(6)
    silu(7)
    for n in range(4):
        act.wait_ge(s["z_mm"], n + 1)
        act.activation(m["zs"][:, 512 * n:512 * n + 512], bank[n], ACT.Silu).then_inc(s["z_silu"], 1)
    for n in range(4):
        act.wait_ge(s["silu_ready"], 8)
        act.activation(m["sq"][:, 512 * n:512 * n + 512], m["cv"][:, 512 * n:512 * n + 512], ACT.Square)\
           .then_inc(s["sq_ready"], 1)
    for q in range(4):
        gq = m["gam"][:, 512 * q:512 * q + 512]
        act.wait_ge(s["gam_diff"], q + 1)
        act.activation(gq, gq, ACT.Exp, scale=-1.0).then_inc(s["gam_ready"], 1)
    for lv in range(1, 6):
        for q in range(4):
            act.wait_ge(s["cy_mm"], 4 * lv + q + 1)
            if lv > 1:
                act.wait_ge(s["d_mm"], 4 * (lv - 2) + q + 1)
            act.copy(m["z"][:, 512 * q:512 * q + 512], bank[q][0:S, :]).then_inc(s["cy_in"], 1)
    for n in range(8):
        act.wait_ge(s["u_mm"], n + 1)
        act.copy(m["u"][:, 512 * n:512 * n + 512], bank[n][0:S, :]).then_inc(s["u_in"], 1)
    for n in range(4):
        act.wait_ge(s["o_ready"], n + 1)
        act.activation(m["o2"][:, 512 * n:512 * n + 512], m["o"][:, 512 * n:512 * n + 512], ACT.Square)\
           .then_inc(s["o_sq"], 1)
    act.wait_ge(s["logit_done"], 2)
    act.activation(m["route"][:, 0:8], m["route"][:, 0:8], ACT.Exp).then_inc(s["r_exp"], 1)
    for n in range(9):
        act.wait_ge(s["up_mm"], n + 1)
        act.activation(m["hx"][:, 256 * n:256 * n + 256], bank[n % 4][:, 0:256], ACT.Silu).then_inc(s["gate_silu"], 1)


def second_vector(dve, s, m, v, layernorm_rows, bank, small, x_res, ident):
    def diagonals(dst, n):
        return dve.tensor_tensor(dst[:, 512 * n:512 * n + 512].rearrange("p (k t) -> p k t", k=4),
                                 m["rn"][:, 4 * n:4 * n + 4].unsqueeze(2).broadcast_to([128, 4, 128]),
                                 ident[:, :].unsqueeze(1).broadcast_to([128, 4, 128]), ALU.mult)

    layernorm_rows(m["xn"], x_res[:, :])
    dve.wait_ge(s["hT_done"], 1)
    dve.tensor_copy(m["h_t"], bank[7][:, 0:128]).then_inc(s["hT_ready"], 1)
    dve.wait_ge(s["pool_step"], 9)
    far, mask = m["far"], m["mask"]
    v.settle(dve, dve.tensor_tensor(far.bitcast(I32), far.bitcast(I32), mask[:, 0:S].bitcast(I32), ALU.bitwise_xor))
    v.settle(dve, dve.tensor_copy(far, far.bitcast(I32)))
    for lv in range(6):
        mk = mask[:, S * lv:S * lv + S]
        v.settle(dve, dve.tensor_scalar(mk, far, float(1 << lv), None, ALU.is_ge))
        dve.scalar_tensor_tensor(out=mk, in0=far, scalar=float(2 << lv), in1=mk, op0=ALU.is_lt, op1=ALU.mult)\
           .then_inc(s["masks_ready"], 1)
    one = m["stat"][0:S, 15:16]
    v.by(dve.memset(one, 1.0))
    dve.wait_ge(s["ba_done"], 1)
    dve.wait_ge(s["gates_a"], 1)
    a = SMALL["dt_bias"][0]
    v.settle(dve, dve.tensor_tensor(m["t2"], bank[6][0:S, 32:64], small[0:S, a:a + 32], ALU.add))
    dve.scalar_tensor_tensor(out=m["t3"], in0=m["t2"], scalar=-1.0, in1=m["t2"], op0=ALU.mult, op1=ALU.max).then_inc(s["gates_b"], 1)
    v.settle(dve, dve.tensor_scalar(m["t1"], m["t1"], 1.0, None, ALU.add))
    v.by(dve.reciprocal(m["beta"], m["t1"]))
    dve.wait_ge(s["sp_done"], 1)
    v.settle(dve, dve.scalar_tensor_tensor(out=m["t3"], in0=m["t2"], scalar=0.0, in1=m["t3"], op0=ALU.max, op1=ALU.add))
    dve.wait_ge(s["ea_done"], 1)
    dve.scalar_tensor_tensor(out=m["g"], in0=m["t3"], scalar=-1.0, in1=m["ea"], op0=ALU.mult, op1=ALU.mult)\
       .then_inc(s["g_ready"], 1)
    dve.wait_ge(s["g_ready"], 1)
    for q in range(4):
        dve.tensor_tensor(by_head(m["gt"], q), over_tokens(m["g"], q), over_heads(m["tri"]), ALU.mult)\
           .then_inc(s["gt_ready"], 1)
    dve.wait_ge(s["cg_done"], 1)
    dve.tensor_copy(m["cg"], bank[6][0:S, 64:96]).then_inc(s["cg_ready"], 1)
    w = small[:, SMALL["conv"][0]:SMALL["conv"][0] + 256].rearrange("p (c j) -> p c j", j=4)
    for n in range(8):
        c = slice(8 * n, 8 * n + 8)
        out = m["cv"][:, 512 * n:512 * n + 512]
        tap = m["tap2"][:, n % 2, :]
        dve.wait_ge(s["qkv_in"], n + 1)
        v.by(dve.tensor_tensor(out.rearrange("p (c t) -> p c t", t=S), m["raw"][:, c, 3:S + 3],
                               w[:, c, 3:4].broadcast_to([128, 8, S]), ALU.mult))
        v.settle(dve, dve.tensor_tensor(tap.rearrange("p (c t) -> p c t", t=S), m["raw"][:, c, 2:S + 2],
                                        w[:, c, 2:3].broadcast_to([128, 8, S]), ALU.mult))
        v.settle(dve, dve.tensor_tensor(out, out, tap, ALU.add))
        dve.wait_ge(s["tap_ready"], n + 1)
        dve.tensor_tensor(out, out, m["tap"][:, n % 2, 0, :], ALU.add).then_inc(s["conv_ready"], 1)
    dve.wait_ge(s["conv_ready"], 8)
    dve.wait_ge(s["cgb_done"], 1)
    for q in range(4):
        v.settle(dve, dve.tensor_tensor(by_head(m["gam"], q), by_head(bank[4 + q][0:S, :], 0), over_tokens(m["cg"], q),
                                        ALU.subtract))
        gq = m["gam"][:, 512 * q:512 * q + 512]
        dve.scalar_tensor_tensor(out=gq, in0=gq, scalar=-1.0, in1=gq, op0=ALU.mult, op1=ALU.max).then_inc(s["gam_diff"], 1)
    dve.wait_ge(s["sq_mm"], 1)
    dve.tensor_scalar(m["rn"], bank[4][:, 0:16], 1e-24, None, ALU.max).then_inc(s["norm_in"], 1)
    dve.wait_ge(s["norm_pow"], 1)
    for n in range(4):
        diagonals(m["sq"], n).then_inc(s["norm_diag"], 1)
    for n in range(4):
        dve.wait_ge(s["norm_bc"], n + 1)
        c = m["cv"][:, 512 * n:512 * n + 512]
        dve.tensor_tensor(c, c, bank[4 + n], ALU.mult).then_inc(s["normed_qk"], 1)
    for n in range(8):
        dve.wait_ge(s["vT_done"], n + 1)
        dve.tensor_tensor(m["bv"][:, 512 * n:512 * n + 512].rearrange("p (h d) -> p h d", d=D),
                          bank[n][0:S, :].rearrange("p (h d) -> p h d", d=D),
                          m["beta"][:, 4 * n:4 * n + 4].unsqueeze(2).broadcast_to([S, 4, D]), ALU.mult)\
           .then_inc(s["bv_ready"], 1)
    for q in range(4):
        dve.wait_ge(s["gam_ready"], q + 1)
        v.by(dve.tensor_tensor(by_head(m["a_t"], q), by_head(m["gam"], q), over_heads(m["tri"]), ALU.mult))
        dve.wait_ge(s["l_masked"], q + 1)
        v.settle(dve, dve.tensor_tensor(by_head(m["l"], q), by_head(m["l"], q), over_tokens(m["beta"], q), ALU.mult))
    dve.wait_ge(s["kk_done"], 1)
    for q in range(4):
        for name, b, done in (("l", 0, "l_ready"), ("a_t", 2, "at_ready")):
            pair = m[name][:, 512 * q:512 * q + 512].rearrange("p (k e t) -> p k e t", e=2, t=S)
            prod = bank[b + q // 2][0:S, 256 * (q % 2):256 * (q % 2) + 256].rearrange("p (k t) -> p k t", t=S)
            dve.tensor_tensor(pair, pair, prod.unsqueeze(2).broadcast_to([S, 4, 2, S]), ALU.mult).then_inc(s[done], 1)
    for q in range(4):
        dve.wait_ge(s["cy_mm"], q + 1)
        dve.tensor_tensor(by_head(m["y"], q), over_heads(ident[0:S, 0:S]), by_head(bank[q][0:S, :], 0), ALU.subtract)\
           .then_inc(s["y_new"], 1)
        dve.tensor_tensor(by_head(m["yt"], q), over_heads(ident[0:S, 0:S]), by_head(m["lm"][0], q), ALU.subtract)\
           .then_inc(s["y_new"], 1)
    for lv in range(1, 6):
        for q in range(4):
            dve.wait_ge(s["d_mm"], 4 * (lv - 1) + q + 1)
            dve.wait_ge(s["y_new"], 8 * (lv - 1) + 2 * q + 2)
            for k, name in enumerate(("y", "yt") if lv < 5 else ("y",)):
                a = m[name][:, 512 * q:512 * q + 512]
                dve.tensor_tensor(a, a, bank[4 + 2 * (q % 2) + k][0:S, :], ALU.subtract).then_inc(s["y_new"], 1)
    for n in range(4):
        dve.wait_ge(s["o_mm"], n + 1)
        c = slice(512 * n, 512 * n + 512)
        dve.wait_ge(s["z_silu"], n + 1)
        dve.tensor_tensor(m["o"][:, c], bank[n], m["zs"][:, c], ALU.mult).then_inc(s["o_ready"], 1)
    dve.wait_ge(s["o_ms"], 1)
    dve.tensor_scalar(m["rn"], bank[4][:, 0:16], 1.0 / D, 1e-6, ALU.mult, ALU.add).then_inc(s["ms_in"], 1)
    dve.wait_ge(s["ms_pow"], 1)
    for n in range(4):
        diagonals(m["o2"], n).then_inc(s["ms_diag"], 1)
    for n in range(4):
        c = slice(512 * n, 512 * n + 512)
        dve.wait_ge(s["ms_bc"], n + 1)
        a = SMALL["norm_w"][0]
        dve.wait_ge(s["o_ready"], n + 1)
        dve.scalar_tensor_tensor(out=m["o"][:, c], in0=m["o"][:, c], scalar=small[:, a:a + 1], in1=bank[4 + n],
                                 op0=ALU.mult, op1=ALU.mult).then_inc(s["yn_ready"], 1)
    dve.wait_ge(s["out_mm"], 1)
    dve.tensor_tensor(x_res[:, :], x_res[:, :], bank[0][0:S, 0:H], ALU.add).then_inc(s["x2_ready"], 1)
    dve.wait_ge(s["x2_ready"], 1)
    layernorm_rows(m["xn"], x_res[:, :])
    dve.wait_ge(s["x3T_done"], 1)
    dve.tensor_copy(m["h_t"], bank[7][:, 0:128]).then_inc(s["x3T_ready"], 1)
    r = m["route"]
    p, w1, w2, pos, pick, top, tot = (r[:, 8 * k:8 * k + 8] for k in range(7))

    def first_best(out, vals, best):
        v.settle(dve, dve.tensor_reduce(best, vals, X, ALU.max))
        v.settle(dve, dve.tensor_scalar(pick, vals, best, None, ALU.is_ge))
        v.settle(dve, dve.tensor_tensor(pick, pick, pos, ALU.mult))
        v.settle(dve, dve.tensor_reduce(tot[:, 7:8], pick, X, ALU.max))
        v.settle(dve, dve.tensor_scalar(out, pos, tot[:, 7:8], None, ALU.is_equal))

    for e in range(EXPERTS):
        v.by(dve.memset(pos[:, e:e + 1], float(EXPERTS - e)))
    dve.wait_ge(s["logit_done"], 1)
    lg = bank[6][0:S, 0:EXPERTS]
    v.settle(dve, dve.tensor_reduce(top[:, 0:1], lg, X, ALU.max))
    dve.tensor_scalar(p, lg, top[:, 0:1], None, ALU.subtract).then_inc(s["logit_done"], 1)
    dve.wait_ge(s["r_exp"], 1)
    v.settle(dve, dve.tensor_reduce(top[:, 1:2], p, X, ALU.add))
    v.settle(dve, dve.reciprocal(top[:, 1:2], top[:, 1:2]))
    v.settle(dve, dve.tensor_scalar(p, p, top[:, 1:2], None, ALU.mult))
    first_best(w1, p, top[:, 2:3])
    v.settle(dve, dve.scalar_tensor_tensor(out=w2, in0=w1, scalar=-2.0, in1=p, op0=ALU.mult, op1=ALU.add))
    v.settle(dve, dve.tensor_copy(r[:, 56:64], w2))
    first_best(w2, r[:, 56:64], top[:, 3:4])
    v.settle(dve, dve.tensor_tensor(top[:, 4:5], top[:, 2:3], top[:, 3:4], ALU.add))
    v.settle(dve, dve.reciprocal(top[:, 4:5], top[:, 4:5]))
    v.settle(dve, dve.tensor_tensor(w1, w1, w2, ALU.add))
    v.settle(dve, dve.scalar_tensor_tensor(out=p, in0=p, scalar=top[:, 4:5], in1=w1, op0=ALU.mult, op1=ALU.mult))
    dve.tensor_tensor(by_head(m["comb_d"], 0), p.unsqueeze(2).broadcast_to([S, EXPERTS, S]), over_heads(ident[0:S, 0:S]),
                      ALU.mult).then_inc(s["comb_ready"], 1)
    dve.wait_ge(s["combb_done"], 1)
    dve.tensor_copy(m["comb_bc"], bank[5]).then_inc(s["combb_ready"], 1)
    for n in range(9):
        dve.wait_ge(s["gate_silu"], n + 1)
        hx = m["hx"][:, 256 * n:256 * n + 256]
        dve.tensor_tensor(hx, hx, bank[n % 4][:, 256:512], ALU.mult).then_inc(s["hid_part"], 1)
    dve.wait_ge(s["down_mm"], 1)
    dve.tensor_tensor(x_res[:, :], x_res[:, :], bank[4][0:S, 0:H], ALU.add).then_inc(s["out_ready"], 1)


def second_tensor(pe, s, m, bank, small, ident, ones, wide, mid):
    h_t = m["h_t"]

    def turn(done):
        for c in range(HC):
            ins = pe.transpose(bank[7][:, c * S:c * S + S], m["xn"][:, 128 * c:128 * c + 128], ident[0:S, 0:S])
        ins.then_inc(s[done], 1)

    pe.wait_ge(s["normed"], 3)
    turn("hT_done")
    pe.wait_ge(s["hT_ready"], 1)
    a = SMALL["W_ba"][0]
    for c in range(HC):
        ins = pe.matmul(bank[6][0:S, 0:64], h_t[:, S * c:S * c + S], small[:, a + 64 * c:a + 64 * c + 64],
                        start=(c == 0), stop=(c == HC - 1))
    ins.then_inc(s["ba_done"], 1)
    pe.wait_ge(s["wqkv_in"], 16)
    w = wide[:, :].rearrange("p (h n) -> p h n", h=HC)
    for n in range(8):
        if n == 4:
            pe.wait_ge(s["g_ready"], 1)
            pe.matmul(bank[6][0:S, 64:96], m["tri"], m["g"], start=True, stop=True).then_inc(s["cg_done"], 1)
            pe.wait_ge(s["gt_ready"], 4)
            pe.wait_ge(s["cg_ready"], 1)
            for q in range(4):
                ins = pe.matmul(bank[4 + q][0:S, :], ones[0:S, 0:S], m["gt"][:, 512 * q:512 * q + 512], start=True, stop=True)
            ins.then_inc(s["cgb_done"], 1)
        if n >= 4:
            pe.wait_ge(s["qkv_in"], n - 3)
        for k in range(8):
            ch = 128 * (8 * n + k)
            for c in range(HC):
                ins = pe.matmul(bank[n % 4][:, S * k:S * k + S], w[:, c, ch:ch + 128], h_t[:, S * c:S * c + S],
                                start=(c == 0), stop=(c == HC - 1))
        ins.then_inc(s["qkv_mm"], 1)
    pe.wait_ge(s["wz_in"], 16)
    pe.wait_ge(s["qkv_in"], 8)
    wz = mid[:, :].rearrange("p (h n) -> p h n", h=HC)
    for n in range(4):
        for k in range(8):
            ch = 128 * (8 * n + k)
            for c in range(HC):
                ins = pe.matmul(bank[n][:, S * k:S * k + S], wz[:, c, ch:ch + 128], h_t[:, S * c:S * c + S],
                                start=(c == 0), stop=(c == HC - 1))
        ins.then_inc(s["z_mm"], 1)
    pe.wait_ge(s["gam_diff"], 4)
    def sums_by_pair(sq, ready, done):
        for p in range(16):
            if p % 4 == 0:
                pe.wait_ge(s[ready], p // 4 + 1)
            ins = pe.matmul(bank[4][:, p:p + 1], sq[:, 128 * p:128 * p + 128], ones[:, 0:1], start=True, stop=True)
        ins.then_inc(s[done], 1)

    def spread(diag, ready, done):
        for n in range(4):
            pe.wait_ge(s[ready], n + 1)
            pe.matmul(bank[4 + n], ones[:, :], diag[:, 512 * n:512 * n + 512], start=True, stop=True)\
              .then_inc(s[done], 1)

    sums_by_pair(m["sq"], "sq_ready", "sq_mm")
    spread(m["sq"], "norm_diag", "norm_bc")
    pe.wait_ge(s["z_silu"], 4)
    for n in range(8):
        if n >= 4:
            pe.wait_ge(s["normed_qk"], n - 3)
        for k in range(4):
            ch = S * (32 + 4 * n + k)
            ins = pe.transpose(bank[n][0:S, D * k:D * k + D], m["cv"][:, ch:ch + S], ident[:, :])
        ins.then_inc(s["vT_done"], 1)
    pe.wait_ge(s["normed_qk"], 4)
    pe.wait_ge(s["bv_ready"], 4)
    for k in range(NK):
        q, kk = m["cv"][:, S * k:S * k + S], m["cv"][:, S * (NK + k):S * (NK + k) + S]
        c = slice(S * (k % 8), S * (k % 8) + S)
        pe.matmul(bank[k // 8][0:S, c], kk, kk, start=True, stop=True)
        ins = pe.matmul(bank[2 + k // 8][0:S, c], kk, q, start=True, stop=True)
    ins.then_inc(s["kk_done"], 1)

    def head(name, h):
        return m[name][:, S * h:S * h + S]

    for q in range(4):
        pe.wait_ge(s["lm_ready"], q + 1)
        pe.wait_ge(s["at_ready"], 4)
        for h in range(8 * q, 8 * q + 8):
            ins = pe.transpose(bank[q][0:S, S * (h % 8):S * (h % 8) + S], m["lm"][0][:, S * h:S * h + S], ident[0:S, 0:S])
        ins.then_inc(s["cy_mm"], 1)
    pe.wait_ge(s["bv_ready"], 8)
    for lv in range(1, 6):
        for q in range(4):
            pe.wait_ge(s["lm_ready"], 4 * lv + q + 1)
            pe.wait_ge(s["y_new"], 8 * (lv - 1) + 2 * q + 2)
            for h in range(8 * q, 8 * q + 8):
                ins = pe.matmul(bank[q][0:S, S * (h % 8):S * (h % 8) + S], m["lm"][lv % 2][:, S * h:S * h + S],
                                head("y", h), start=True, stop=True)
            ins.then_inc(s["cy_mm"], 1)
        for q in range(4):
            pe.wait_ge(s["cy_in"], 4 * (lv - 1) + q + 1)
            if q >= 2:
                n = 1 if lv == 5 else 2
                pe.wait_ge(s["y_new"], 8 * lv + n * (q - 1))
            elif lv > 1:
                pe.wait_ge(s["y_new"], 8 * (lv - 1) + 2 * (q + 3))
            for h in range(8 * q, 8 * q + 8):
                c = slice(S * (h % 8), S * (h % 8) + S)
                ins = pe.matmul(bank[4 + 2 * (q % 2)][0:S, c], head("yt", h), head("z", h), start=True, stop=True)
                if lv < 5:
                    ins = pe.matmul(bank[5 + 2 * (q % 2)][0:S, c], head("z", h), head("yt", h), start=True, stop=True)
            ins.then_inc(s["d_mm"], 1)
    for n in range(8):
        pe.wait_ge(s["y_new"], 40 + n // 2 + 1)
        if n >= 4:
            pe.wait_ge(s["y_new"], 44)
        for h in range(4 * n, 4 * n + 4):
            ins = pe.matmul(bank[n][0:S, D * (h % 4):D * (h % 4) + D], head("y", h), m["bv"][:, D * h:D * h + D],
                            start=True, stop=True)
        ins.then_inc(s["u_mm"], 1)
    pe.wait_ge(s["u_in"], 8)
    for n in range(4):
        for h in range(8 * n, 8 * n + 8):
            ins = pe.matmul(bank[n][:, S * (h % 8):S * (h % 8) + S], m["u"][:, D * h:D * h + D], head("a_t", h),
                            start=True, stop=True)
        ins.then_inc(s["o_mm"], 1)
    sums_by_pair(m["o2"], "o_sq", "o_ms")
    spread(m["o2"], "ms_diag", "ms_bc")
    pe.wait_ge(s["wout_in"], 16)
    pe.wait_ge(s["o_ready"], 4)
    for h in range(NV):
        pe.wait_ge(s["yn_ready"], h // 8 + 1)
        ins = pe.matmul(bank[0][0:S, 0:H], m["o"][:, S * h:S * h + S], mid[:, H * h:H * h + H],
                        start=(h == 0), stop=(h == NV - 1))
    ins.then_inc(s["out_mm"], 1)
    pe.wait_ge(s["normed"], 4)
    turn("x3T_done")
    pe.wait_ge(s["x3T_ready"], 1)
    a = SMALL["gate"][0]
    for c in range(HC):
        ins = pe.matmul(bank[6][0:S, 0:EXPERTS], h_t[:, S * c:S * c + S], small[:, a + 8 * c:a + 8 * c + 8],
                        start=(c == 0), stop=(c == HC - 1))
    ins.then_inc(s["logit_done"], 1)
    pe.wait_ge(s["up_in"], 16)
    pe.wait_ge(s["base_in"], 32)

    def up(n):
        e = EXPERT_ORDER[n]
        w = m["base_up"] if e == EXPERTS else wide[:, 2048 * e:2048 * e + 2048]
        if n >= 4:
            pe.wait_ge(s["hid_part"], n - 3)
        for k in range(8):
            for c in range(HC):
                ins = pe.matmul(bank[n % 4][:, S * k:S * k + S], w[:, 1024 * c + 128 * k:1024 * c + 128 * k + 128],
                                h_t[:, S * c:S * c + S], start=(c == 0), stop=(c == HC - 1))
        ins.then_inc(s["up_mm"], 1)

    def down(n):
        e = EXPERT_ORDER[n]
        w = m["base_down"] if e == EXPERTS else m["down"][:, 1024 * e:1024 * e + 1024]
        if e == EXPERTS:
            pe.wait_ge(s["hid_part"], 1)
        else:
            pe.wait_ge(s["hid_ready"], n)
        for k in range(4):
            ins = pe.matmul(bank[4][0:S, 0:H], m["hx"][:, 256 * n + S * k:256 * n + S * k + S], w[:, H * k:H * k + H],
                            start=(n == 0 and k == 0), stop=(n == 8 and k == 3))
        return ins

    for n in range(4):
        up(n)
    pe.wait_ge(s["comb_ready"], 1)
    pe.matmul(bank[5], ones[0:S, :], m["comb_d"], start=True, stop=True).then_inc(s["combb_done"], 1)
    for n in range(4, 9):
        up(n)
    down(0)
    pe.wait_ge(s["down_in"], 16)
    for n in range(1, 9):
        ins = down(n)
    ins.then_inc(s["down_mm"], 1)


def layout(i):
    f = lambda n: np.asarray(i[n])
    c = np.ascontiguousarray

    def by_width(w):
        return c(w.reshape(w.shape[0], HC, 128).transpose(2, 1, 0))

    def row(v):
        return np.broadcast_to(v.reshape(1, -1), (128, v.size))

    halves = lambda v: v.reshape(HC, 128).T
    a = "L0_xattn_"
    col = {"ln_w": halves(f(a + "ln_w")), "ln_b": halves(f(a + "ln_b")),
           "qx_in": halves(f(a + "qx_in_scale")), "q_in": halves(f(a + "q_in_scale")),
           "k_in": halves(f(a + "k_in_scale")), "v_in": halves(f(a + "v_in_scale")),
           "smooth": f(a + "proj_smooth").reshape(32, 128).T, "norm_w": f("L0_attn_norm_w").reshape(128, 1),
           "wqx_s": row(f(a + "wqx_scale")), "wq_s": row(f(a + "wq_scale")), "wk_s": row(f(a + "wk_scale")),
           "wv_s": row(f(a + "wv_scale")), "pw_s": row(f(a + "proj_w_scale")), "pin_s": row(f(a + "proj_in_scale")),
           "conv": f("L0_attn_conv_w").reshape(64, 128, 4).transpose(1, 0, 2).reshape(128, 256),
           "dt_bias": row(f("L0_attn_dt_bias")), "A_log": row(f("L0_attn_A_log")),
           "W_ba": by_width(np.concatenate([f("L0_attn_W_b"), f("L0_attn_W_a")])).reshape(128, 128),
           "gate": f("L0_ffn_gate_w").reshape(HC, 128, EXPERTS).transpose(1, 0, 2).reshape(128, 16)}
    for n in ("qxln", "qln", "kln", "kxln"):
        for e in "wb":
            col[f"{n}_{e}"] = f(f"{a}{n}_{e}").reshape(128, 1)
    ctx = f("ctx_2048").reshape(SC // 128, 128, H)
    kv = f(a + "w_kv_x")
    return {
        "x": c(f("x").reshape(S, H)),
        "small": c(np.concatenate([col[n] for n in SMALL], axis=1)),
        "wqx": by_width(f(a + "wqx")), "wq": by_width(f(a + "wq")), "wk": by_width(f(a + "wk")), "wv": by_width(f(a + "wv")),
        "kxT": by_width(kv[:1024]), "wvxT": by_width(kv[1024:]),
        "kxd": c(kv[:1024].reshape(G, D, H).transpose(1, 0, 2)),
        "ctT": c(ctx.reshape(SC // 128, 128, HC, 128).transpose(0, 3, 2, 1).reshape(SC // 128, 128, H)), "cn": c(ctx),
        "wprojT": c(f(a + "wproj").reshape(H, 32, 128).transpose(2, 1, 0).reshape(128, 8192)),
        "W_qkv": by_width(f("L0_attn_W_qkv")).reshape(128, 16384),
        "W_z": by_width(f("L0_attn_W_z")).reshape(128, 8192),
        "W_out": c(f("L0_attn_W_out").reshape(H, 32, 128).transpose(2, 1, 0).reshape(128, 8192)),
        "up": c(f("L0_ffn_expert_gate_up").reshape(EXPERTS, HC, 128, 1024).transpose(2, 0, 1, 3).reshape(128, 16384)),
        "down": c(f("L0_ffn_expert_down").reshape(EXPERTS, 4, 128, H).transpose(2, 0, 1, 3).reshape(128, 8192)),
        "base_up": c(f("L0_ffn_base_gate_up").reshape(HC, 128, 1024).transpose(1, 0, 2).reshape(128, 2048)),
        "base_down": c(f("L0_ffn_base_down").reshape(4, 128, H).transpose(1, 0, 2).reshape(128, 1024)),
    }


def kernel(**inputs):
    import concourse.bacc as bacc
    from concourse.bass_utils import run_bass_kernel_spmd

    nc = bacc.Bacc("TRN2", target_bir_lowering=False, num_devices=1)
    arrays = layout(inputs)
    t = {n: nc.dram_tensor("in_" + n, a.shape, F32, kind="ExternalInput").ap() for n, a in arrays.items()}
    t["out"] = nc.dram_tensor("out", (S, H), F32, kind="ExternalOutput").ap()
    build(nc, t)
    r = run_bass_kernel_spmd(nc, [{"in_" + n: a for n, a in arrays.items()}], core_ids=[0])
    return r.results[0]["out"].reshape(1, S, H)
```

```python
from contextlib import ExitStack

import numpy as np
import concourse.bass as bass
from concourse import mybir

ALU = mybir.AluOpType
ACT = mybir.ActivationFunctionType
F32 = mybir.dt.float32
F32R = mybir.dt.float32r
BF16 = mybir.dt.bfloat16
U16 = mybir.dt.uint16
I32 = mybir.dt.int32
X = mybir.AxisListType.X

S = 64
H = 256
HC = H // 128
D = 128
G = 8
NH = 16
ROWS = (NH // G) * S
GR = G * ROWS
SC = 6272
CH = 7
NCH = SC // 128 // CH
BUF = [0, 1, 0, 1, 0, 1, 2]
USES = [3, 3, 1]
NV = 32
NK = 16
EXPERTS = 8
INNER = 512
EPS = 1e-5
FP8_MAX = 448.0


def prev_use(i):
    return {0: 3, 1: 3, 6: 7}.get(i, 2)


def buf_use(j, i):
    return j * USES[BUF[i]] + BUF[:i].count(BUF[i])


class Tally:

    def __init__(self, sem):
        self.sem, self.n = sem, 0

    def by(self, ins):
        ins.then_inc(self.sem, 1)
        self.n += 1
        return self.n

    def settle(self, eng, ins):
        self.by(ins)
        eng.wait_ge(self.sem, self.n)


SMALL = {}
_at = 0
for _name, _n in (("ln_w", 2), ("ln_b", 2), ("qx_in", 2), ("q_in", 2), ("k_in", 2), ("v_in", 2),
                  ("qxln_w", 1), ("qxln_b", 1), ("qln_w", 1), ("qln_b", 1), ("kln_w", 1), ("kln_b", 1),
                  ("kxln_w", 1), ("kxln_b", 1), ("smooth", 32), ("norm_w", 1), ("wqx_s", 1), ("wq_s", 1),
                  ("wk_s", 1), ("wv_s", 1), ("pw_s", 1), ("pin_s", 1), ("conv", 256), ("dt_bias", 16),
                  ("A_log", 16), ("W_ba", 128), ("gate", 16)):
    SMALL[_name] = (_at, _n)
    _at += _n
NSMALL = _at


def build(nc, t):
    t = dict(t)
    t["l_blocks"] = nc.dram_tensor("l_blocks", (128, 1024), F32, kind="Internal").ap()
    t["inverses"] = nc.dram_tensor("inverses", (2, 128, BLK * BLK), F32, kind="Internal").ap()
    ctx = ExitStack()
    phase1 = ExitStack()
    loop_only = ExitStack()
    split_weights = ExitStack()

    def sb(name, shape, dt=F32, at=ctx):
        return at.enter_context(nc.sbuf_tensor(name, shape, dt))

    def sem(name):
        return ctx.enter_context(nc.semaphore(name))

    with ctx:
        wide = sb("wide", [128, 16384])
        k_hi = sb("k_hi", [128, HC, 1024], F32R, split_weights)
        k_lo = sb("k_lo", [128, HC, 1024], F32R, split_weights)
        q_hi = sb("q_hi", [128, HC, 1024], F32R, split_weights)
        q_lo = sb("q_lo", [128, HC, 1024], F32R, split_weights)
        split_weights.close()
        mid = sb("mid", [128, 8192])
        ident = sb("ident", [128, 128])
        ones = sb("ones", [128, 128])
        fold = sb("fold", [128, S])
        small = sb("small", [128, NSMALL])
        x_res = sb("x_res", [S, H])
        stat = sb("stat", [128, 64])
        rstd1 = sb("rstd1", [128, 8])
        smooth_inv = sb("smooth_inv", [128, 32])
        cst = sb("cst", [128, 8])

        eps8 = sb("eps8", [128, 8])

        scores = sb("scores", [128, CH, GR], F32, phase1)
        neg_max = sb("neg_max", [128, GR], F32, phase1)
        alpha = sb("alpha", [128, GR], F32, phase1)
        run_max = sb("run_max", [128, GR], F32, phase1)
        c_col = sb("c_col", [128, G], F32, phase1)
        mx = sb("mx", [128, G], F32, phase1)
        p_sum = sb("p_sum", [128, GR], F32, phase1)
        o_acc = sb("o_acc", [128, HC, GR], F32, phase1)
        p_hi = sb("p_hi", [128, 2, 512], F32R, phase1)
        p_lo = sb("p_lo", [128, 2, 512], F32R, phase1)
        ct_raw = sb("ct_raw", [128, 3, 256], F32, phase1)
        ct_hi = sb("ct_hi", [128, 3, 256], F32R, phase1)
        ct_lo = sb("ct_lo", [128, 3, 256], F32R, phase1)
        cn_raw = sb("cn_raw", [128, 3, 256], F32, phase1)
        cn_hi = sb("cn_hi", [128, 3, 256], F32R, phase1)
        cn_lo = sb("cn_lo", [128, 3, 256], F32R, phase1)
        ss = sb("ss", [128, 8], F32, phase1)
        cat_t = sb("cat_t", [128, 2048], F32, phase1)
        p_f = sb("p_f", [128, 2, 512], F32, loop_only)
        ksq = sb("ksq", [128, 2, 512], F32, loop_only)
        loop_only.close()
        p_lo2 = sb("p_lo2", [128, 2, 512], F32R, phase1)
        p_hi2 = sb("p_hi2", [128, 2, 512], F32R, phase1)
        last_hi = [p_hi, p_hi2]
        last_lo = [p_lo, p_lo2]
        half = o_acc[:, 0, 0:H]
        cn_buf = [(cn_raw[:, b, :], cn_hi[:, b, :], cn_lo[:, b, :]) for b in range(3)]
        ct_buf = [(ct_raw[:, b, :], ct_hi[:, b, :], ct_lo[:, b, :]) for b in range(3)]
        wv_x = scores[:, 0:2, :]
        phase1.close()
        ph2 = {}
        second_memory(ph2, sb)
        ph2["stat"] = stat
        ph2["fold"] = fold

        pk = ctx.enter_context(nc.psum_tensor("pk", [128, 2, 512], F32))
        ps = ctx.enter_context(nc.psum_tensor("ps", [128, 2, 512], F32))
        po = ctx.enter_context(nc.psum_tensor("po", [128, 4, 512], F32))
        bank = [po[:, 0, :], po[:, 1, :], po[:, 2, :], po[:, 3, :], pk[:, 0, :], pk[:, 1, :], ps[:, 0, :], ps[:, 1, :]]

        def sm(name, rows=128, k=None):
            a, n = SMALL[name]
            return small[0:rows, a:a + n] if k is None else small[0:rows, a + k:a + k + 1]

        names = """x_in small_in w_qx w_q w_k w_v kxT_in kxd_in const_ready pow_ask pow_done dve_step pool_step xT_done
            xq_ready lin_done lin_evac heads_ready headT_done qkT_ready qmean_done qc_ready cbc_done qk_done
            q_split k_split s_self p_self pT_self pT_evac core_done cat_core ct_split cn_split ksq_mm ksq_act
            ssum rstd_ready s_mm evac_v evac_a max_done rt_done mx_ready mb_done c_ready mx_raw mx_full
            alpha_diff max_ready alpha_ready p_shift p_exp p_hi_ready p_lo_ready pv_rh psum_add merged
            psum_scaled wv_in den_done den_in den_spread xo_done wproj_in catq_ready proj_done x1_ready stored""".split()
        s = {n: sem(n) for n in names}
        ct_in = [sem(f"ct_in{b}") for b in range(3)]
        cn_in = [sem(f"cn_in{b}") for b in range(3)]
        s.update({n: sem(n) for n in SECOND})
        last_tiles = [(cn_buf[0], cn_in[0], 16 * (USES[0] * (NCH - 1) + 1)), (cn_buf[1], cn_in[1], 16 * (USES[1] * (NCH - 1) + 1)),
                      (ct_buf[0], ct_in[0], 16 * (USES[0] * NCH + 1)), (ct_buf[1], ct_in[1], 16 * (USES[1] * NCH + 1)),
                      (ct_buf[2], ct_in[2], 16 * (USES[2] * NCH + 1)), (cn_buf[2], cn_in[2], 16 * (USES[2] * (NCH - 1) + 1)),
                      (cn_buf[0], cn_in[0], 16 * (USES[0] * (NCH - 1) + 2))]

        wqx = wide[:, 0:4096].rearrange("p (h n) -> p h n", h=HC)
        wq = wide[:, 4096:8192].rearrange("p (h n) -> p h n", h=HC)
        wk = wide[:, 8192:10240].rearrange("p (h n) -> p h n", h=HC)
        wv = wide[:, 10240:12288].rearrange("p (h n) -> p h n", h=HC)
        kxT = wide[:, 12288:14336].rearrange("p (h n) -> p h n", h=HC)
        kxd = wide[:, 14336:16384].rearrange("p (g n) -> p g n", g=G)
        heads = scores[0:S, 0:5, :].rearrange("p a b -> p (a b)")
        vrow = scores[0:S, 5, :]
        hst = scores[0:S, 6, 0:240]
        hm = scores[0:S, 6, 256:296]
        hv = scores[0:S, 6, 296:336]
        ht = scores[0:S, 6, 336:376]
        hr = scores[0:S, 6, 376:416]
        xn = scores[0:S, 6, 512:768]
        qxT = o_acc[:, 0, :]
        qkw = o_acc[:, 1, :]
        qT = p_sum[:, :]
        kT = p_f[:, 0, :]
        pself = p_f[:, 1, :]
        pTs = run_max[0:S, :]
        xT = ct_raw[:, 0, 0:128]
        xy = ct_raw[:, 1, 0:128]
        xm = ct_raw[:, 2, 0:128]
        xb16 = cn_raw[:, 0, 0:64].bitcast(BF16)
        xe16 = cn_raw[:, 0, 64:128].bitcast(BF16)
        xq = [cn_raw[:, 1, 0:128], cn_raw[:, 1, 128:256], cn_raw[:, 2, 0:128], cn_raw[:, 2, 128:256]]
        mean_w = ct_raw[:, 1, 128:256]

        block = ctx.enter_context(nc.Block())

        @block.sync
        def _(sp):
            sp.dma_start(x_res[:, :], t["x"]).then_inc(s["x_in"], 16)
            sp.dma_start(small[:, :], t["small"]).then_inc(s["small_in"], 16)
            sp.dma_start(wqx, t["wqx"]).then_inc(s["w_qx"], 16)
            sp.dma_start(wq, t["wq"]).then_inc(s["w_q"], 16)
            sp.dma_start(wk, t["wk"]).then_inc(s["w_k"], 16)
            sp.dma_start(kxd, t["kxd"]).then_inc(s["kxd_in"], 16)
            sp.dma_start(kxT, t["kxT"]).then_inc(s["kxT_in"], 16)
            sp.dma_start(wv, t["wv"]).then_inc(s["w_v"], 16)

            def load_t(j, i):
                if isinstance(j, int) and j == 0:
                    if i in (0, 1, 6):
                        pass
                    else:
                        sp.wait_ge(s["ct_split"], i - 1)
                else:
                    sp.wait_ge(s["ct_split"], j * CH + i - prev_use(i) + 1)
                sp.dma_start(ct_raw[:, BUF[i], :], t["ctT"][j * CH + i]).then_inc(ct_in[BUF[i]], 16)

            def load_n(j, i):
                if isinstance(j, int) and j == 0:
                    if i not in (0, 1, 6):
                        sp.wait_ge(s["cn_split"], i - 1)
                else:
                    sp.wait_ge(s["cn_split"], j * CH + i - prev_use(i) + 1)
                sp.dma_start(cn_raw[:, BUF[i], :], t["cn"][j * CH + i]).then_inc(cn_in[BUF[i]], 16)

            sp.wait_ge(s["core_done"], 1)
            sp.wait_ge(s["lin_done"], 12)
            for i in range(CH):
                load_t(0, i)
            sp.wait_ge(s["q_split"], 1)
            sp.dma_start(wide[:, :], t["W_qkv"], max_dma_last_dim=8192).then_inc(s["wqkv_in"], 16)
            with sp.Fori(1, 2) as j:
                for i in range(CH):
                    load_t(j, i)
                    load_n(0, i)
            with sp.Fori(2, NCH) as j:
                for i in range(CH):
                    load_t(j, i)
                    load_n(j - 1, i)
            for i, ((raw, _, _), landed, _) in enumerate(last_tiles):
                if i in (2, 3, 4):
                    sp.wait_ge(s["ct_split"], CH * NCH)
                elif i == 6:
                    sp.wait_ge(s["cn_split"], CH * (NCH - 1) + 1)
                else:
                    sp.wait_ge(s["cn_split"], CH * (NCH - 1) + (-2, -1, 0, 0, 0, 0)[i])
                sp.dma_start(raw, t["cn"][CH * (NCH - 1) + i]).then_inc(landed, 16)
            sp.wait_ge(s["s_mm"], 2 * CH * NCH)
            sp.dma_start(mid[:, :], t["wprojT"], max_dma_last_dim=8192).then_inc(s["wproj_in"], 16)
            sp.wait_ge(s["psum_add"], 2 * (CH * (NCH - 1) + 2))
            sp.wait_ge(s["p_lo_ready"], 2 * (CH * (NCH - 1) + 2))
            sp.dma_start(wv_x, t["wvxT"]).then_inc(s["wv_in"], 16)
            second_loads(sp, s, t, ph2, wide, mid)
            sp.wait_ge(s["out_ready"], 1)
            sp.dma_start(t["out"], x_res[:, :]).then_inc(s["stored"], 16)
            sp.wait_ge(s["stored"], 16)

        @block.gpsimd
        def _(pool):
            step = Tally(s["pool_step"])
            asked = Tally(s["pow_ask"])

            def inv_root(out, in_, rows, width):
                asked.n += 1
                pool.wait_ge(s["pow_ask"], asked.n)
                pool.tensor_tensor(out, in_, cst[0:rows, 0:1].broadcast_to([rows, width]) if width > 1
                                   else cst[0:rows, 0:1], ALU.pow).then_inc(s["pow_done"], 1)

            pool.memset(cst[:, :], -0.5).then_inc(s["pool_step"], 1)
            pool.memset(eps8[:, :], 128.0 * EPS)
            pool.memset(ones[:, :], 1.0).then_inc(s["pool_step"], 1)
            pool.memset(ident[:, :], 0.0).then_inc(s["pool_step"], 1)
            pool.wait_ge(s["pool_step"], 3)
            pool.affine_select(out=ident[:, :], in_=ident[:, :], compare_op=ALU.not_equal, fill=1.0, base=0,
                               pattern=[[-1, 128]], channel_multiplier=1).then_inc(s["const_ready"], 1)
            inv_root(stat[0:S, 8:9], stat[0:S, 7:8], S, 1)
            inv_root(stat[0:S, 8:9], stat[0:S, 7:8], S, 1)
            inv_root(hr, hv, S, 40)

            def root(j, i):
                pool.wait_ge(s["ssum"], 2 * (j * CH + i + 1))
                if not (isinstance(j, int) and j == 0 and i == 0):
                    pool.wait_ge(s["evac_v"], j * CH + i)
                    pool.wait_ge(s["evac_a"], j * CH + i)
                pool.tensor_tensor(ss[:, :], ss[:, :], eps8[:, :], ALU.add).then_inc(s["ss_eps"], 1)
                pool.wait_ge(s["ss_eps"], j * CH + i + 1)
                pool.tensor_tensor(rstd1[:, :], ss[:, :], cst[:, :], ALU.pow).then_inc(s["rstd_ready"], 1)

            def shift(j, i):
                if i == 0:
                    pool.wait_ge(s["max_ready"], j + 1)
                for h in range(2):
                    if not (isinstance(j, int) and j == 0 and i == 0):
                        pool.wait_ge(s["psum_add"], 2 * (j * CH + i) + h - 1)
                        pool.wait_ge(s["p_lo_ready"], 2 * (j * CH + i) + h - 1)
                    pool.tensor_tensor(p_f[:, h, :], scores[:, i, 512 * h:512 * h + 512],
                                       neg_max[:, 512 * h:512 * h + 512], ALU.add).then_inc(s["p_shift"], 1)

            def add_p(j, i, h, probs):
                pool.wait_ge(s["p_exp"], 2 * (j * CH + i) + h + 1)
                if i == 0:
                    pool.wait_ge(s["psum_scaled"], j + 1)
                else:
                    pool.wait_ge(s["psum_add"], 2 * (j * CH + i) - 1 + h)
                cols = p_sum[:, 512 * h:512 * h + 512]
                pool.tensor_tensor(cols, cols, probs, ALU.add).then_inc(s["psum_add"], 1)

            for i in range(CH):
                root(0, i)

            def pool_chunk(j, k):
                for i in range(CH):
                    shift(k, i)
                    if i == 0:
                        root(j, i)
                        add_p(k, i, 0, p_f[:, 0, :])
                    else:
                        add_p(k, i, 0, p_f[:, 0, :])
                        root(j, i)
                    add_p(k, i, 1, p_f[:, 1, :])

            pool_chunk(1, 0)
            with pool.Fori(2, NCH) as j:
                pool_chunk(j, j - 1)
            for i in range(CH):
                for h in range(2):
                    add_p(NCH - 1, i, h, scores[:, i, 512 * h:512 * h + 512])
            second_pool(pool, s, ph2, inv_root, ident, cst, small)

        @block.scalar
        def _(act):
            ends = [("wqx_s", 4), ("wq_s", 4), ("wk_s", 2), ("wv_s", 2)]
            act.wait_ge(s["small_in"], 16)
            n = 0
            for name, count in ends:
                for _ in range(count):
                    act.wait_ge(s["lin_done"], n + 1)
                    dst = heads[:, 512 * n:512 * n + 512] if n < 10 else vrow[:, 512 * (n - 10):512 * (n - 9)]
                    act.activation(dst, bank[n % 8][0:S, :], ACT.Identity, scale=sm(name, S)).then_inc(s["lin_evac"], 1)
                    n += 1
            act.wait_ge(s["s_self"], 2)
            act.activation(pself, pself, ACT.Exp, scale=float(D) ** -0.5).then_inc(s["p_self"], 1)

            def high(j, i, half, raw, hi, landed, used):
                b = BUF[i]
                act.wait_ge(landed[b], 16 * (buf_use(j, i) + 1))
                if not (isinstance(j, int) and j == 0 and i in (0, 1, 6)):
                    act.wait_ge(used, 2 * (j * CH + i - prev_use(i) + 1))
                act.activation(hi[:, b, :], raw[:, b, :], ACT.Identity).then_inc(half, 1)

            def high_t(j, i):
                high(j, i, s["ct_half"], ct_raw, ct_hi, ct_in, s["s_mm"])

            def high_n(j, i):
                high(j, i, s["cn_half"], cn_raw, cn_hi, cn_in, s["pv_rh"])

            def square(j, i):
                for n in range(2):
                    act.wait_ge(s["ksq_mm"], 2 * (j * CH + i) + n + 1)
                    if not (isinstance(j, int) and j == 0 and i == 0):
                        act.wait_ge(s["ssum"], 2 * (j * CH + i) + n - 1)
                    act.activation(ksq[:, n, :], pk[:, n, :], ACT.Square).then_inc(s["ksq_act"], 1)

            def probs(j, i, h, p, hi, used):
                act.wait_ge(s["p_shift"], 2 * (j * CH + i) + h + 1)
                act.activation(p, p, ACT.Exp).then_inc(s["p_exp"], 1)
                act.wait_ge(s["p_exp"], 2 * (j * CH + i) + h + 1)
                if used is not None:
                    act.wait_ge(s["pv_rh"], used)
                act.copy(hi, p).then_inc(s["p_hi_ready"], 1)

            def evacuate(j, i):
                act.wait_ge(s["rstd_ready"], j * CH + i + 1)
                if not (isinstance(j, int) and j == 0):
                    act.wait_ge(s["p_shift"], 2 * (j * CH + i + 1 - CH))
                act.wait_ge(s["s_mm"], 2 * (j * CH + i) + 2)
                for g in range(4, G):
                    ins = act.activation(scores[:, i, ROWS * g:ROWS * g + ROWS], ps[:, 1, ROWS * (g - 4):ROWS * (g - 3)],
                                         ACT.Identity, scale=rstd1[:, g:g + 1])
                ins.then_inc(s["evac_a"], 1)

            def rescale(j):
                act.wait_ge(s["alpha_diff"], j + 1)
                act.activation(alpha[:, :], alpha[:, :], ACT.Exp).then_inc(s["alpha_ready"], 1)

            high_t(0, 0)
            for i in range(CH):
                square(0, i)
                high_t((i + 1) // CH, (i + 1) % CH)
                evacuate(0, i)
            rescale(0)

            def act_chunk(j, k, last=False):
                for i in range(CH):
                    high_n(k, i)
                    first = isinstance(k, int) and k == 0 and i == 0
                    probs(k, i, 0, p_f[:, 0, :], p_hi[:, 0, :], None if first else 2 * (k * CH + i) - 1)
                    square(j, i)
                    probs(k, i, 1, p_f[:, 1, :], p_hi[:, 1, :], None if first else 2 * (k * CH + i))
                    if i < CH - 1:
                        high_t(j, i + 1)
                    elif not last:
                        high_t(j + 1, 0)
                    evacuate(j, i)
                rescale(j)

            act_chunk(1, 0)
            with act.Fori(2, NCH - 1) as j:
                act_chunk(j, j - 1)
            act_chunk(NCH - 1, NCH - 2, last=True)
            for i, ((raw, hi, _), landed, count) in enumerate(last_tiles):
                act.wait_ge(landed, count)
                if i in (2, 3, 4):
                    act.wait_ge(s["s_mm"], 2 * CH * NCH)
                else:
                    act.wait_ge(s["pv_rh"], 2 * (CH * (NCH - 1) + (-2, -1, 0, 0, 0, 0, 1)[i]))
                act.activation(hi, raw, ACT.Identity).then_inc(s["cn_half"], 1)
                for h in range(2):
                    n = 2 * (CH * (NCH - 1) + i) + h
                    probs(NCH - 1, i, h, scores[:, i, 512 * h:512 * h + 512], last_hi[i % 2][:, h, :],
                          (n - 1, None)[i] if i < 2 else n - 3)
            second_scalar(act, s, ph2, bank, small)

        @block.vector
        def _(dve):
            v = Tally(s["dve_step"])
            asked = Tally(s["pow_ask"])
            normed = Tally(s["normed"])

            def ask_root(ins):
                asked.by(ins)
                dve.wait_ge(s["pow_done"], asked.n)

            def layernorm_rows(dst, src):
                v.settle(dve, dve.bn_stats(stat[0:S, 0:6], src))
                v.settle(dve, dve.bn_aggr(stat[0:S, 6:8], stat[0:S, 0:6]))
                ask_root(dve.tensor_scalar(stat[0:S, 7:8], stat[0:S, 7:8], EPS, None, ALU.add))
                dve.tensor_scalar(dst, src, stat[0:S, 6:7], stat[0:S, 8:9], ALU.subtract, ALU.mult)\
                   .then_inc(s["normed"], 1)
                normed.n += 1
                dve.wait_ge(s["normed"], normed.n)

            def fp8_round(out, y, b16, e16, mag, ready=None):
                v.settle(dve, dve.tensor_scalar(b16, y, FP8_MAX, -FP8_MAX, ALU.min, ALU.max))
                v.settle(dve, dve.tensor_scalar(e16.bitcast(U16), b16.bitcast(U16), 0x7F80, None, ALU.bitwise_and))
                v.settle(dve, dve.tensor_scalar(mag, e16, 2.0 ** -6, 1.5 * 2.0 ** 20, ALU.max, ALU.mult))
                v.settle(dve, dve.tensor_tensor(out, b16, mag, ALU.add))
                ins = dve.tensor_tensor(out, out, mag, ALU.subtract)
                if ready is None:
                    v.settle(dve, ins)
                else:
                    ins.then_inc(ready, 1)

            dve.wait_ge(s["x_in"], 16)
            dve.wait_ge(s["const_ready"], 1)
            layernorm_rows(xn, x_res[:, :])
            layernorm_rows(xn, xn)
            dve.wait_ge(s["small_in"], 16)
            dve.wait_ge(s["xT_done"], 1)
            xT2 = xT.rearrange("p (h t) -> p h t", h=HC)
            for c in range(HC):
                v.settle(dve, dve.tensor_scalar(xT2[:, c, :], bank[0][:, c * S:c * S + S], sm("ln_w", k=c),
                                                sm("ln_b", k=c), ALU.mult, ALU.add))
            inv_in = stat[:, 16:24]
            a = SMALL["qx_in"][0]
            v.settle(dve, dve.reciprocal(inv_in, small[:, a:a + 8]))
            for n in range(4):
                for c in range(HC):
                    v.settle(dve, dve.tensor_scalar(xy[:, c * S:c * S + S], xT2[:, c, :],
                                                    inv_in[:, 2 * n + c:2 * n + c + 1], None, ALU.mult))
                fp8_round(xq[n], xy, xb16, xe16, xm)
                for c in range(HC):
                    col = xq[n][:, c * S:c * S + S]
                    dve.tensor_scalar(col, col, small[:, a + 2 * n + c:a + 2 * n + c + 1], None, ALU.mult)\
                       .then_inc(s["xq_ready"], 1)
            dve.wait_ge(s["kxT_in"], 16)
            km = stat[:, 24:40]
            kx4 = kxT.rearrange("p h (g d) -> p (h g) d", g=G)
            v.settle(dve, dve.tensor_reduce(km, kx4, X, ALU.add))
            v.settle(dve, dve.tensor_scalar(km, km, 1.0 / D, None, ALU.mult))
            v.settle(dve, dve.tensor_tensor(kx4, kx4, km.unsqueeze(2).broadcast_to([128, 16, D]), ALU.subtract))
            v.settle(dve, dve.tensor_copy(k_hi[:, :, :], kxT))
            dve.tensor_tensor(k_lo[:, :, :], kxT, k_hi[:, :, :].bitcast(F32), ALU.subtract).then_inc(s["k_split"], 1)

            dve.wait_ge(s["lin_evac"], 10)
            for h in range(40):
                v.by(dve.bn_stats(hst[:, 6 * h:6 * h + 6], heads[:, D * h:D * h + D]))
            dve.wait_ge(s["dve_step"], v.n)
            st = hst.rearrange("p (h k) -> p h k", k=6)
            v.by(dve.tensor_tensor(hm, st[:, :, 1], st[:, :, 4], ALU.add))
            v.by(dve.tensor_tensor(ht, st[:, :, 1], st[:, :, 4], ALU.subtract))
            v.settle(dve, dve.tensor_tensor(hv, st[:, :, 2], st[:, :, 5], ALU.add))
            v.by(dve.tensor_scalar(hm, hm, 0.5, None, ALU.mult))
            v.by(dve.tensor_scalar(hv, hv, 1.0 / D, EPS, ALU.mult, ALU.add))
            v.settle(dve, dve.scalar_tensor_tensor(ht, ht, 0.25, ht, ALU.mult, ALU.mult))
            ask_root(dve.tensor_tensor(hv, hv, ht, ALU.add))
            for h in range(40):
                hh = heads[:, D * h:D * h + D]
                dve.tensor_scalar(hh, hh, hm[:, h:h + 1], hr[:, h:h + 1], ALU.subtract, ALU.mult)\
                   .then_inc(s["heads_ready"], 1)
            dve.wait_ge(s["headT_done"], 1)
            for n in range(2):
                v.by(dve.tensor_scalar(qxT[:, 512 * n:512 * n + 512], bank[n], sm("qxln_w"), sm("qxln_b"), ALU.mult, ALU.add))
            dve.wait_ge(s["headT_done"], 2)
            for n in range(2):
                v.by(dve.tensor_scalar(qT[:, 512 * n:512 * n + 512], bank[2 + n], sm("qln_w"), sm("qln_b"), ALU.mult, ALU.add))
            dve.wait_ge(s["headT_done"], 3)
            v.settle(dve, dve.tensor_scalar(kT, bank[4], sm("kln_w"), sm("kln_b"), ALU.mult, ALU.add))
            v.by(dve.tensor_scalar(mean_w, ones[:, :], 1.0 / D, None, ALU.mult))
            dve.tensor_scalar(qkw, qxT, sm("kxln_w"), None, ALU.mult).then_inc(s["qkT_ready"], 1)
            dve.wait_ge(s["qkT_ready"], 1)
            dve.wait_ge(s["qmean_done"], 1)
            for n in range(2):
                dve.tensor_tensor(qkw[:, 512 * n:512 * n + 512], qkw[:, 512 * n:512 * n + 512], bank[5 + n],
                                  ALU.subtract).then_inc(s["qc_ready"], 1)
            dve.wait_ge(s["s_self"], 1)
            sg = bank[7].rearrange("p (g t) -> p g t", g=G)
            v.settle(dve, dve.tensor_reduce(stat[:, 40:48], sg, X, ALU.max))
            pg = pself.rearrange("p (g t) -> p g t", g=G)
            dve.tensor_tensor(pg, sg, stat[:, 40:48].unsqueeze(2).broadcast_to([128, G, S]), ALU.subtract)\
               .then_inc(s["s_self"], 1)
            dve.wait_ge(s["cbc_done"], 1)
            dve.tensor_scalar(c_col[:, :], bank[0][:, 0:G], float(D) ** -0.5, None, ALU.mult).then_inc(s["c_ready"], 1)
            dve.wait_ge(s["p_self"], 1)
            v.settle(dve, dve.tensor_reduce(stat[:, 48:56], pg, X, ALU.add))
            v.settle(dve, dve.reciprocal(stat[:, 48:56], stat[:, 48:56]))
            dve.tensor_tensor(pg, pg, stat[:, 48:56].unsqueeze(2).broadcast_to([128, G, S]), ALU.mult)\
               .then_inc(s["p_self"], 1)
            dve.wait_ge(s["qk_done"], 1)
            qp = po.rearrange("p (c b) n -> p c (b n)", c=HC)
            v.settle(dve, dve.tensor_copy(q_hi[:, :, :], qp))
            dve.tensor_tensor(q_lo[:, :, :], qp, q_hi[:, :, :].bitcast(F32), ALU.subtract).then_inc(s["q_split"], 1)
            dve.wait_ge(s["pT_self"], 1)
            dve.tensor_copy(pTs.rearrange("p (b n) -> p b n", b=2), pk[0:S, :, :]).then_inc(s["pT_evac"], 1)
            dve.wait_ge(s["core_done"], 1)
            dve.tensor_copy(cat_t[:, 0:1024].rearrange("p (b n) -> p b n", b=2), ps[:, :, :]).then_inc(s["cat_core"], 1)
            v.by(dve.reciprocal(smooth_inv[:, :], sm("smooth")))
            v.by(dve.tensor_tensor(fold[:, :], ident[:, 0:S], ident[:, S:2 * S], ALU.add))
            dve.wait_ge(s["cat_core"], 1)
            v.by(dve.memset(neg_max[:, :], 1e30))
            v.by(dve.memset(o_acc[:, :, :], 0.0))
            v.settle(dve, dve.memset(p_sum[:, :], 0.0))
            dve.wait_ge(s["lin_done"], 12)

            def low_t(j, i):
                b = BUF[i]
                dve.wait_ge(s["ct_half"], j * CH + i + 1)
                dve.tensor_tensor(ct_lo[:, b, :], ct_raw[:, b, :], ct_hi[:, b, :].bitcast(F32),
                                  ALU.subtract).then_inc(s["ct_split"], 1)

            def low_n(j, i):
                b = BUF[i]
                dve.wait_ge(s["cn_half"], j * CH + i + 1)
                dve.tensor_tensor(cn_lo[:, b, :], cn_raw[:, b, :], cn_hi[:, b, :].bitcast(F32),
                                  ALU.subtract).then_inc(s["cn_split"], 1)

            def low_p(j, i, h, probs, hi=p_hi, lo=p_lo):
                dve.wait_ge(s["p_hi_ready"], 2 * (j * CH + i) + h + 1)
                dve.tensor_tensor(lo[:, h, :], probs, hi[:, h, :].bitcast(F32),
                                  ALU.subtract).then_inc(s["p_lo_ready"], 1)

            def sums(j, i):
                for n in range(2):
                    dve.wait_ge(s["ksq_act"], 2 * (j * CH + i) + n + 1)
                    if not (isinstance(j, int) and j == 0 and i == 0):
                        dve.wait_ge(s["rstd_ready"], j * CH + i)
                    dve.tensor_reduce(ss[:, 4 * n:4 * n + 4], ksq[:, n, :].rearrange("p (g d) -> p g d", g=4),
                                      X, ALU.add).then_inc(s["ssum"], 1)

            def evacuate(j, i):
                dve.wait_ge(s["rstd_ready"], j * CH + i + 1)
                if not (isinstance(j, int) and j == 0):
                    dve.wait_ge(s["p_shift"], 2 * (j * CH + i + 1 - CH))
                dve.wait_ge(s["s_mm"], 2 * (j * CH + i) + 1)
                for g in range(4):
                    ins = dve.tensor_scalar(scores[:, i, ROWS * g:ROWS * g + ROWS], ps[:, 0, ROWS * g:ROWS * g + ROWS],
                                            rstd1[:, g:g + 1], None, ALU.mult)
                ins.then_inc(s["evac_v"], 1)

            def row_max(j, i):
                dve.wait_ge(s["evac_v"], j * CH + i + 1)
                dve.wait_ge(s["evac_a"], j * CH + i + 1)
                if i > 1:
                    dve.wait_ge(s["max_done"], j * (CH - 1) + i - 1)
                dve.tensor_tensor(run_max[:, :], scores[:, 0, :] if i == 1 else run_max[:, :], scores[:, i, :],
                                  ALU.max).then_inc(s["max_done"], 1)

            def scale_out(k):
                dve.wait_ge(s["alpha_ready"], k + 1)
                dve.wait_ge(s["merged"], HC * k)
                for c in range(HC):
                    dve.scalar_tensor_tensor(out=o_acc[:, c, :], in0=alpha[:, :], scalar=1.0, in1=o_acc[:, c, :],
                                             op0=ALU.min, op1=ALU.mult).then_inc(s["o_scaled"], 1)

            def merge(k):
                dve.wait_ge(s["pv_rh"], 2 * CH * (k + 1))
                if not (isinstance(k, int) and k == 0):
                    dve.wait_ge(s["o_scaled"], HC * k)
                for c in range(HC):
                    dve.tensor_tensor(o_acc[:, c, :], o_acc[:, c, :],
                                      po[:, 2 * c:2 * c + 2, :].rearrange("p b n -> p (b n)"),
                                      ALU.add).then_inc(s["merged"], 1)

            def maxima(j, k, then=None):
                dve.wait_ge(s["rt_done"], j + 1)
                dve.tensor_reduce(mx[:, :], pk.rearrange("p b (g r) -> p (b g) r", g=4), X, ALU.max)\
                   .then_inc(s["mx_raw"], 1)
                dve.wait_ge(s["mx_raw"], j + 1)
                dve.tensor_tensor(mx[:, :], mx[:, :], c_col[:, :], ALU.add).then_inc(s["mx_full"], 1)
                dve.wait_ge(s["mx_full"], j + 1)
                dve.tensor_tensor(mx[:, :], c_col[:, :], mx[:, :], ALU.subtract).then_inc(s["mx_ready"], 1)
                new = ps.rearrange("p b n -> p (b n)")
                if k is not None:
                    dve.wait_ge(s["psum_add"], 2 * CH * (k + 1))
                    dve.wait_ge(s["psum_scaled"], k + 1)
                    if not (isinstance(k, int) and k == 0):
                        dve.wait_ge(s["o_scaled"], HC * k)
                dve.wait_ge(s["mb_done"], j + 1)
                dve.tensor_tensor(alpha[:, :], new, neg_max[:, :], ALU.subtract).then_inc(s["alpha_diff"], 1)
                dve.wait_ge(s["alpha_diff"], j + 1)
                dve.tensor_tensor(neg_max[:, :], neg_max[:, :], new, ALU.min).then_inc(s["max_ready"], 1)
                if then is not None:
                    dve.wait_ge(s["max_ready"], j + 1)
                    then()
                if k is not None:
                    merge(k)

            def scale_sum(j):
                dve.wait_ge(s["alpha_ready"], j + 1)
                dve.scalar_tensor_tensor(out=p_sum[:, :], in0=alpha[:, :], scalar=1.0, in1=p_sum[:, :],
                                         op0=ALU.min, op1=ALU.mult).then_inc(s["psum_scaled"], 1)

            def shift_last(i):
                for h in range(2):
                    q = scores[:, i, 512 * h:512 * h + 512]
                    dve.tensor_tensor(q, q, neg_max[:, 512 * h:512 * h + 512], ALU.add).then_inc(s["p_shift"], 1)

            low_t(0, 0)
            for i in range(CH):
                sums(0, i)
                low_t((i + 1) // CH, (i + 1) % CH)
                evacuate(0, i)
                if i:
                    row_max(0, i)
                if i == 1:
                    c3 = cat_t[:, 0:1024].rearrange("p (h t) -> p h t", t=S)
                    v.settle(dve, dve.tensor_tensor(c3, c3, smooth_inv[:, 0:16].unsqueeze(2).broadcast_to([128, 16, S]),
                                                    ALU.mult))
                if i == 2:
                    fp8_round(cat_t[:, 0:1024], cat_t[:, 0:1024], alpha[:, 0:512].bitcast(BF16),
                              alpha[:, 512:1024].bitcast(BF16), p_f.rearrange("p b n -> p (b n)"), s["catq_ready"])
            maxima(0, None)
            scale_sum(0)

            def dve_chunk(j, k, last=False):
                for i in range(CH):
                    low_n(k, i)
                    low_p(k, i, 0, p_f[:, 0, :])
                    sums(j, i)
                    low_p(k, i, 1, p_f[:, 1, :])
                    if i < CH - 1:
                        low_t(j, i + 1)
                    elif not last:
                        low_t(j + 1, 0)
                    evacuate(j, i)
                    if i:
                        row_max(j, i)
                    elif not (isinstance(k, int) and k == 0):
                        scale_out(k)
                if last:
                    maxima(j, k, lambda: shift_last(0))
                else:
                    maxima(j, k)
                    scale_sum(j)

            dve_chunk(1, 0)
            with dve.Fori(2, NCH - 1) as j:
                dve_chunk(j, j - 1)
            dve_chunk(NCH - 1, NCH - 2, last=True)

            for i in range(CH):
                if 0 < i < CH - 1:
                    shift_last(i + 1)
                (raw, hi, lo), _, _ = last_tiles[i]
                dve.wait_ge(s["cn_half"], CH * (NCH - 1) + i + 1)
                dve.tensor_tensor(lo, raw, hi.bitcast(F32), ALU.subtract).then_inc(s["cn_split"], 1)
                for h in range(2):
                    low_p(NCH - 1, i, h, scores[:, i, 512 * h:512 * h + 512], last_hi[i % 2], last_lo[i % 2])
                if i == 0:
                    scale_sum(NCH - 1)
                    shift_last(1)
                    scale_out(NCH - 1)
            dve.wait_ge(s["den_done"], 1)
            dve.reciprocal(mx[:, :], pk[:, 0, 0:G]).then_inc(s["den_in"], 1)
            merge(NCH - 1)
            cx = cat_t[:, 1024:2048]
            dve.wait_ge(s["den_spread"], 1)
            v.settle(dve, dve.tensor_tensor(neg_max.rearrange("p (h t) -> p h t", t=S), pk.rearrange("p b (h t) -> p (b h) t", t=S),
                                            smooth_inv[:, 16:32].unsqueeze(2).broadcast_to([128, 16, S]), ALU.mult))
            dve.wait_ge(s["xo_done"], 1)
            v.settle(dve, dve.tensor_tensor(cx, ps.rearrange("p b n -> p (b n)"), neg_max[:, :], ALU.mult))
            for n in range(2):
                q = cx[:, 512 * n:512 * n + 512]
                fp8_round(q, q, scores[:, 3, 0:256].bitcast(BF16), scores[:, 3, 256:512].bitcast(BF16),
                          scores[:, 4, 0:512], s["catq_ready"])
            v.settle(dve, dve.tensor_scalar(stat[0:S, 40:41], sm("pw_s", S), sm("pin_s", S), None, ALU.mult))
            dve.wait_ge(s["proj_done"], 1)
            dve.tensor_copy(half, bank[0][:, 0:H]).then_inc(s["half_in"], 1)
            dve.wait_ge(s["fold_done"], 1)
            dve.scalar_tensor_tensor(out=x_res[:, :], in0=bank[1][0:S, 0:H], scalar=stat[0:S, 40:41],
                                     in1=x_res[:, :], op0=ALU.mult, op1=ALU.add).then_inc(s["x1_ready"], 1)
            dve.wait_ge(s["x1_ready"], 1)
            second_vector(dve, s, ph2, v, layernorm_rows, bank, small, x_res, ident)

        @block.tensor
        def _(pe):
            pe.wait_ge(s["const_ready"], 1)
            pe.wait_ge(s["normed"], 2)
            for c in range(HC):
                ins = pe.transpose(bank[0][:, c * S:c * S + S], xn[:, 128 * c:128 * c + 128], ident[0:S, 0:S])
            ins.then_inc(s["xT_done"], 1)
            n = 0
            for k, (w, key, count) in enumerate(((wqx, "w_qx", 4), (wq, "w_q", 4), (wk, "w_k", 2), (wv, "w_v", 2))):
                pe.wait_ge(s["xq_ready"], HC * (k + 1))
                pe.wait_ge(s[key], 16)
                for b in range(count):
                    if n >= 8:
                        pe.wait_ge(s["lin_evac"], n - 7)
                    for c in range(HC):
                        ins = pe.matmul(bank[n % 8][0:S, :], xq[k][:, c * S:c * S + S], w[:, c, 512 * b:512 * b + 512],
                                        start=(c == 0), stop=(c == HC - 1))
                    ins.then_inc(s["lin_done"], 1)
                    n += 1
            pe.wait_ge(s["lin_evac"], 12)
            for h in range(40):
                pe.wait_ge(s["heads_ready"], h + 1)
                ins = pe.transpose(bank[h // 8][:, S * (h % 8):S * (h % 8) + S], heads[:, D * h:D * h + D], ident[0:S, 0:S])
                if h in (15, 31, 39):
                    ins.then_inc(s["headT_done"], 1)
            pe.wait_ge(s["qkT_ready"], 1)
            for b in range(2):
                ins = pe.matmul(bank[5 + b], mean_w, qkw[:, 512 * b:512 * b + 512], start=True, stop=True)
            ins.then_inc(s["qmean_done"], 1)
            for g in range(G):
                ins = pe.matmul(bank[7][:, S * g:S * g + S], qT[:, ROWS * g:ROWS * g + ROWS], kT[:, S * g:S * g + S],
                                start=True, stop=True)
            ins.then_inc(s["s_self"], 1)
            for g in range(G):
                ins = pe.matmul(bank[0][:, g:g + 1], qxT[:, ROWS * g:ROWS * g + ROWS], sm("kxln_b"), start=True, stop=True)
            ins.then_inc(s["cbc_done"], 1)
            pe.wait_ge(s["c_ready"], 1)
            pe.wait_ge(s["qc_ready"], 2)
            pe.wait_ge(s["kxd_in"], 16)
            for c in range(HC):
                for g in range(G):
                    ins = pe.matmul(po[:, 2 * c + g // 4, ROWS * (g % 4):ROWS * (g % 4) + ROWS],
                                    kxd[:, g, 128 * c:128 * c + 128], qkw[:, ROWS * g:ROWS * g + ROWS],
                                    start=True, stop=True)
            ins.then_inc(s["qk_done"], 1)
            pe.wait_ge(s["p_self"], 2)
            for g in range(G):
                ins = pe.transpose(pk[0:S, g // 4, ROWS * (g % 4):ROWS * (g % 4) + ROWS], pself[:, S * g:S * g + S], ident[:, :])
            ins.then_inc(s["pT_self"], 1)
            pe.wait_ge(s["pT_evac"], 1)
            for g in range(G):
                ins = pe.matmul(ps[:, g // 4, ROWS * (g % 4):ROWS * (g % 4) + ROWS], vrow[:, D * g:D * g + D],
                                pTs[:, ROWS * g:ROWS * g + ROWS], start=True, stop=True)
            ins.then_inc(s["core_done"], 1)
            pe.wait_ge(s["q_split"], 1)
            pe.wait_ge(s["k_split"], 1)
            pe.wait_ge(s["cat_core"], 1)

            def product(out, lo_hi, w_hi, w_lo, b, n):
                hi, lo = lo_hi
                k = 0
                for c in range(HC):
                    st = hi[:, b, 128 * c:128 * c + 128]
                    for w in (w_hi, w_lo):
                        pe.matmul(out, st, w[:, c, 512 * n:512 * n + 512], start=(k == 0), stop=False)
                        k += 1
                for c in range(HC):
                    ins = pe.matmul(out, lo[:, b, 128 * c:128 * c + 128], w_hi[:, c, 512 * n:512 * n + 512],
                                    start=False, stop=(c == HC - 1))
                return ins

            def keys_scores(j, i):
                b = BUF[i]
                pe.wait_ge(s["ct_split"], j * CH + i + 1)
                for n in range(2):
                    if not (isinstance(j, int) and j == 0 and i == 0):
                        pe.wait_ge(s["ksq_act"], 2 * (j * CH + i) + n - 1)
                        if i == 0:
                            pe.wait_ge(s["mx_raw"], j)
                    product(pk[:, n, :], (ct_hi, ct_lo), k_hi, k_lo, b, n).then_inc(s["ksq_mm"], 1)
                for n in range(2):
                    if not (isinstance(j, int) and j == 0 and i == 0):
                        pe.wait_ge(s["evac_a" if n else "evac_v"], j * CH + i)
                        if i == 0:
                            pe.wait_ge(s["max_ready"], j)
                    product(ps[:, n, :], (ct_hi, ct_lo), q_hi, q_lo, b, n).then_inc(s["s_mm"], 1)

            def weighted(j, i, ctx_hi, ctx_lo, hi=p_hi, lo=p_lo):
                pe.wait_ge(s["cn_split"], j * CH + i + 1)
                if i == 0 and not (isinstance(j, int) and j == 0):
                    pe.wait_ge(s["merged"], HC * j)
                for h in range(2):
                    pe.wait_ge(s["p_lo_ready"], 2 * (j * CH + i) + h + 1)
                    for c in range(HC):
                        out = po[:, 2 * c + h, :]
                        st = ctx_hi[:, 128 * c:128 * c + 128]
                        pe.matmul(out, st, hi[:, h, :], start=(i == 0), stop=False)
                        pe.matmul(out, st, lo[:, h, :], start=False, stop=False)
                        ins = pe.matmul(out, ctx_lo[:, 128 * c:128 * c + 128], hi[:, h, :],
                                        start=False, stop=(i == CH - 1))
                    ins.then_inc(s["pv_rh"], 1)

            def turn_max(j):
                pe.wait_ge(s["max_done"], (CH - 1) * (j + 1))
                pe.wait_ge(s["ksq_act"], 2 * CH * (j + 1))
                for g in range(G):
                    ins = pe.transpose(pk[:, g // 4, ROWS * (g % 4):ROWS * (g % 4) + ROWS],
                                       run_max[:, ROWS * g:ROWS * g + ROWS], ident[:, :])
                ins.then_inc(s["rt_done"], 1)

            def spread_max(j):
                pe.wait_ge(s["mx_ready"], j + 1)
                pe.wait_ge(s["evac_v"], CH * (j + 1))
                pe.wait_ge(s["evac_a"], CH * (j + 1))
                for g in range(G):
                    ins = pe.transpose(ps[:, g // 4, ROWS * (g % 4):ROWS * (g % 4) + ROWS],
                                       mx[:, g:g + 1].broadcast_to([128, 128]), ident[:, :])
                ins.then_inc(s["mb_done"], 1)

            for i in range(CH):
                keys_scores(0, i)
            turn_max(0)
            spread_max(0)

            def pe_chunk(j, k):
                for i in range(CH):
                    keys_scores(j, i)
                    weighted(k, i, cn_hi[:, BUF[i], :], cn_lo[:, BUF[i], :])
                turn_max(j)
                spread_max(j)

            pe_chunk(1, 0)
            with pe.Fori(2, NCH) as j:
                pe_chunk(j, j - 1)
            for i in range(CH):
                weighted(NCH - 1, i, *last_tiles[i][0][1:], last_hi[i % 2], last_lo[i % 2])
            pe.wait_ge(s["psum_add"], 2 * CH * NCH)
            for g in range(G):
                ins = pe.matmul(pk[:, 0, g:g + 1], p_sum[:, ROWS * g:ROWS * g + ROWS], ones[:, 0:1], start=True, stop=True)
            ins.then_inc(s["den_done"], 1)
            pe.wait_ge(s["den_in"], 1)
            for g in range(G):
                ins = pe.transpose(pk[:, g // 4, ROWS * (g % 4):ROWS * (g % 4) + ROWS],
                                   mx[:, g:g + 1].broadcast_to([128, 128]), ident[:, :])
            ins.then_inc(s["den_spread"], 1)
            pe.wait_ge(s["merged"], HC * NCH)
            pe.wait_ge(s["wv_in"], 16)
            for g in range(G):
                for c in range(HC):
                    ins = pe.matmul(ps[:, g // 4, ROWS * (g % 4):ROWS * (g % 4) + ROWS],
                                    wv_x[:, c, D * g:D * g + D], o_acc[:, c, ROWS * g:ROWS * g + ROWS],
                                    start=(c == 0), stop=(c == HC - 1))
            ins.then_inc(s["xo_done"], 1)
            pe.wait_ge(s["wproj_in"], 16)
            for k in range(32):
                if k % 8 == 0 and k != 8:
                    pe.wait_ge(s["catq_ready"], max(k // 8, 1))
                r = HALVES[k % 2]
                ins = pe.matmul(bank[0][r, 0:H], cat_t[:, S * k:S * k + S], mid[:, H * k:H * k + H],
                                start=(k < 2), stop=(k >= 30))
            ins.then_inc(s["proj_done"], 1)
            pe.wait_ge(s["half_in"], 1)
            pe.matmul(bank[1][0:S, 0:H], fold[:, :], half, start=True, stop=True).then_inc(s["fold_done"], 1)
            second_tensor(pe, s, ph2, bank, small, ident, ones, wide, mid)


def second_memory(m, sb):
    area = sb("area", [128, 27000])

    def at(a, n, rows=128):
        return area[0:rows, a:a + n]

    m["raw"] = at(0, 4288).rearrange("p (c t) -> p c t", t=S + 3)
    m["cv"] = at(4288, 4096)
    m["tok"] = at(8384, 1024).rearrange("p (b n) -> p b n", b=2)
    m["bv"] = at(9408, 2048)
    m["yo"] = at(9408, 2048)
    m["tap0"] = at(11456, 1024).rearrange("p (b n) -> p b n", b=2)
    m["tap1"] = at(12480, 1024).rearrange("p (b n) -> p b n", b=2)
    m["u"] = at(11456, 2048)
    m["tap2"] = at(13504, 512)
    m["sq"] = at(14016, 2048)
    m["zs"] = at(16064, 2048)
    m["gam"] = at(18112, 1024)
    m["z"] = at(18112, 1024)
    m["a_t"] = at(19136, 1024)
    m["yo_t"] = at(18112, 2048)
    m["l"] = at(20160, 1024)
    m["gt"] = at(21184, 1024)
    m["lm"] = [at(21184, 1024), at(22208, 1024)]
    m["y"] = at(23232, 1024)
    m["yt"] = at(24256, 1024)
    b = 25280
    for name, n in (("lb", 256), ("tb", 256), ("tbt", 256), ("tmp", 64), ("xn", 256), ("h_t", 128), ("tri", 64),
                    ("strict", 64), ("mask", 128), ("g", 16), ("beta", 16), ("t1", 16), ("t2", 16),
                    ("t3", 16), ("cg", 16), ("ea", 16), ("rn", 16)):
        m[name] = at(b, n)
        b += n
    m["xn"] = m["xn"][0:S, :]
    m["far"] = m["lb"][:, 0:S]
    m["row"] = m["lb"][:, S:2 * S]
    m["down"] = at(0, 8192)
    m["hx"] = at(8384, 2304)
    m["hx_t"] = at(10688, 2304)
    m["half"] = at(13504, 256)
    m["route"] = at(13760, 128)
    m["base_up"] = at(20160, 2048)
    m["base_down"] = at(22208, 1024)


SECOND = """wqkv_in normed ct_half cn_half ss_eps o_scaled out_ready wz_in wout_in up_in down_in base_in hT_done
    hT_ready ba_done gates_act gates_b g_ready cg_done cg_ready gt_ready cgb_done tok_mm tok_in turn_mm
    raw_in pad_ready tap1_ready tap_ready conv_ready silu_ready z_mm z_silu sq_ready sq_mm norm_in
    norm_pow norm_diag norm_bc normed_qk vT_done bv_ready gam_diff gam_ready l_masked kk_done at_ready
    l_ready blocks_moved y_zero inverse_ready lm_ready cy_mm cy_in d_mm y_new u_mm u_in o_mm o_ready
    yn_ready yoT_done yoT_in out_mm half_in fold_done x2_ready logit_done r_exp comb_ready up_mm
    gate_silu hid_ready hidT_done hidT_in down_mm""".split()
EXPERT_ORDER = [EXPERTS] + list(range(EXPERTS))
OUT_BANK = [6, 7, 0, 1]
HALVES = (slice(0, S), slice(S, 2 * S))
BLK = 16


def second_loads(sp, s, t, m, wide, mid):
    sp.wait_ge(s["proj_done"], 1)
    sp.dma_start(mid[:, :], t["W_z"], max_dma_last_dim=8192).then_inc(s["wz_in"], 16)
    sp.wait_ge(s["tok_mm"], 8)
    sp.dma_start(wide[:, :], t["up"], max_dma_last_dim=8192).then_inc(s["up_in"], 16)
    sp.wait_ge(s["l_ready"], 2)
    sp.dma_start(t["l_blocks"], m["l"]).then_inc(s["blocks_moved"], 16)
    sp.wait_ge(s["blocks_moved"], 16)
    rows = t["l_blocks"].rearrange("r (p c) -> r p c", c=S)
    for k in range(8):
        at, col = BLK * k, BLK * (k % 4)
        sp.dma_start(m["lb"][at:at + BLK, :].rearrange("p (r c) -> p r c", c=BLK),
                     rows[at:at + BLK, :, col:col + BLK].rearrange("r p c -> p r c")).then_inc(s["blocks_moved"], 16)
    sp.wait_ge(s["inverse_ready"], 2)
    sp.dma_start(t["inverses"][0], m["tb"]).then_inc(s["blocks_moved"], 16)
    sp.dma_start(t["inverses"][1], m["tbt"]).then_inc(s["blocks_moved"], 16)
    sp.wait_ge(s["blocks_moved"], (1 + 8 + 2) * 16)
    sp.wait_ge(s["y_zero"], 2)
    for dst, src in ((m["yt"], t["inverses"][0]), (m["y"], t["inverses"][1])):
        for k in range(8):
            at, col = BLK * k, BLK * (k % 4)
            sp.dma_start(dst[at:at + BLK, :].rearrange("r (p c) -> r p c", c=S)[:, :, col:col + BLK],
                         src[at:at + BLK, :].rearrange("p (r c) -> r p c", c=BLK)).then_inc(s["blocks_moved"], 16)
    sp.wait_ge(s["z_mm"], 4)
    sp.dma_start(mid[:, :], t["W_out"], max_dma_last_dim=8192).then_inc(s["wout_in"], 16)
    sp.wait_ge(s["bv_ready"], 4)
    sp.dma_start(m["down"], t["down"], max_dma_last_dim=8192).then_inc(s["down_in"], 16)
    sp.wait_ge(s["u_mm"], 4)
    sp.dma_start(m["base_up"], t["base_up"]).then_inc(s["base_in"], 16)
    sp.dma_start(m["base_down"], t["base_down"]).then_inc(s["base_in"], 16)


def second_pool(pool, s, m, inv_root, ident, cst, small):
    pool.wait_ge(s["x1_ready"], 1)
    pool.memset(m["tri"], 1.0).then_inc(s["pool_step"], 1)
    pool.memset(m["strict"], 1.0).then_inc(s["pool_step"], 1)
    pool.memset(m["raw"][:, :, 0:3], 0.0).then_inc(s["pad_ready"], 1)
    pool.wait_ge(s["pool_step"], 5)
    pool.wait_ge(s["pad_ready"], 1)
    for k, r in enumerate(HALVES):
        for name, op, pattern, mul in (("tri", ALU.is_ge, [[1, S]], -1), ("strict", ALU.is_gt, [[-1, S]], 1)):
            pool.affine_select(out=m[name][r, :], in_=m[name][r, :], compare_op=op, fill=0.0, base=0,
                               pattern=pattern, channel_multiplier=mul).then_inc(s["pool_step"], 1)
        pool.iota(m["row"][r, :].bitcast(I32), [[0, S]], base=0, channel_multiplier=1).then_inc(s["pool_step"], 1)
        pool.wait_ge(s["pool_step"], 5 + 3 * (k + 1))
    pool.iota(m["far"].bitcast(I32), [[1, S]], base=0, channel_multiplier=0).then_inc(s["pool_step"], 1)
    pool.wait_ge(s["pool_step"], 12)
    inv_root(m["stat"][0:S, 8:9], m["stat"][0:S, 7:8], S, 1)
    w = small[:, SMALL["conv"][0]:SMALL["conv"][0] + 256].rearrange("p (c j) -> p c j", j=4)

    def first_tap(n):
        c = slice(8 * n, 8 * n + 8)
        pool.wait_ge(s["raw_in"], n + 1)
        if n >= 2:
            pool.wait_ge(s["conv_ready"], n - 1)
        pool.tensor_tensor(m["tap0"][:, n % 2, :].rearrange("p (c t) -> p c t", t=S), m["raw"][:, c, 0:S],
                           w[:, c, 0:1].broadcast_to([128, 8, S]), ALU.mult).then_inc(s["pool_step"], 1)
        pool.wait_ge(s["pool_step"], 12 + n + 1)
        pool.wait_ge(s["tap1_ready"], n + 1)
        pool.tensor_tensor(m["tap0"][:, n % 2, :], m["tap0"][:, n % 2, :], m["tap1"][:, n % 2, :],
                           ALU.add).then_inc(s["tap_ready"], 1)

    for n in range(4):
        first_tap(n)
    for q in range(2):
        pool.wait_ge(s["gam_ready"], q + 1)
        pool.tensor_tensor(by_head(m["l"], q), by_head(m["gam"], q), over_heads(m["strict"]),
                           ALU.mult).then_inc(s["l_masked"], 1)
    pool.wait_ge(s["norm_in"], 1)
    pool.tensor_tensor(m["rn"], m["rn"], cst[:, 0:1].broadcast_to([128, 16]), ALU.pow).then_inc(s["norm_pow"], 1)
    pool.memset(m["y"], 0.0).then_inc(s["y_zero"], 1)
    pool.memset(m["yt"], 0.0).then_inc(s["y_zero"], 1)
    first_tap(4)
    first_tap(5)
    pool.wait_ge(s["cgb_done"], 1)
    pool.wait_ge(s["l_ready"], 2)
    for lv in range(2):
        for q in range(2):
            pool.tensor_tensor(by_head(m["lm"][lv], q), by_head(m["l"], q), over_heads(m["mask"][:, S * lv:S * lv + S]),
                               ALU.mult).then_inc(s["lm_ready"], 1)
    first_tap(6)
    first_tap(7)
    pool.wait_ge(s["norm_in"], 2)
    pool.tensor_tensor(m["rn"], m["rn"], cst[:, 0:1].broadcast_to([128, 16]), ALU.pow).then_inc(s["norm_pow"], 1)
    inv_root(m["stat"][0:S, 8:9], m["stat"][0:S, 7:8], S, 1)


def by_head(a, q):
    return a[:, 512 * q:512 * q + 512].rearrange("p (h t) -> p h t", t=S)


def over_heads(a):
    return a.unsqueeze(1).broadcast_to([a.shape[0], 8, a.shape[1]])


def over_tokens(a, q):
    return a[:, 8 * q:8 * q + 8].unsqueeze(2).broadcast_to([a.shape[0], 8, S])


def second_scalar(act, s, m, bank, small):
    def to_rows(n):
        act.wait_ge(s["tok_mm"], n + 1)
        if n >= 2:
            act.wait_ge(s["turn_mm"], n - 1)
        act.copy(m["tok"][:, n % 2, :], bank[n % 2]).then_inc(s["tok_in"], 1)

    def to_channels(n):
        act.wait_ge(s["turn_mm"], n + 1)
        dst = m["raw"][:, 8 * n:8 * n + 8, 3:S + 3].rearrange("p (e k) t -> p e k t", e=2)
        act.copy(dst, bank[2 + n % 2].rearrange("p (k e t) -> p e k t", e=2, t=S)).then_inc(s["raw_in"], 1)

    def silu(n):
        c = m["cv"][:, 512 * n:512 * n + 512]
        act.wait_ge(s["conv_ready"], n + 1)
        act.activation(c, c, ACT.Silu).then_inc(s["silu_ready"], 1)

    act.wait_ge(s["ba_done"], 1)
    act.activation(m["t1"], bank[6][:, 0:16], ACT.Exp, scale=-1.0).then_inc(s["gates_act"], 1)
    a = SMALL["A_log"][0]
    act.activation(m["ea"], small[:, a:a + 16], ACT.Exp).then_inc(s["gates_act"], 1)
    to_rows(0)
    act.wait_ge(s["gates_b"], 1)
    act.activation(m["t3"], m["t3"], ACT.Exp, scale=-1.0).then_inc(s["gates_act"], 1)
    act.wait_ge(s["gates_act"], 3)
    act.activation(m["t3"], m["t3"], ACT.Ln, bias=m["stat"][:, 15:16]).then_inc(s["gates_act"], 1)
    act.wait_ge(s["pad_ready"], 1)
    to_rows(1)
    to_channels(0)
    to_rows(2)
    to_channels(1)
    to_rows(3)
    to_channels(2)
    to_channels(3)
    for n in range(4):
        silu(n)
        act.wait_ge(s["silu_ready"], n + 1)
        act.activation(m["sq"][:, 512 * n:512 * n + 512], m["cv"][:, 512 * n:512 * n + 512], ACT.Square)\
           .then_inc(s["sq_ready"], 1)
        to_rows(4 + n)
        if n:
            to_channels(3 + n)
    to_channels(7)
    for q in range(2):
        gq = m["gam"][:, 512 * q:512 * q + 512]
        act.wait_ge(s["gam_diff"], q + 1)
        act.activation(gq, gq, ACT.Exp, scale=-1.0).then_inc(s["gam_ready"], 1)
    for n in range(4):
        act.wait_ge(s["z_mm"], n + 1)
        act.activation(m["zs"][:, 512 * n:512 * n + 512], bank[4 + n % 2], ACT.Silu).then_inc(s["z_silu"], 1)
    for n in range(4, 8):
        silu(n)
    for lv in range(2):
        for q in range(2):
            act.wait_ge(s["cy_mm"], 2 * lv + q + 1)
            if lv:
                act.wait_ge(s["d_mm"], q + 1)
            act.copy(m["z"][:, 512 * q:512 * q + 512], bank[4 + q]).then_inc(s["cy_in"], 1)
    for n in range(4):
        act.wait_ge(s["u_mm"], n + 1)
        act.copy(m["u"][:, 512 * n:512 * n + 512], bank[2 + n]).then_inc(s["u_in"], 1)
    for n in range(4):
        c = slice(512 * n, 512 * n + 512)
        act.wait_ge(s["o_ready"], n + 1)
        act.activation(m["sq"][:, c], m["yo"][:, c], ACT.Square).then_inc(s["sq_ready"], 1)
    a = SMALL["norm_w"][0]
    for n in range(4):
        act.wait_ge(s["yoT_done"], n + 1)
        act.activation(m["yo_t"][:, 512 * n:512 * n + 512], bank[2 + n], ACT.Identity, scale=small[:, a:a + 1])\
           .then_inc(s["yoT_in"], 1)
    act.wait_ge(s["logit_done"], 2)
    act.activation(m["route"][:, 0:8], m["route"][:, 0:8], ACT.Exp).then_inc(s["r_exp"], 1)
    for n in range(9):
        act.wait_ge(s["up_mm"], n + 1)
        act.activation(m["hx"][:, 256 * n:256 * n + 256], bank[2 + n % 4][:, 0:256], ACT.Silu).then_inc(s["gate_silu"], 1)
        if n:
            hidden_turned(act, s, m, bank, n - 1)
    hidden_turned(act, s, m, bank, 8)


def hidden_turned(act, s, m, bank, n):
    act.wait_ge(s["hidT_done"], n + 1)
    act.copy(m["hx_t"][:, 256 * n:256 * n + 256], bank[6 + n % 2][:, 0:256]).then_inc(s["hidT_in"], 1)


def second_vector(dve, s, m, v, layernorm_rows, bank, small, x_res, ident):
    layernorm_rows(m["xn"], x_res[:, :])
    dve.wait_ge(s["hT_done"], 1)
    dve.tensor_copy(m["h_t"], bank[7][:, 0:128]).then_inc(s["hT_ready"], 1)
    v.by(dve.memset(m["stat"][:, 15:16], 1.0))
    dve.wait_ge(s["ba_done"], 1)
    dve.wait_ge(s["gates_act"], 1)
    a = SMALL["dt_bias"][0]
    v.settle(dve, dve.tensor_tensor(m["t2"], bank[6][:, 16:32], small[:, a:a + 16], ALU.add))
    dve.scalar_tensor_tensor(out=m["t3"], in0=m["t2"], scalar=-1.0, in1=m["t2"], op0=ALU.mult, op1=ALU.max)\
       .then_inc(s["gates_b"], 1)
    v.settle(dve, dve.tensor_scalar(m["t1"], m["t1"], 1.0, None, ALU.add))
    v.by(dve.reciprocal(m["beta"], m["t1"]))
    dve.wait_ge(s["pool_step"], 12)
    far, mask = m["far"], m["mask"]
    v.settle(dve, dve.tensor_tensor(far.bitcast(I32), far.bitcast(I32), m["row"].bitcast(I32), ALU.bitwise_xor))
    v.settle(dve, dve.tensor_copy(far, far.bitcast(I32)))
    v.settle(dve, dve.tensor_scalar(mask[:, 0:S], far, float(BLK), None, ALU.is_ge))
    v.by(dve.scalar_tensor_tensor(out=mask[:, 0:S], in0=far, scalar=float(2 * BLK), in1=mask[:, 0:S],
                                  op0=ALU.is_lt, op1=ALU.mult))
    v.by(dve.tensor_scalar(mask[:, S:2 * S], far, float(2 * BLK), None, ALU.is_ge))
    dve.wait_ge(s["gates_act"], 4)
    v.settle(dve, dve.scalar_tensor_tensor(out=m["t3"], in0=m["t2"], scalar=0.0, in1=m["t3"], op0=ALU.max, op1=ALU.add))
    dve.scalar_tensor_tensor(out=m["g"], in0=m["t3"], scalar=-1.0, in1=m["ea"], op0=ALU.mult, op1=ALU.mult)\
       .then_inc(s["g_ready"], 1)
    dve.wait_ge(s["g_ready"], 1)
    for q in range(2):
        dve.tensor_tensor(by_head(m["gt"], q), over_tokens(m["g"], q), over_heads(m["tri"]), ALU.mult)\
           .then_inc(s["gt_ready"], 1)
    w = small[:, SMALL["conv"][0]:SMALL["conv"][0] + 256].rearrange("p (c j) -> p c j", j=4)

    def tap(out, n, j):
        c = slice(8 * n, 8 * n + 8)
        return dve.tensor_tensor(out.rearrange("p (c t) -> p c t", t=S), m["raw"][:, c, j:S + j],
                                 w[:, c, j:j + 1].broadcast_to([128, 8, S]), ALU.mult)

    def convolve(n):
        out = m["cv"][:, 512 * n:512 * n + 512]
        dve.wait_ge(s["raw_in"], n + 1)
        if n >= 2:
            dve.wait_ge(s["tap_ready"], n - 1)
        tap(m["tap1"][:, n % 2, :], n, 1).then_inc(s["tap1_ready"], 1)
        v.by(tap(out, n, 3))
        v.settle(dve, tap(m["tap2"], n, 2))
        v.settle(dve, dve.tensor_tensor(out, out, m["tap2"], ALU.add))
        dve.wait_ge(s["tap_ready"], n + 1)
        dve.tensor_tensor(out, out, m["tap0"][:, n % 2, :], ALU.add).then_inc(s["conv_ready"], 1)

    convolve(0)
    dve.wait_ge(s["cg_done"], 1)
    dve.tensor_copy(m["cg"], bank[6][:, 32:48]).then_inc(s["cg_ready"], 1)
    dve.wait_ge(s["cg_ready"], 1)
    dve.wait_ge(s["cgb_done"], 1)
    for q in range(2):
        v.settle(dve, dve.tensor_tensor(by_head(m["gam"], q), by_head(bank[4 + q], 0), over_tokens(m["cg"], q),
                                        ALU.subtract))
        gq = m["gam"][:, 512 * q:512 * q + 512]
        dve.scalar_tensor_tensor(out=gq, in0=gq, scalar=-1.0, in1=gq, op0=ALU.mult, op1=ALU.max).then_inc(s["gam_diff"], 1)
    for n in range(1, 4):
        convolve(n)

    def diagonals(n):
        return dve.tensor_tensor(m["sq"][:, 512 * n:512 * n + 512].rearrange("p (k t) -> p k t", k=4),
                                 m["rn"][:, 4 * n:4 * n + 4].unsqueeze(2).broadcast_to([128, 4, 128]),
                                 ident[:, :].unsqueeze(1).broadcast_to([128, 4, 128]), ALU.mult)

    dve.wait_ge(s["sq_mm"], 1)
    dve.tensor_scalar(m["rn"], bank[7][:, 0:16], 1e-24, None, ALU.max).then_inc(s["norm_in"], 1)
    for q in range(2):
        dve.wait_ge(s["gam_ready"], q + 1)
        v.by(dve.tensor_tensor(by_head(m["a_t"], q), by_head(m["gam"], q), over_heads(m["tri"]), ALU.mult))
        dve.wait_ge(s["l_masked"], q + 1)
        v.by(dve.tensor_tensor(by_head(m["l"], q), by_head(m["l"], q), over_tokens(m["beta"], q), ALU.mult))
    dve.wait_ge(s["norm_pow"], 1)
    for n in range(4):
        diagonals(n).then_inc(s["norm_diag"], 1)
    for n in range(4):
        dve.wait_ge(s["norm_bc"], n + 1)
        c = m["cv"][:, 512 * n:512 * n + 512]
        dve.tensor_tensor(c, c, bank[4 + n % 2], ALU.mult).then_inc(s["normed_qk"], 1)
    dve.wait_ge(s["kk_done"], 1)
    v.by(dve.memset(m["tb"], 0.0))
    dve.wait_ge(s["dve_step"], v.n)
    for name, b, done in (("l", 6, "l_ready"), ("a_t", 7, "at_ready")):
        for q in range(2):
            pair = m[name][:, 512 * q:512 * q + 512].rearrange("p (k e t) -> p k e t", e=2, t=S)
            prod = bank[b][:, 256 * q:256 * q + 256].rearrange("p (k t) -> p k t", t=S)
            dve.tensor_tensor(pair, pair, prod.unsqueeze(2).broadcast_to([128, 4, 2, S]), ALU.mult).then_inc(s[done], 1)
    convolve(4)
    convolve(5)
    lb = m["lb"].rearrange("p (r c) -> p r c", c=BLK)
    tb = m["tb"].rearrange("p (r c) -> p r c", c=BLK)
    v.by(dve.memset(m["tb"][:, 0:BLK * BLK:BLK + 1], 1.0))
    dve.wait_ge(s["blocks_moved"], (1 + 8) * 16)
    dve.wait_ge(s["dve_step"], v.n)
    for j in range(BLK - 1):
        below, done = BLK - 1 - j, j + 1
        tmp = m["tmp"][:, 0:below * done].rearrange("p (r c) -> p r c", c=done)
        rows = tb[:, j + 1:BLK, 0:done]
        v.settle(dve, dve.tensor_tensor(tmp, lb[:, j + 1:BLK, j:j + 1].broadcast_to([128, below, done]),
                                        tb[:, j:j + 1, 0:done].broadcast_to([128, below, done]), ALU.mult))
        ins = dve.tensor_tensor(rows, rows, tmp, ALU.subtract)
        if j < BLK - 2:
            v.settle(dve, ins)
    ins.then_inc(s["inverse_ready"], 1)
    dve.wait_ge(s["inverse_ready"], 1)
    dve.tensor_copy(m["tbt"].rearrange("p (c r) -> p r c", r=BLK), tb).then_inc(s["inverse_ready"], 1)
    convolve(6)
    convolve(7)
    for n in range(4):
        dve.wait_ge(s["vT_done"], n + 1)
        dve.tensor_tensor(m["bv"][:, 512 * n:512 * n + 512].rearrange("p (h d) -> p h d", d=D),
                          bank[n].rearrange("p (h d) -> p h d", d=D),
                          m["beta"][:, 4 * n:4 * n + 4].unsqueeze(2).broadcast_to([128, 4, D]), ALU.mult)\
           .then_inc(s["bv_ready"], 1)
    dve.wait_ge(s["blocks_moved"], (1 + 8 + 2 + 16) * 16)
    for q in range(2):
        dve.wait_ge(s["d_mm"], q + 1)
        for name, b in (("y", 6 + q), ("yt", q)):
            a = m[name][:, 512 * q:512 * q + 512]
            dve.tensor_tensor(a, a, bank[b], ALU.subtract).then_inc(s["y_new"], 1)
    dve.wait_ge(s["y_new"], 4)
    for q in range(2):
        dve.wait_ge(s["d_mm"], 2 + q + 1)
        a = m["y"][:, 512 * q:512 * q + 512]
        dve.tensor_tensor(a, a, bank[6 + q], ALU.subtract).then_inc(s["y_new"], 1)
    for n in range(4):
        dve.wait_ge(s["o_mm"], n + 1)
        dve.wait_ge(s["z_silu"], n + 1)
        c = slice(512 * n, 512 * n + 512)
        dve.tensor_tensor(m["yo"][:, c], bank[OUT_BANK[n]], m["zs"][:, c], ALU.mult).then_inc(s["o_ready"], 1)
    for n in range(4):
        dve.wait_ge(s["sq_ready"], 4 + n + 1)
        v.by(dve.tensor_reduce(m["rn"][:, 4 * n:4 * n + 4],
                               m["sq"][:, 512 * n:512 * n + 512].rearrange("p (h d) -> p h d", d=D), X, ALU.add))
    dve.wait_ge(s["dve_step"], v.n)
    dve.tensor_scalar(m["rn"], m["rn"], 1.0 / D, 1e-6, ALU.mult, ALU.add).then_inc(s["norm_in"], 1)
    dve.wait_ge(s["norm_pow"], 2)
    for n in range(4):
        y = m["yo"][:, 512 * n:512 * n + 512].rearrange("p (h d) -> p h d", d=D)
        dve.tensor_tensor(y, y, m["rn"][:, 4 * n:4 * n + 4].unsqueeze(2).broadcast_to([128, 4, D]), ALU.mult)\
           .then_inc(s["yn_ready"], 1)
    dve.wait_ge(s["out_mm"], 1)
    dve.tensor_copy(m["half"], bank[6][:, 0:H]).then_inc(s["half_in"], 1)
    dve.wait_ge(s["fold_done"], 2)
    dve.tensor_tensor(x_res[:, :], x_res[:, :], bank[7][0:S, 0:H], ALU.add).then_inc(s["x2_ready"], 1)
    dve.wait_ge(s["x2_ready"], 1)
    layernorm_rows(m["xn"], x_res[:, :])
    dve.wait_ge(s["hT_done"], 2)
    dve.tensor_copy(m["h_t"], bank[0][:, 0:128]).then_inc(s["hT_ready"], 1)
    r = m["route"]
    p, w1, w2, pos, pick, top, tot = (r[:, 8 * k:8 * k + 8] for k in range(7))

    def first_best(out, vals, best):
        v.settle(dve, dve.tensor_reduce(best, vals, X, ALU.max))
        v.settle(dve, dve.tensor_scalar(pick, vals, best, None, ALU.is_ge))
        v.settle(dve, dve.tensor_tensor(pick, pick, pos, ALU.mult))
        v.settle(dve, dve.tensor_reduce(tot[:, 7:8], pick, X, ALU.max))
        v.settle(dve, dve.tensor_scalar(out, pos, tot[:, 7:8], None, ALU.is_equal))

    for e in range(EXPERTS):
        v.by(dve.memset(pos[:, e:e + 1], float(EXPERTS - e)))
    dve.wait_ge(s["logit_done"], 1)
    lg = bank[1][:, 0:EXPERTS]
    v.settle(dve, dve.tensor_reduce(top[:, 0:1], lg, X, ALU.max))
    dve.tensor_scalar(p, lg, top[:, 0:1], None, ALU.subtract).then_inc(s["logit_done"], 1)
    dve.wait_ge(s["r_exp"], 1)
    v.settle(dve, dve.tensor_reduce(top[:, 1:2], p, X, ALU.add))
    v.settle(dve, dve.reciprocal(top[:, 1:2], top[:, 1:2]))
    v.settle(dve, dve.tensor_scalar(p, p, top[:, 1:2], None, ALU.mult))
    first_best(w1, p, top[:, 2:3])
    v.settle(dve, dve.scalar_tensor_tensor(out=w2, in0=w1, scalar=-2.0, in1=p, op0=ALU.mult, op1=ALU.add))
    v.settle(dve, dve.tensor_copy(r[:, 56:64], w2))
    first_best(w2, r[:, 56:64], top[:, 3:4])
    v.settle(dve, dve.tensor_tensor(top[:, 4:5], top[:, 2:3], top[:, 3:4], ALU.add))
    v.settle(dve, dve.reciprocal(top[:, 4:5], top[:, 4:5]))
    v.settle(dve, dve.tensor_tensor(w1, w1, w2, ALU.add))
    dve.scalar_tensor_tensor(out=p, in0=p, scalar=top[:, 4:5], in1=w1, op0=ALU.mult, op1=ALU.mult)\
       .then_inc(s["comb_ready"], 1)
    for n, e in enumerate(EXPERT_ORDER):
        dve.wait_ge(s["gate_silu"], n + 1)
        hx = m["hx"][:, 256 * n:256 * n + 256]
        up = bank[2 + n % 4][:, 256:512]
        if e == EXPERTS:
            dve.tensor_tensor(hx, hx, up, ALU.mult).then_inc(s["hid_ready"], 1)
            dve.wait_ge(s["comb_ready"], 1)
        else:
            dve.scalar_tensor_tensor(out=hx, in0=hx, scalar=p[:, e:e + 1], in1=up, op0=ALU.mult, op1=ALU.mult)\
               .then_inc(s["hid_ready"], 1)
    dve.wait_ge(s["down_mm"], 1)
    dve.tensor_copy(m["half"], bank[0][:, 0:H]).then_inc(s["half_in"], 1)
    dve.wait_ge(s["fold_done"], 3)
    dve.tensor_tensor(x_res[:, :], x_res[:, :], bank[1][0:S, 0:H], ALU.add).then_inc(s["out_ready"], 1)


def second_tensor(pe, s, m, bank, small, ident, ones, wide, mid):
    h_t = m["h_t"]

    def turn(out, done):
        for c in range(HC):
            ins = pe.transpose(out[:, c * S:c * S + S], m["xn"][:, 128 * c:128 * c + 128], ident[0:S, 0:S])
        ins.then_inc(s[done], 1)

    def fold_halves(out, n):
        pe.wait_ge(s["half_in"], n)
        pe.matmul(out, m["fold"][:, :], m["half"], start=True, stop=True).then_inc(s["fold_done"], 1)

    pe.wait_ge(s["normed"], 3)
    turn(bank[7], "hT_done")
    pe.wait_ge(s["hT_ready"], 1)
    a = SMALL["W_ba"][0]
    wba = small[:, a:a + 128].rearrange("p (c b h) -> p c b h", c=HC, b=2)
    gates = bank[6][:, 0:32].rearrange("p (b h) -> p b h", b=2)
    for c in range(HC):
        for e, r in enumerate(HALVES):
            ins = pe.matmul(gates[r], h_t[:, S * c:S * c + S], wba[:, c, :, 16 * e:16 * e + 16],
                            start=(c == 0), stop=(c == HC - 1))
    ins.then_inc(s["ba_done"], 1)
    pe.wait_ge(s["wqkv_in"], 16)
    wq = wide[:, :].rearrange("p (h n) -> p h n", h=HC)

    def rows_round(n):
        if n >= 2:
            pe.wait_ge(s["tok_in"], n - 1)
        for c in range(HC):
            for e, r in enumerate(HALVES):
                ch = 1024 * n + 512 * e
                ins = pe.matmul(bank[n % 2][r, :], h_t[:, S * c:S * c + S], wq[:, c, ch:ch + 512],
                                start=(c == 0), stop=(c == HC - 1))
        ins.then_inc(s["tok_mm"], 1)

    def turn_round(n):
        pe.wait_ge(s["tok_in"], n + 1)
        if n >= 2:
            pe.wait_ge(s["raw_in"], n - 1)
        for k in range(4):
            ins = pe.transpose(bank[2 + n % 2][:, 128 * k:128 * k + 128], m["tok"][:, n % 2, 128 * k:128 * k + 128], ident[:, :])
        ins.then_inc(s["turn_mm"], 1)

    rows_round(0)
    for n in range(1, 4):
        rows_round(n)
        turn_round(n - 1)
    turn_round(3)
    pe.wait_ge(s["g_ready"], 1)
    for r in HALVES:
        ins = pe.matmul(bank[6][r, 32:48], m["tri"][r, :], m["g"][r, :], start=True, stop=True)
    ins.then_inc(s["cg_done"], 1)
    pe.wait_ge(s["gt_ready"], 2)
    for q in range(2):
        for r in HALVES:
            ins = pe.matmul(bank[4 + q][r, :], ones[r, 0:S], m["gt"][r, 512 * q:512 * q + 512], start=True, stop=True)
    ins.then_inc(s["cgb_done"], 1)
    for n in range(4, 8):
        rows_round(n)
        if n > 4:
            turn_round(n - 1)
    for k in range(16):
        pe.wait_ge(s["sq_ready"], k // 4 + 1)
        ins = pe.matmul(bank[7][:, k:k + 1], m["sq"][:, 128 * k:128 * k + 128], ones[:, 0:1], start=True, stop=True)
    ins.then_inc(s["sq_mm"], 1)
    turn_round(7)
    pe.wait_ge(s["gam_diff"], 2)
    for n in range(4):
        pe.wait_ge(s["norm_diag"], n + 1)
        if n >= 2:
            pe.wait_ge(s["normed_qk"], n - 1)
        pe.matmul(bank[4 + n % 2], ones[:, :], m["sq"][:, 512 * n:512 * n + 512], start=True, stop=True)\
          .then_inc(s["norm_bc"], 1)
    pe.wait_ge(s["normed_qk"], 4)
    pe.wait_ge(s["cg_ready"], 1)
    for k in range(8):
        for other, b in ((NK, 6), (0, 7)):
            for e, r in enumerate(HALVES):
                h = 8 * e + k
                key = m["cv"][:, S * (NK + h):S * (NK + h) + S]
                ins = pe.matmul(bank[b][r, S * k:S * k + S], key, m["cv"][:, S * (other + h):S * (other + h) + S],
                                start=True, stop=True)
    ins.then_inc(s["kk_done"], 1)
    pe.wait_ge(s["wz_in"], 16)
    wz = mid[:, :].rearrange("p (h n) -> p h n", h=HC)
    for n in range(4):
        if n >= 2:
            pe.wait_ge(s["z_silu"], n - 1)
        for c in range(HC):
            for e, r in enumerate(HALVES):
                ch = 2048 * e + 512 * n
                ins = pe.matmul(bank[4 + n % 2][r, :], h_t[:, S * c:S * c + S], wz[:, c, ch:ch + 512],
                                start=(c == 0), stop=(c == HC - 1))
        ins.then_inc(s["z_mm"], 1)
    pe.wait_ge(s["raw_in"], 8)
    pe.wait_ge(s["silu_ready"], 8)
    for n in range(4):
        for k in range(4):
            for e, r in enumerate(HALVES):
                at = 2048 + S * (16 * e + 4 * n + k)
                ins = pe.matmul(bank[n][r, D * k:D * k + D], m["cv"][:, at:at + S], ident[:, :], start=True, stop=True)
        ins.then_inc(s["vT_done"], 1)

    def pairs(out, lhs, rhs, ps, width):
        for i, p in enumerate(ps):
            for r in HALVES:
                ins = pe.matmul(out[r, width * i:width * i + width], lhs[r, S * p:S * p + S],
                                rhs[r, width * p:width * p + width], start=True, stop=True)
        return ins

    pe.wait_ge(s["blocks_moved"], (1 + 8 + 2 + 16) * 16)
    pe.wait_ge(s["z_silu"], 4)
    pe.wait_ge(s["at_ready"], 2)
    for lv in range(2):
        for q in range(2):
            pe.wait_ge(s["lm_ready"], 2 * lv + q + 1)
            if lv:
                pe.wait_ge(s["y_new"], 2 * q + 1)
            pairs(bank[4 + q], m["lm"][lv], m["y"], range(8 * q, 8 * q + 8), S).then_inc(s["cy_mm"], 1)
        for q in range(2):
            pe.wait_ge(s["cy_in"], 2 * lv + q + 1)
            if lv:
                pe.wait_ge(s["y_new"], 2 * q + 2)
            else:
                pe.wait_ge(s["bv_ready"], q + 1)
            ps = range(8 * q, 8 * q + 8)
            ins = pairs(bank[6 + q], m["yt"], m["z"], ps, S)
            if lv == 0:
                ins = pairs(bank[q], m["z"], m["yt"], ps, S)
            ins.then_inc(s["d_mm"], 1)
    pe.wait_ge(s["bv_ready"], 4)
    for n in range(4):
        pe.wait_ge(s["y_new"], 4 + n // 2 + 1)
        pairs(bank[2 + n], m["y"], m["bv"], range(4 * n, 4 * n + 4), D).then_inc(s["u_mm"], 1)
    pe.wait_ge(s["y_new"], 6)
    for n in range(4):
        pe.wait_ge(s["u_in"], n + 1)
        pairs(bank[OUT_BANK[n]], m["a_t"], m["u"], range(4 * n, 4 * n + 4), D).then_inc(s["o_mm"], 1)
    for n in range(4):
        pe.wait_ge(s["yn_ready"], n + 1)
        for k in range(4 * n, 4 * n + 4):
            ins = pe.transpose(bank[2 + n][:, 128 * (k % 4):128 * (k % 4) + 128], m["yo"][:, D * k:D * k + D], ident[:, :])
        ins.then_inc(s["yoT_done"], 1)
    pe.wait_ge(s["wout_in"], 16)
    for p in range(16):
        pe.wait_ge(s["yoT_in"], p // 4 + 1)
        for e, r in enumerate(HALVES):
            ins = pe.matmul(bank[6][r, 0:H], m["yo_t"][:, 128 * p + S * e:128 * p + S * e + S],
                            mid[:, H * (16 * e + p):H * (16 * e + p) + H], start=(p == 0), stop=(p == 15))
    ins.then_inc(s["out_mm"], 1)
    fold_halves(bank[7][0:S, 0:H], 2)
    pe.wait_ge(s["normed"], 4)
    turn(bank[0], "hT_done")
    pe.wait_ge(s["hT_ready"], 2)
    a = SMALL["gate"][0]
    for c in range(HC):
        for r in HALVES:
            ins = pe.matmul(bank[1][r, 0:EXPERTS], h_t[:, S * c:S * c + S], small[:, a + 8 * c:a + 8 * c + 8],
                            start=(c == 0), stop=(c == HC - 1))
    ins.then_inc(s["logit_done"], 1)
    pe.wait_ge(s["up_in"], 16)
    pe.wait_ge(s["base_in"], 32)

    def up(n):
        e = EXPERT_ORDER[n]
        w = (m["base_up"] if e == EXPERTS else wide[:, 2048 * e:2048 * e + 2048])\
            .rearrange("p (c b i) -> p c b i", c=HC, b=2)
        out = bank[2 + n % 4].rearrange("p (b i) -> p b i", b=2)
        if n >= 4:
            pe.wait_ge(s["hid_ready"], n - 3)
        for c in range(HC):
            for k, r in enumerate(HALVES):
                ins = pe.matmul(out[r], h_t[:, S * c:S * c + S], w[:, c, :, 256 * k:256 * k + 256],
                                start=(c == 0), stop=(c == HC - 1))
        ins.then_inc(s["up_mm"], 1)

    def turn_hidden(n):
        pe.wait_ge(s["hid_ready"], n + 1)
        if n >= 2:
            pe.wait_ge(s["hidT_in"], n - 1)
        for k in range(2):
            ins = pe.transpose(bank[6 + n % 2][:, 128 * k:128 * k + 128],
                               m["hx"][:, 256 * n + 128 * k:256 * n + 128 * k + 128], ident[:, :])
        ins.then_inc(s["hidT_done"], 1)

    def down(n):
        e = EXPERT_ORDER[n]
        w = m["base_down"] if e == EXPERTS else m["down"][:, 1024 * e:1024 * e + 1024]
        pe.wait_ge(s["hidT_in"], n + 1)
        if n == 1:
            pe.wait_ge(s["down_in"], 16)
        for k in range(2):
            for half, r in enumerate(HALVES):
                at, row = 256 * n + 128 * k + S * half, H * (2 * half + k)
                ins = pe.matmul(bank[0][r, 0:H], m["hx_t"][:, at:at + S], w[:, row:row + H],
                                start=(n == 0 and k == 0), stop=(n == 8 and k == 1))
        return ins

    for n in range(12):
        if n < 9:
            up(n)
        if 0 <= n - 2 < 9:
            turn_hidden(n - 2)
        if n >= 3:
            ins = down(n - 3)
    ins.then_inc(s["down_mm"], 1)
    fold_halves(bank[1][0:S, 0:H], 3)


def layout(i):
    f = lambda n: np.asarray(i[n])
    c = np.ascontiguousarray

    def by_width(w):
        return c(w.reshape(w.shape[0], HC, 128).transpose(2, 1, 0))

    def row(v):
        return np.broadcast_to(v.reshape(1, -1), (128, v.size))

    by_half = lambda v: np.repeat(v.reshape(2, NV // 2), S, axis=0)
    halves = lambda v: v.reshape(HC, 128).T
    a = "L0_xattn_"
    col = {"ln_w": halves(f(a + "ln_w")), "ln_b": halves(f(a + "ln_b")),
           "qx_in": halves(f(a + "qx_in_scale")), "q_in": halves(f(a + "q_in_scale")),
           "k_in": halves(f(a + "k_in_scale")), "v_in": halves(f(a + "v_in_scale")),
           "smooth": f(a + "proj_smooth").reshape(32, 128).T, "norm_w": f("L0_attn_norm_w").reshape(128, 1),
           "wqx_s": row(f(a + "wqx_scale")), "wq_s": row(f(a + "wq_scale")), "wk_s": row(f(a + "wk_scale")),
           "wv_s": row(f(a + "wv_scale")), "pw_s": row(f(a + "proj_w_scale")), "pin_s": row(f(a + "proj_in_scale")),
           "conv": f("L0_attn_conv_w").reshape(64, 128, 4).transpose(1, 0, 2).reshape(128, 256),
           "dt_bias": by_half(f("L0_attn_dt_bias")), "A_log": by_half(f("L0_attn_A_log")),
           "W_ba": by_width(np.concatenate([f("L0_attn_W_b"), f("L0_attn_W_a")])).reshape(128, 128),
           "gate": f("L0_ffn_gate_w").reshape(HC, 128, EXPERTS).transpose(1, 0, 2).reshape(128, 16)}
    for n in ("qxln", "qln", "kln", "kxln"):
        for e in "wb":
            col[f"{n}_{e}"] = f(f"{a}{n}_{e}").reshape(128, 1)
    ctx = f("ctx_2048").reshape(SC // 128, 128, H)
    kv = f(a + "w_kv_x")
    return {
        "x": c(f("x").reshape(S, H)),
        "small": c(np.concatenate([col[n] for n in SMALL], axis=1)),
        "wqx": by_width(f(a + "wqx")), "wq": by_width(f(a + "wq")), "wk": by_width(f(a + "wk")), "wv": by_width(f(a + "wv")),
        "kxT": by_width(kv[:1024]), "wvxT": by_width(kv[1024:]),
        "kxd": c(kv[:1024].reshape(G, D, H).transpose(1, 0, 2)),
        "ctT": c(ctx.reshape(SC // 128, 128, HC, 128).transpose(0, 3, 2, 1).reshape(SC // 128, 128, H)), "cn": c(ctx),
        "wprojT": c(f(a + "wproj").reshape(H, 32, 128).transpose(2, 1, 0).reshape(128, 8192)),
        "W_qkv": by_width(f("L0_attn_W_qkv")).reshape(128, 16384),
        "W_z": by_width(f("L0_attn_W_z")).reshape(128, 8192),
        "W_out": c(f("L0_attn_W_out").reshape(H, 32, 128).transpose(2, 1, 0).reshape(128, 8192)),
        "up": c(f("L0_ffn_expert_gate_up").reshape(EXPERTS, HC, 128, 1024).transpose(2, 0, 1, 3).reshape(128, 16384)),
        "down": c(f("L0_ffn_expert_down").reshape(EXPERTS, 4, 128, H).transpose(2, 0, 1, 3).reshape(128, 8192)),
        "base_up": c(f("L0_ffn_base_gate_up").reshape(HC, 128, 1024).transpose(1, 0, 2).reshape(128, 2048)),
        "base_down": c(f("L0_ffn_base_down").reshape(4, 128, H).transpose(1, 0, 2).reshape(128, 1024)),
    }


def kernel(**inputs):
    import concourse.bacc as bacc
    from concourse.bass_utils import run_bass_kernel_spmd

    nc = bacc.Bacc("TRN2", target_bir_lowering=False, num_devices=1)
    arrays = layout(inputs)
    t = {n: nc.dram_tensor("in_" + n, a.shape, F32, kind="ExternalInput").ap() for n, a in arrays.items()}
    t["out"] = nc.dram_tensor("out", (S, H), F32, kind="ExternalOutput").ap()
    build(nc, t)
    r = run_bass_kernel_spmd(nc, [{"in_" + n: a for n, a in arrays.items()}], core_ids=[0])
    return r.results[0]["out"].reshape(1, S, H)
```

```python
from contextlib import ExitStack

import numpy as np
import concourse.bass as bass
from concourse import mybir

ALU = mybir.AluOpType
ACT = mybir.ActivationFunctionType
F32 = mybir.dt.float32
F32R = mybir.dt.float32r
BF16 = mybir.dt.bfloat16
U16 = mybir.dt.uint16
I32 = mybir.dt.int32
X = mybir.AxisListType.X

S = 64
H = 256
HC = H // 128
D = 128
G = 8
NH = 16
ROWS = (NH // G) * S
GR = G * ROWS
SC = 6272
CH = 7
NCH = SC // 128 // CH
BUF = [0, 1, 0, 1, 0, 1, 2]
USES = [3, 3, 1]
NV = 32
NK = 16
EXPERTS = 8
INNER = 512
EPS = 1e-5
LIN_BANK = [0, 1, 2, 3, 4, 6, 7]
TURN_BANK = [0, 1, 6, 7, 4]
HALVES = (slice(0, S), slice(S, 2 * S))
FP8_MAX = 448.0


def prev_use(i):
    return {0: 3, 1: 3, 6: 7}.get(i, 2)


def buf_use(j, i):
    return j * USES[BUF[i]] + BUF[:i].count(BUF[i])


def ahead(j, i, n, last):
    if i + n < CH:
        return [(j, i + n)]
    return [] if last else [(j + 1, i + n - CH)]


class Tally:

    def __init__(self, sem):
        self.sem, self.n = sem, 0

    def by(self, ins):
        ins.then_inc(self.sem, 1)
        self.n += 1
        return self.n

    def settle(self, eng, ins):
        self.by(ins)
        eng.wait_ge(self.sem, self.n)


SMALL = {}
_at = 0
for _name, _n in (("ln_w", 2), ("ln_b", 2), ("qx_in", 2), ("q_in", 2), ("k_in", 2), ("v_in", 2),
                  ("qxln_w", 1), ("qxln_b", 1), ("qln_w", 1), ("qln_b", 1), ("kln_w", 1), ("kln_b", 1),
                  ("kxln_w", 1), ("kxln_b", 1), ("smooth", 32), ("norm_w", 1), ("wqx_s", 1), ("wq_s", 1),
                  ("wk_s", 1), ("wv_s", 1), ("pw_s", 1), ("pin_s", 1), ("conv", 256), ("dt_bias", 16),
                  ("A_log", 16), ("W_ba", 128), ("gate", 16)):
    SMALL[_name] = (_at, _n)
    _at += _n
NSMALL = _at


def build(nc, t):
    t = dict(t)
    t["l_blocks"] = nc.dram_tensor("l_blocks", (128, 1024), F32, kind="Internal").ap()
    t["inverses"] = nc.dram_tensor("inverses", (2, 128, BLK * BLK), F32, kind="Internal").ap()
    ctx = ExitStack()
    phase1 = ExitStack()
    loop_only = ExitStack()
    split_weights = ExitStack()

    def sb(name, shape, dt=F32, at=ctx):
        return at.enter_context(nc.sbuf_tensor(name, shape, dt))

    def sem(name):
        return ctx.enter_context(nc.semaphore(name))

    with ctx:
        wide = sb("wide", [128, 16384])
        k_hi = sb("k_hi", [128, HC, 1024], F32R, split_weights)
        k_lo = sb("k_lo", [128, HC, 1024], F32R, split_weights)
        q_hi = sb("q_hi", [128, HC, 1024], F32R, split_weights)
        q_lo = sb("q_lo", [128, HC, 1024], F32R, split_weights)
        split_weights.close()
        mid = sb("mid", [128, 8192])
        ident = sb("ident", [128, 128])
        ones = sb("ones", [128, 128])
        fold = sb("fold", [128, S])
        small = sb("small", [128, NSMALL])
        x_res = sb("x_res", [S, H])
        stat = sb("stat", [128, 64])
        rstd1 = sb("rstd1", [128, 8])
        smooth_inv = sb("smooth_inv", [128, 32])
        cst = sb("cst", [128, 8])

        eps8 = sb("eps8", [128, 8])

        scores = sb("scores", [128, CH, GR], F32, phase1)
        neg_max = sb("neg_max", [128, GR], F32, phase1)
        alpha = sb("alpha", [128, GR], F32, phase1)
        run_max = sb("run_max", [128, GR], F32, phase1)
        c_col = sb("c_col", [128, G], F32, phase1)
        mx = sb("mx", [128, G], F32, phase1)
        p_sum = sb("p_sum", [128, GR], F32, phase1)
        o_acc = sb("o_acc", [128, HC, GR], F32, phase1)
        p_hi = sb("p_hi", [128, 2, 512], F32R, phase1)
        p_lo = sb("p_lo", [128, 2, 512], F32R, phase1)
        ct_raw = sb("ct_raw", [128, 3, 256], F32, phase1)
        ct_hi = sb("ct_hi", [128, 3, 256], F32R, phase1)
        ct_lo = sb("ct_lo", [128, 3, 256], F32R, phase1)
        cn_raw = sb("cn_raw", [128, 3, 256], F32, phase1)
        cn_hi = sb("cn_hi", [128, 3, 256], F32R, phase1)
        cn_lo = sb("cn_lo", [128, 3, 256], F32R, phase1)
        ss = sb("ss", [128, 8], F32, phase1)
        cat_t = sb("cat_t", [128, 2048], F32, phase1)
        p_f = sb("p_f", [128, 2, 512], F32, loop_only)
        ksq = sb("ksq", [128, 2, 512], F32, loop_only)
        loop_only.close()
        p_lo2 = sb("p_lo2", [128, 2, 512], F32R, phase1)
        p_hi2 = sb("p_hi2", [128, 2, 512], F32R, phase1)
        last_hi = [p_hi, p_hi2]
        last_lo = [p_lo, p_lo2]
        half = o_acc[:, 0, 0:H]
        cn_buf = [(cn_raw[:, b, :], cn_hi[:, b, :], cn_lo[:, b, :]) for b in range(3)]
        ct_buf = [(ct_raw[:, b, :], ct_hi[:, b, :], ct_lo[:, b, :]) for b in range(3)]
        wv_x = scores[:, 0:2, :]
        phase1.close()
        ph2 = {}
        second_memory(ph2, sb)
        ph2["stat"] = stat
        ph2["fold"] = fold

        pk = ctx.enter_context(nc.psum_tensor("pk", [128, 2, 512], F32))
        ps = ctx.enter_context(nc.psum_tensor("ps", [128, 2, 512], F32))
        po = ctx.enter_context(nc.psum_tensor("po", [128, 4, 512], F32))
        bank = [po[:, 0, :], po[:, 1, :], po[:, 2, :], po[:, 3, :], pk[:, 0, :], pk[:, 1, :], ps[:, 0, :], ps[:, 1, :]]

        def sm(name, rows=128, k=None):
            a, n = SMALL[name]
            return small[0:rows, a:a + n] if k is None else small[0:rows, a + k:a + k + 1]

        names = """x_in small_in w_qx w_q w_k w_v kxT_in kxd_in const_ready pow_ask pow_done dve_step pool_step xT_done
            xq_ready lin_done lin_evac heads_ready headT_done qkT_ready heads_out km_ready k_centred k_high softmax_init
            qmean_done qc_ready cbc_done qk_done q_split k_split s_self p_self pT_self pT_evac core_done ct_split
            cn_split ksq_mm ksq_act ssum rstd_ready s_mm evac_v evac_a max_done rt_done mx_ready mb_done c_ready
            mx_raw mx_full alpha_diff max_ready alpha_ready p_shift p_exp p_hi_ready p_lo_ready pv_rh psum_add
            merged psum_scaled wv_in den_done den_in den_spread xo_done wproj_in catq_ready proj_done x1_ready
            stored""".split()
        s = {n: sem(n) for n in names}
        ct_in = [sem(f"ct_in{b}") for b in range(3)]
        cn_in = [sem(f"cn_in{b}") for b in range(3)]
        s.update({n: sem(n) for n in SECOND})
        last_tiles = [(cn_buf[0], cn_in[0], 16 * (USES[0] * (NCH - 1) + 1)), (cn_buf[1], cn_in[1], 16 * (USES[1] * (NCH - 1) + 1)),
                      (ct_buf[0], ct_in[0], 16 * (USES[0] * NCH + 1)), (ct_buf[1], ct_in[1], 16 * (USES[1] * NCH + 1)),
                      (ct_buf[2], ct_in[2], 16 * (USES[2] * NCH + 1)), (cn_buf[2], cn_in[2], 16 * (USES[2] * (NCH - 1) + 1)),
                      (cn_buf[0], cn_in[0], 16 * (USES[0] * (NCH - 1) + 2))]

        wqx = wide[:, 0:4096].rearrange("p (h n) -> p h n", h=HC)
        wq = wide[:, 4096:8192].rearrange("p (h n) -> p h n", h=HC)
        wk = wide[:, 8192:10240].rearrange("p (h n) -> p h n", h=HC)
        wv = wide[:, 10240:12288].rearrange("p (h n) -> p h n", h=HC)
        kxT = wide[:, 12288:14336].rearrange("p (h n) -> p h n", h=HC)
        kxd = wide[:, 14336:16384].rearrange("p (g n) -> p g n", g=G)
        slots = [run_max[:, D * n:D * n + D] for n in range(8)] + [cat_t[:, D * n:D * n + D] for n in range(8)] +\
            [neg_max[:, D * n:D * n + D] for n in range(4)]
        vrow = cat_t[0:S, 1024:2048]
        mean_w = neg_max[:, 512:640]
        hst = neg_max[:, 640:760]
        hm = neg_max[:, 760:780]
        hv = neg_max[:, 780:800]
        ht = neg_max[:, 800:820]
        hr = neg_max[:, 820:840]
        xn = ksq[0:S, 0, 0:256]
        qxT = o_acc[:, 0, :]
        qkw = o_acc[:, 1, :]
        qT = p_sum[:, :]
        kT = p_f[:, 0, :]
        pself = p_f[:, 1, :]
        pTs = alpha[0:S, :]
        km = stat[:, 24:40]
        xT = ct_raw[:, 0, 0:128]
        xy = ct_raw[:, 1, 0:128]
        xm = ct_raw[:, 2, 0:128]
        xb16 = cn_raw[:, 0, 0:64].bitcast(BF16)
        xe16 = cn_raw[:, 0, 64:128].bitcast(BF16)
        xq = [cn_raw[:, 1, 0:128], cn_raw[:, 1, 128:256], cn_raw[:, 2, 0:128], cn_raw[:, 2, 128:256]]

        block = ctx.enter_context(nc.Block())

        @block.sync
        def _(sp):
            sp.dma_start(x_res[:, :], t["x"]).then_inc(s["x_in"], 16)
            sp.dma_start(small[:, :], t["small"]).then_inc(s["small_in"], 16)
            sp.dma_start(wqx, t["wqx"]).then_inc(s["w_qx"], 16)
            sp.dma_start(wq, t["wq"]).then_inc(s["w_q"], 16)
            sp.dma_start(wk, t["wk"]).then_inc(s["w_k"], 16)
            sp.dma_start(kxT, t["kxT"]).then_inc(s["kxT_in"], 16)
            sp.dma_start(kxd, t["kxd"]).then_inc(s["kxd_in"], 16)
            sp.dma_start(wv, t["wv"]).then_inc(s["w_v"], 16)

            def load_t(j, i):
                if isinstance(j, int) and j == 0:
                    if i in (0, 1, 6):
                        pass
                    else:
                        sp.wait_ge(s["ct_split"], i - 1)
                else:
                    sp.wait_ge(s["ct_split"], j * CH + i - prev_use(i) + 1)
                sp.dma_start(ct_raw[:, BUF[i], :], t["ctT"][j * CH + i]).then_inc(ct_in[BUF[i]], 16)

            def load_n(j, i):
                if isinstance(j, int) and j == 0:
                    if i not in (0, 1, 6):
                        sp.wait_ge(s["cn_split"], i - 1)
                else:
                    sp.wait_ge(s["cn_split"], j * CH + i - prev_use(i) + 1)
                sp.dma_start(cn_raw[:, BUF[i], :], t["cn"][j * CH + i]).then_inc(cn_in[BUF[i]], 16)

            sp.wait_ge(s["xq_ready"], 4 * HC)
            for i in range(CH):
                load_t(0, i)
            sp.wait_ge(s["q_split"], 1)
            sp.wait_ge(s["k_split"], 2)
            sp.wait_ge(s["lin_done"], 7)
            sp.dma_start(wide[:, :], t["W_qkv"], max_dma_last_dim=8192).then_inc(s["wqkv_in"], 16)
            with sp.Fori(1, 2) as j:
                for i in range(CH):
                    load_t(j, i)
                    load_n(0, i)
            with sp.Fori(2, NCH) as j:
                for i in range(CH):
                    load_t(j, i)
                    load_n(j - 1, i)
            for i, ((raw, _, _), landed, _) in enumerate(last_tiles):
                if i in (2, 3, 4):
                    sp.wait_ge(s["ct_split"], CH * NCH)
                elif i == 6:
                    sp.wait_ge(s["cn_split"], CH * (NCH - 1) + 1)
                else:
                    sp.wait_ge(s["cn_split"], CH * (NCH - 1) + (-2, -1, 0, 0, 0, 0)[i])
                sp.dma_start(raw, t["cn"][CH * (NCH - 1) + i]).then_inc(landed, 16)
            sp.wait_ge(s["s_mm"], 2 * CH * NCH)
            sp.dma_start(mid[:, :], t["wprojT"], max_dma_last_dim=8192).then_inc(s["wproj_in"], 16)
            sp.wait_ge(s["psum_add"], 2 * (CH * (NCH - 1) + 2))
            sp.wait_ge(s["p_lo_ready"], 2 * (CH * (NCH - 1) + 2))
            sp.dma_start(wv_x, t["wvxT"]).then_inc(s["wv_in"], 16)
            second_loads(sp, s, t, ph2, wide, mid)
            sp.wait_ge(s["out_ready"], 1)
            sp.dma_start(t["out"], x_res[:, :]).then_inc(s["stored"], 16)
            sp.wait_ge(s["stored"], 16)

        @block.gpsimd
        def _(pool):
            step = Tally(s["pool_step"])
            asked = Tally(s["pow_ask"])

            def inv_root(out, in_, rows, width):
                asked.n += 1
                pool.wait_ge(s["pow_ask"], asked.n)
                pool.tensor_tensor(out, in_, cst[0:rows, 0:1].broadcast_to([rows, width]) if width > 1
                                   else cst[0:rows, 0:1], ALU.pow).then_inc(s["pow_done"], 1)

            pool.memset(cst[:, :], -0.5).then_inc(s["pool_step"], 1)
            pool.memset(eps8[:, :], 128.0 * EPS)
            pool.memset(ones[:, :], 1.0).then_inc(s["pool_step"], 1)
            pool.memset(ident[:, :], 0.0).then_inc(s["pool_step"], 1)
            pool.wait_ge(s["pool_step"], 3)
            pool.affine_select(out=ident[:, :], in_=ident[:, :], compare_op=ALU.not_equal, fill=1.0, base=0,
                               pattern=[[-1, 128]], channel_multiplier=1).then_inc(s["const_ready"], 1)
            inv_root(stat[0:S, 8:9], stat[0:S, 7:8], S, 1)
            inv_root(stat[0:S, 8:9], stat[0:S, 7:8], S, 1)
            inv_root(hr[:, 0:8], hv[:, 0:8], 128, 8)
            inv_root(hr[:, 8:20], hv[:, 8:20], 128, 12)
            pool.wait_ge(s["km_ready"], 1)
            for c in range(HC):
                kc = kxT[:, c, :].rearrange("p (g d) -> p g d", g=G)
                pool.tensor_tensor(kc, kc, km[:, G * c:G * c + G].unsqueeze(2).broadcast_to([128, G, D]), ALU.subtract)\
                    .then_inc(s["k_centred"], 1)
            for c in range(HC):
                pool.wait_ge(s["k_high"], c + 1)
                pool.tensor_tensor(k_lo[:, c, :], kxT[:, c, :], k_hi[:, c, :].bitcast(F32), ALU.subtract)\
                    .then_inc(s["k_split"], 1)

            def root(j, i):
                pool.wait_ge(s["ssum"], 2 * (j * CH + i + 1))
                if not (isinstance(j, int) and j == 0 and i == 0):
                    pool.wait_ge(s["evac_v"], j * CH + i)
                    pool.wait_ge(s["evac_a"], j * CH + i)
                pool.tensor_tensor(ss[:, :], ss[:, :], eps8[:, :], ALU.add).then_inc(s["ss_eps"], 1)
                pool.wait_ge(s["ss_eps"], j * CH + i + 1)
                pool.tensor_tensor(rstd1[:, :], ss[:, :], cst[:, :], ALU.pow).then_inc(s["rstd_ready"], 1)

            def shift(j, i):
                if i == 0:
                    pool.wait_ge(s["max_ready"], j + 1)
                for h in range(2):
                    if not (isinstance(j, int) and j == 0 and i == 0):
                        pool.wait_ge(s["psum_add"], 2 * (j * CH + i) + h - 1)
                        pool.wait_ge(s["p_lo_ready"], 2 * (j * CH + i) + h - 1)
                    pool.tensor_tensor(p_f[:, h, :], scores[:, i, 512 * h:512 * h + 512],
                                       neg_max[:, 512 * h:512 * h + 512], ALU.add).then_inc(s["p_shift"], 1)

            def add_p(j, i, h, probs):
                pool.wait_ge(s["p_exp"], 2 * (j * CH + i) + h + 1)
                if i == 0:
                    pool.wait_ge(s["psum_scaled"], j + 1)
                else:
                    pool.wait_ge(s["psum_add"], 2 * (j * CH + i) - 1 + h)
                cols = p_sum[:, 512 * h:512 * h + 512]
                pool.tensor_tensor(cols, cols, probs, ALU.add).then_inc(s["psum_add"], 1)

            pool.wait_ge(s["headT_done"], 3)
            pool.wait_ge(s["qmean_done"], 1)
            pool.memset(neg_max[:, :], 1e30).then_inc(s["softmax_init"], 1)
            pool.wait_ge(s["cbc_done"], 1)
            pool.memset(o_acc[:, :, :], 0.0).then_inc(s["softmax_init"], 1)
            for i in range(CH):
                root(0, i)
                if i == 1:
                    pool.wait_ge(s["s_self"], 1)
                    pool.memset(p_sum[:, :], 0.0).then_inc(s["softmax_init"], 1)

            def pool_chunk(j, k):
                for i in range(CH):
                    shift(k, i)
                    root(j, i)
                    for h in range(2):
                        add_p(k, i, h, p_f[:, h, :])

            pool_chunk(1, 0)
            with pool.Fori(2, NCH) as j:
                pool_chunk(j, j - 1)
            for i in range(CH):
                for h in range(2):
                    add_p(NCH - 1, i, h, scores[:, i, 512 * h:512 * h + 512])
            second_pool(pool, s, ph2, inv_root, ident, cst, small)

        @block.scalar
        def _(act):
            act.wait_ge(s["small_in"], 16)
            n = 0
            for name, dst in (("wqx_s", run_max[:, 0:1024]), ("wq_s", cat_t[:, 0:1024]), ("wk_s", neg_max[:, 0:512]),
                              ("wv_s", vrow)):
                if name == "wv_s":
                    act.wait_ge(s["headT_done"], 1)
                    for k in range(2):
                        act.activation(qxT[:, 512 * k:512 * k + 512], bank[k], ACT.Identity, scale=sm("qxln_w"),
                                       bias=sm("qxln_b")).then_inc(s["heads_out"], 1)
                    for c in range(HC):
                        act.wait_ge(s["k_centred"], c + 1)
                        act.copy(k_hi[:, c, :], kxT[:, c, :]).then_inc(s["k_high"], 1)
                    act.wait_ge(s["headT_done"], 2)
                    for k in range(2):
                        act.activation(qT[:, 512 * k:512 * k + 512], bank[6 + k], ACT.Identity, scale=sm("qln_w"),
                                       bias=sm("qln_b")).then_inc(s["heads_out"], 1)
                    act.wait_ge(s["headT_done"], 3)
                    act.activation(kT, bank[4], ACT.Identity, scale=sm("kln_w"), bias=sm("kln_b")).then_inc(s["heads_out"], 1)
                    act.wait_ge(s["qk_done"], 1)
                    for c in range(HC):
                        act.copy(q_hi[:, c, :], po[:, 2 * c:2 * c + 2, :].rearrange("p b n -> p (b n)")).then_inc(s["heads_out"], 1)
                rows = dst.shape[0]
                for k in range(dst.shape[1] // 512):
                    act.wait_ge(s["lin_done"], n + 1)
                    act.activation(dst[:, 512 * k:512 * k + 512], bank[LIN_BANK[n]][0:rows, :], ACT.Identity,
                                   scale=sm(name, rows)).then_inc(s["lin_evac"], 1)
                    n += 1

            def high(j, i, half, raw, hi, landed, used):
                b = BUF[i]
                act.wait_ge(landed[b], 16 * (buf_use(j, i) + 1))
                if not (isinstance(j, int) and j == 0 and i in (0, 1, 6)):
                    act.wait_ge(used, 2 * (j * CH + i - prev_use(i) + 1))
                act.activation(hi[:, b, :], raw[:, b, :], ACT.Identity).then_inc(half, 1)

            def high_t(j, i):
                high(j, i, s["ct_half"], ct_raw, ct_hi, ct_in, s["s_mm"])

            def high_n(j, i):
                high(j, i, s["cn_half"], cn_raw, cn_hi, cn_in, s["pv_rh"])

            def square(j, i):
                for n in range(2):
                    act.wait_ge(s["ksq_mm"], 2 * (j * CH + i) + n + 1)
                    if not (isinstance(j, int) and j == 0 and i == 0):
                        act.wait_ge(s["ssum"], 2 * (j * CH + i) + n - 1)
                    act.activation(ksq[:, n, :], pk[:, n, :], ACT.Square).then_inc(s["ksq_act"], 1)

            def probs(j, i, h, p, hi, used):
                act.wait_ge(s["p_shift"], 2 * (j * CH + i) + h + 1)
                act.activation(p, p, ACT.Exp).then_inc(s["p_exp"], 1)
                act.wait_ge(s["p_exp"], 2 * (j * CH + i) + h + 1)
                if used is not None:
                    act.wait_ge(s["pv_rh"], used)
                act.copy(hi, p).then_inc(s["p_hi_ready"], 1)

            def evacuate(j, i):
                act.wait_ge(s["rstd_ready"], j * CH + i + 1)
                if not (isinstance(j, int) and j == 0):
                    act.wait_ge(s["p_shift"], 2 * (j * CH + i + 1 - CH))
                act.wait_ge(s["s_mm"], 2 * (j * CH + i) + 2)
                for g in range(4, G):
                    ins = act.activation(scores[:, i, ROWS * g:ROWS * g + ROWS], ps[:, 1, ROWS * (g - 4):ROWS * (g - 3)],
                                         ACT.Identity, scale=rstd1[:, g:g + 1])
                ins.then_inc(s["evac_a"], 1)

            def rescale(j):
                act.wait_ge(s["alpha_diff"], j + 1)
                act.activation(alpha[:, :], alpha[:, :], ACT.Exp).then_inc(s["alpha_ready"], 1)

            high_t(0, 0)
            high_t(0, 1)
            square(0, 0)
            for i in range(CH):
                evacuate(0, i)
                for tile in ahead(0, i, 1, False):
                    square(*tile)
                for tile in ahead(0, i, 2, False):
                    high_t(*tile)
                if i == 0:
                    act.wait_ge(s["s_self"], 2)
                    act.activation(pself, pself, ACT.Exp, scale=float(D) ** -0.5).then_inc(s["p_self"], 1)
            rescale(0)

            def act_chunk(j, k, last=False):
                for i in range(CH):
                    high_n(k, i)
                    first = isinstance(k, int) and k == 0 and i == 0
                    probs(k, i, 0, p_f[:, 0, :], p_hi[:, 0, :], None if first else 2 * (k * CH + i) - 1)
                    probs(k, i, 1, p_f[:, 1, :], p_hi[:, 1, :], None if first else 2 * (k * CH + i))
                    evacuate(j, i)
                    for tile in ahead(j, i, 1, last):
                        square(*tile)
                    for tile in ahead(j, i, 2, last):
                        high_t(*tile)
                rescale(j)

            act_chunk(1, 0)
            with act.Fori(2, NCH - 1) as j:
                act_chunk(j, j - 1)
            act_chunk(NCH - 1, NCH - 2, last=True)
            for i, ((raw, hi, _), landed, count) in enumerate(last_tiles):
                act.wait_ge(landed, count)
                if i in (2, 3, 4):
                    act.wait_ge(s["s_mm"], 2 * CH * NCH)
                else:
                    act.wait_ge(s["pv_rh"], 2 * (CH * (NCH - 1) + (-2, -1, 0, 0, 0, 0, 1)[i]))
                act.activation(hi, raw, ACT.Identity).then_inc(s["cn_half"], 1)
                for h in range(2):
                    n = 2 * (CH * (NCH - 1) + i) + h
                    probs(NCH - 1, i, h, scores[:, i, 512 * h:512 * h + 512], last_hi[i % 2][:, h, :],
                          (n - 1, None)[i] if i < 2 else n - 3)
            second_scalar(act, s, ph2, bank, small)

        @block.vector
        def _(dve):
            v = Tally(s["dve_step"])
            asked = Tally(s["pow_ask"])
            normed = Tally(s["normed"])

            def ask_root(ins):
                asked.by(ins)
                dve.wait_ge(s["pow_done"], asked.n)

            def layernorm_rows(dst, src):
                v.settle(dve, dve.bn_stats(stat[0:S, 0:6], src))
                v.settle(dve, dve.bn_aggr(stat[0:S, 6:8], stat[0:S, 0:6]))
                ask_root(dve.tensor_scalar(stat[0:S, 7:8], stat[0:S, 7:8], EPS, None, ALU.add))
                dve.tensor_scalar(dst, src, stat[0:S, 6:7], stat[0:S, 8:9], ALU.subtract, ALU.mult)\
                   .then_inc(s["normed"], 1)
                normed.n += 1
                dve.wait_ge(s["normed"], normed.n)

            def fp8_round(out, y, b16, e16, mag, ready=None):
                v.settle(dve, dve.tensor_scalar(b16, y, FP8_MAX, -FP8_MAX, ALU.min, ALU.max))
                v.settle(dve, dve.tensor_scalar(e16.bitcast(U16), b16.bitcast(U16), 0x7F80, None, ALU.bitwise_and))
                v.settle(dve, dve.tensor_scalar(mag, e16, 2.0 ** -6, 1.5 * 2.0 ** 20, ALU.max, ALU.mult))
                v.settle(dve, dve.tensor_tensor(out, b16, mag, ALU.add))
                ins = dve.tensor_tensor(out, out, mag, ALU.subtract)
                if ready is None:
                    v.settle(dve, ins)
                else:
                    ins.then_inc(ready, 1)

            dve.wait_ge(s["x_in"], 16)
            dve.wait_ge(s["const_ready"], 1)
            layernorm_rows(xn, x_res[:, :])
            layernorm_rows(xn, xn)
            dve.wait_ge(s["small_in"], 16)
            dve.wait_ge(s["xT_done"], 1)
            xT2 = xT.rearrange("p (h t) -> p h t", h=HC)
            for c in range(HC):
                v.settle(dve, dve.tensor_scalar(xT2[:, c, :], bank[0][:, c * S:c * S + S], sm("ln_w", k=c),
                                                sm("ln_b", k=c), ALU.mult, ALU.add))
            inv_in = stat[:, 16:24]
            a = SMALL["qx_in"][0]
            v.settle(dve, dve.reciprocal(inv_in, small[:, a:a + 8]))
            for n in range(4):
                for c in range(HC):
                    v.settle(dve, dve.tensor_scalar(xy[:, c * S:c * S + S], xT2[:, c, :],
                                                    inv_in[:, 2 * n + c:2 * n + c + 1], None, ALU.mult))
                fp8_round(xq[n], xy, xb16, xe16, xm)
                for c in range(HC):
                    col = xq[n][:, c * S:c * S + S]
                    dve.tensor_scalar(col, col, small[:, a + 2 * n + c:a + 2 * n + c + 1], None, ALU.mult)\
                       .then_inc(s["xq_ready"], 1)
            v.by(dve.tensor_scalar(mean_w, ones[:, :], 1.0 / D, None, ALU.mult))
            v.by(dve.reciprocal(smooth_inv[:, :], sm("smooth")))
            v.by(dve.tensor_tensor(fold[:, :], ident[:, 0:S], ident[:, S:2 * S], ALU.add))

            def statistics(first, count):
                for n in range(first, first + count):
                    v.by(dve.bn_stats(hst[:, 6 * n:6 * n + 6], slots[n]))

            def moments(first, count):
                c = slice(first, first + count)
                dve.wait_ge(s["dve_step"], v.n)
                st = hst.rearrange("p (h k) -> p h k", k=6)[:, c]
                v.by(dve.tensor_tensor(hm[:, c], st[:, :, 1], st[:, :, 4], ALU.add))
                v.by(dve.tensor_tensor(ht[:, c], st[:, :, 1], st[:, :, 4], ALU.subtract))
                v.settle(dve, dve.tensor_tensor(hv[:, c], st[:, :, 2], st[:, :, 5], ALU.add))
                v.by(dve.tensor_scalar(hm[:, c], hm[:, c], 0.5, None, ALU.mult))
                v.by(dve.tensor_scalar(hv[:, c], hv[:, c], 1.0 / D, EPS, ALU.mult, ALU.add))
                v.settle(dve, dve.scalar_tensor_tensor(ht[:, c], ht[:, c], 0.25, ht[:, c], ALU.mult, ALU.mult))
                return asked.by(dve.tensor_tensor(hv[:, c], hv[:, c], ht[:, c], ALU.add))

            def normalise(first, count, root):
                dve.wait_ge(s["pow_done"], root)
                for n in range(first, first + count):
                    dve.tensor_scalar(slots[n], slots[n], hm[:, n:n + 1], hr[:, n:n + 1], ALU.subtract, ALU.mult)\
                       .then_inc(s["heads_ready"], 1)

            dve.wait_ge(s["lin_evac"], 2)
            statistics(0, 8)
            root_qx = moments(0, 8)
            dve.wait_ge(s["lin_evac"], 4)
            statistics(8, 8)
            normalise(0, 8, root_qx)
            dve.wait_ge(s["lin_evac"], 5)
            statistics(16, 4)
            root_qk = moments(8, 12)
            dve.wait_ge(s["kxT_in"], 16)
            v.settle(dve, dve.tensor_reduce(km, kxT.rearrange("p h (g d) -> p (h g) d", g=G), X, ALU.add))
            dve.tensor_scalar(km, km, 1.0 / D, None, ALU.mult).then_inc(s["km_ready"], 1)
            dve.wait_ge(s["heads_out"], 2)
            dve.tensor_scalar(qkw, qxT, sm("kxln_w"), None, ALU.mult).then_inc(s["qkT_ready"], 1)
            normalise(8, 12, root_qk)
            dve.wait_ge(s["qkT_ready"], 1)
            dve.wait_ge(s["qmean_done"], 1)
            for n in range(2):
                dve.tensor_tensor(qkw[:, 512 * n:512 * n + 512], qkw[:, 512 * n:512 * n + 512], bank[n],
                                  ALU.subtract).then_inc(s["qc_ready"], 1)
            for c in range(HC):
                dve.wait_ge(s["heads_out"], 5 + c + 1)
                ins = dve.tensor_tensor(q_lo[:, c, :], po[:, 2 * c:2 * c + 2, :].rearrange("p b n -> p (b n)"),
                                        q_hi[:, c, :].bitcast(F32), ALU.subtract)
            ins.then_inc(s["q_split"], 1)
            dve.wait_ge(s["cbc_done"], 1)
            dve.tensor_scalar(c_col[:, :], bank[5][:, 0:G], float(D) ** -0.5, None, ALU.mult).then_inc(s["c_ready"], 1)

            def self_attention(step):
                pg = pself.rearrange("p (g t) -> p g t", g=G)
                if step == 0:
                    dve.wait_ge(s["s_self"], 1)
                    sg = bank[0].rearrange("p (g t) -> p g t", g=G)
                    v.settle(dve, dve.tensor_reduce(stat[:, 40:48], sg, X, ALU.max))
                    dve.tensor_tensor(pg, sg, stat[:, 40:48].unsqueeze(2).broadcast_to([128, G, S]), ALU.subtract)\
                       .then_inc(s["s_self"], 1)
                elif step == 1:
                    dve.wait_ge(s["p_self"], 1)
                    v.settle(dve, dve.tensor_reduce(stat[:, 48:56], pg, X, ALU.add))
                    v.settle(dve, dve.reciprocal(stat[:, 48:56], stat[:, 48:56]))
                    dve.tensor_tensor(pg, pg, stat[:, 48:56].unsqueeze(2).broadcast_to([128, G, S]), ALU.mult)\
                       .then_inc(s["p_self"], 1)
                elif step == 2:
                    dve.wait_ge(s["pT_self"], 1)
                    dve.tensor_copy(pTs.rearrange("p (b n) -> p b n", b=2), po[0:S, 2:4, :]).then_inc(s["pT_evac"], 1)
                elif step == 3:
                    dve.wait_ge(s["core_done"], 1)
                    v.settle(dve, dve.tensor_tensor(
                        cat_t[:, 0:1024].rearrange("p (h t) -> p h t", t=S), po[:, 0:2, :].rearrange("p b (h t) -> p (b h) t", t=S),
                        smooth_inv[:, 0:16].unsqueeze(2).broadcast_to([128, 16, S]), ALU.mult))
                elif step <= 5:
                    q = cat_t[:, 512 * (step - 4):512 * (step - 4) + 512]
                    fp8_round(q, q, alpha[:, 0:256].bitcast(BF16), alpha[:, 256:512].bitcast(BF16), p_f[:, 0, :],
                              s["catq_ready"])

            def low_t(j, i):
                b = BUF[i]
                dve.wait_ge(s["ct_half"], j * CH + i + 1)
                dve.tensor_tensor(ct_lo[:, b, :], ct_raw[:, b, :], ct_hi[:, b, :].bitcast(F32),
                                  ALU.subtract).then_inc(s["ct_split"], 1)

            def low_n(j, i):
                b = BUF[i]
                dve.wait_ge(s["cn_half"], j * CH + i + 1)
                dve.tensor_tensor(cn_lo[:, b, :], cn_raw[:, b, :], cn_hi[:, b, :].bitcast(F32),
                                  ALU.subtract).then_inc(s["cn_split"], 1)

            def low_p(j, i, h, probs, hi=p_hi, lo=p_lo):
                dve.wait_ge(s["p_hi_ready"], 2 * (j * CH + i) + h + 1)
                dve.tensor_tensor(lo[:, h, :], probs, hi[:, h, :].bitcast(F32),
                                  ALU.subtract).then_inc(s["p_lo_ready"], 1)

            def sums(j, i):
                for n in range(2):
                    dve.wait_ge(s["ksq_act"], 2 * (j * CH + i) + n + 1)
                    if not (isinstance(j, int) and j == 0 and i == 0):
                        dve.wait_ge(s["rstd_ready"], j * CH + i)
                    dve.tensor_reduce(ss[:, 4 * n:4 * n + 4], ksq[:, n, :].rearrange("p (g d) -> p g d", g=4),
                                      X, ALU.add).then_inc(s["ssum"], 1)

            def evacuate(j, i):
                dve.wait_ge(s["rstd_ready"], j * CH + i + 1)
                if not (isinstance(j, int) and j == 0):
                    dve.wait_ge(s["p_shift"], 2 * (j * CH + i + 1 - CH))
                dve.wait_ge(s["s_mm"], 2 * (j * CH + i) + 1)
                for g in range(4):
                    ins = dve.tensor_scalar(scores[:, i, ROWS * g:ROWS * g + ROWS], ps[:, 0, ROWS * g:ROWS * g + ROWS],
                                            rstd1[:, g:g + 1], None, ALU.mult)
                ins.then_inc(s["evac_v"], 1)

            def row_max(j, i):
                dve.wait_ge(s["evac_v"], j * CH + i + 1)
                dve.wait_ge(s["evac_a"], j * CH + i + 1)
                if i > 1:
                    dve.wait_ge(s["max_done"], j * (CH - 1) + i - 1)
                dve.tensor_tensor(run_max[:, :], scores[:, 0, :] if i == 1 else run_max[:, :], scores[:, i, :],
                                  ALU.max).then_inc(s["max_done"], 1)

            def scale_out(k):
                dve.wait_ge(s["alpha_ready"], k + 1)
                dve.wait_ge(s["merged"], HC * k)
                for c in range(HC):
                    dve.scalar_tensor_tensor(out=o_acc[:, c, :], in0=alpha[:, :], scalar=1.0, in1=o_acc[:, c, :],
                                             op0=ALU.min, op1=ALU.mult).then_inc(s["o_scaled"], 1)

            def merge(k):
                dve.wait_ge(s["pv_rh"], 2 * CH * (k + 1))
                if not (isinstance(k, int) and k == 0):
                    dve.wait_ge(s["o_scaled"], HC * k)
                for c in range(HC):
                    dve.tensor_tensor(o_acc[:, c, :], o_acc[:, c, :],
                                      po[:, 2 * c:2 * c + 2, :].rearrange("p b n -> p (b n)"),
                                      ALU.add).then_inc(s["merged"], 1)

            def maxima(j, k, then=None):
                dve.wait_ge(s["rt_done"], j + 1)
                dve.tensor_reduce(mx[:, :], ps.rearrange("p b (g r) -> p (b g) r", g=4), X, ALU.max)\
                   .then_inc(s["mx_raw"], 1)
                dve.wait_ge(s["mx_raw"], j + 1)
                dve.tensor_tensor(mx[:, :], mx[:, :], c_col[:, :], ALU.add).then_inc(s["mx_full"], 1)
                dve.wait_ge(s["mx_full"], j + 1)
                dve.tensor_tensor(mx[:, :], c_col[:, :], mx[:, :], ALU.subtract).then_inc(s["mx_ready"], 1)
                new = pk.rearrange("p b n -> p (b n)")
                if k is not None:
                    dve.wait_ge(s["psum_add"], 2 * CH * (k + 1))
                    dve.wait_ge(s["psum_scaled"], k + 1)
                    if not (isinstance(k, int) and k == 0):
                        dve.wait_ge(s["o_scaled"], HC * k)
                dve.wait_ge(s["mb_done"], j + 1)
                dve.tensor_tensor(alpha[:, :], new, neg_max[:, :], ALU.subtract).then_inc(s["alpha_diff"], 1)
                dve.wait_ge(s["alpha_diff"], j + 1)
                dve.tensor_tensor(neg_max[:, :], neg_max[:, :], new, ALU.min).then_inc(s["max_ready"], 1)
                if then is not None:
                    dve.wait_ge(s["max_ready"], j + 1)
                    then()
                if k is not None:
                    merge(k)

            def scale_sum(j):
                dve.wait_ge(s["alpha_ready"], j + 1)
                dve.scalar_tensor_tensor(out=p_sum[:, :], in0=alpha[:, :], scalar=1.0, in1=p_sum[:, :],
                                         op0=ALU.min, op1=ALU.mult).then_inc(s["psum_scaled"], 1)

            def shift_last(i):
                for h in range(2):
                    q = scores[:, i, 512 * h:512 * h + 512]
                    dve.tensor_tensor(q, q, neg_max[:, 512 * h:512 * h + 512], ALU.add).then_inc(s["p_shift"], 1)

            low_t(0, 0)
            low_t(0, 1)
            sums(0, 0)
            for i in range(CH):
                evacuate(0, i)
                if i:
                    row_max(0, i)
                for tile in ahead(0, i, 1, False):
                    sums(*tile)
                for tile in ahead(0, i, 2, False):
                    low_t(*tile)
                self_attention(i)
            dve.wait_ge(s["softmax_init"], 3)
            maxima(0, None)

            def dve_chunk(j, k, last=False):
                for i in range(CH):
                    low_n(k, i)
                    low_p(k, i, 0, p_f[:, 0, :])
                    if i == 0:
                        scale_sum(k)
                    low_p(k, i, 1, p_f[:, 1, :])
                    evacuate(j, i)
                    if i:
                        row_max(j, i)
                    for tile in ahead(j, i, 1, last):
                        sums(*tile)
                    for tile in ahead(j, i, 2, last):
                        low_t(*tile)
                    if i == 1 and not (isinstance(k, int) and k == 0):
                        scale_out(k)
                maxima(j, k, (lambda: shift_last(0)) if last else None)

            dve_chunk(1, 0)
            with dve.Fori(2, NCH - 1) as j:
                dve_chunk(j, j - 1)
            dve_chunk(NCH - 1, NCH - 2, last=True)

            for i in range(CH):
                if 0 < i < CH - 1:
                    shift_last(i + 1)
                (raw, hi, lo), _, _ = last_tiles[i]
                dve.wait_ge(s["cn_half"], CH * (NCH - 1) + i + 1)
                dve.tensor_tensor(lo, raw, hi.bitcast(F32), ALU.subtract).then_inc(s["cn_split"], 1)
                for h in range(2):
                    low_p(NCH - 1, i, h, scores[:, i, 512 * h:512 * h + 512], last_hi[i % 2], last_lo[i % 2])
                if i == 0:
                    shift_last(1)
                    scale_sum(NCH - 1)
                if i == 2:
                    scale_out(NCH - 1)
            dve.wait_ge(s["den_done"], 1)
            dve.reciprocal(mx[:, :], pk[:, 0, 0:G]).then_inc(s["den_in"], 1)
            merge(NCH - 1)
            cx = cat_t[:, 1024:2048]
            dve.wait_ge(s["den_spread"], 1)
            v.settle(dve, dve.tensor_tensor(neg_max.rearrange("p (h t) -> p h t", t=S), pk.rearrange("p b (h t) -> p (b h) t", t=S),
                                            smooth_inv[:, 16:32].unsqueeze(2).broadcast_to([128, 16, S]), ALU.mult))
            dve.wait_ge(s["xo_done"], 1)
            v.settle(dve, dve.tensor_tensor(cx, ps.rearrange("p b n -> p (b n)"), neg_max[:, :], ALU.mult))
            for n in range(2):
                q = cx[:, 512 * n:512 * n + 512]
                fp8_round(q, q, scores[:, 3, 0:256].bitcast(BF16), scores[:, 3, 256:512].bitcast(BF16),
                          scores[:, 4, 0:512], s["catq_ready"])
            v.settle(dve, dve.tensor_scalar(stat[0:S, 40:41], sm("pw_s", S), sm("pin_s", S), None, ALU.mult))
            dve.wait_ge(s["proj_done"], 1)
            dve.tensor_copy(half, bank[0][:, 0:H]).then_inc(s["half_in"], 1)
            dve.wait_ge(s["fold_done"], 1)
            dve.scalar_tensor_tensor(out=x_res[:, :], in0=bank[1][0:S, 0:H], scalar=stat[0:S, 40:41],
                                     in1=x_res[:, :], op0=ALU.mult, op1=ALU.add).then_inc(s["x1_ready"], 1)
            dve.wait_ge(s["x1_ready"], 1)
            second_vector(dve, s, ph2, v, layernorm_rows, bank, small, x_res, ident)

        @block.tensor
        def _(pe):
            pe.wait_ge(s["const_ready"], 1)
            pe.wait_ge(s["normed"], 2)
            for c in range(HC):
                ins = pe.transpose(bank[0][:, c * S:c * S + S], xn[:, 128 * c:128 * c + 128], ident[0:S, 0:S])
            ins.then_inc(s["xT_done"], 1)
            def latents(k, w, key, first, count):
                pe.wait_ge(s["xq_ready"], HC * (k + 1))
                pe.wait_ge(s[key], 16)
                w5 = w.rearrange("p h (n e d) -> p h n e d", e=2, d=D)
                for b in range(count):
                    out = bank[LIN_BANK[first + b]].rearrange("p (n d) -> p n d", d=D)
                    for c in range(HC):
                        for e, r in enumerate(HALVES):
                            ins = pe.matmul(out[r], xq[k][:, c * S:c * S + S], w5[:, c, 4 * b:4 * b + 4, e],
                                            start=(c == 0), stop=(c == HC - 1))
                    ins.then_inc(s["lin_done"], 1)

            def turn_heads(first, count):
                for n in range(first, first + count):
                    pe.wait_ge(s["heads_ready"], n + 1)
                    ins = pe.transpose(bank[TURN_BANK[n // 4]][:, D * (n % 4):D * (n % 4) + D], slots[n], ident[:, :])
                ins.then_inc(s["headT_done"], 1)

            latents(0, wqx, "w_qx", 0, 2)
            latents(1, wq, "w_q", 2, 2)
            latents(2, wk, "w_k", 4, 1)
            turn_heads(0, 8)
            pe.wait_ge(s["qkT_ready"], 1)
            for b in range(2):
                ins = pe.matmul(bank[b], mean_w, qkw[:, 512 * b:512 * b + 512], start=True, stop=True)
            ins.then_inc(s["qmean_done"], 1)
            turn_heads(8, 8)
            turn_heads(16, 4)
            pe.wait_ge(s["qc_ready"], 2)
            pe.wait_ge(s["kxd_in"], 16)
            for c in range(HC):
                for g in range(G):
                    ins = pe.matmul(po[:, 2 * c + g // 4, ROWS * (g % 4):ROWS * (g % 4) + ROWS],
                                    kxd[:, g, 128 * c:128 * c + 128], qkw[:, ROWS * g:ROWS * g + ROWS],
                                    start=True, stop=True)
            ins.then_inc(s["qk_done"], 1)
            for g in range(G):
                ins = pe.matmul(bank[5][:, g:g + 1], qxT[:, ROWS * g:ROWS * g + ROWS], sm("kxln_b"), start=True, stop=True)
            ins.then_inc(s["cbc_done"], 1)
            pe.wait_ge(s["heads_out"], 4)
            pe.wait_ge(s["xq_ready"], HC * 4)
            pe.wait_ge(s["w_v"], 16)
            for b in range(2):
                for c in range(HC):
                    ins = pe.matmul(bank[LIN_BANK[5 + b]][0:S, :], xq[3][:, c * S:c * S + S], wv[:, c, 512 * b:512 * b + 512],
                                    start=(c == 0), stop=(c == HC - 1))
                ins.then_inc(s["lin_done"], 1)
            pe.wait_ge(s["q_split"], 1)
            pe.wait_ge(s["k_split"], 2)
            pe.wait_ge(s["c_ready"], 1)
            pe.wait_ge(s["lin_evac"], 7)

            def self_attention(step):
                if step == 0:
                    pe.wait_ge(s["heads_out"], 5)
                    for g in range(G):
                        ins = pe.matmul(bank[0][:, S * g:S * g + S], qT[:, ROWS * g:ROWS * g + ROWS],
                                        kT[:, S * g:S * g + S], start=True, stop=True)
                    ins.then_inc(s["s_self"], 1)
                elif step == 2:
                    pe.wait_ge(s["p_self"], 2)
                    for g in range(G):
                        ins = pe.transpose(po[0:S, 2 + g // 4, ROWS * (g % 4):ROWS * (g % 4) + ROWS],
                                           pself[:, S * g:S * g + S], ident[:, :])
                    ins.then_inc(s["pT_self"], 1)
                elif step == 3:
                    pe.wait_ge(s["pT_evac"], 1)
                    for g in range(G):
                        ins = pe.matmul(po[:, g // 4, ROWS * (g % 4):ROWS * (g % 4) + ROWS], vrow[:, D * g:D * g + D],
                                        pTs[:, ROWS * g:ROWS * g + ROWS], start=True, stop=True)
                    ins.then_inc(s["core_done"], 1)

            def product(out, lo_hi, w_hi, w_lo, b, n):
                hi, lo = lo_hi
                k = 0
                for c in range(HC):
                    st = hi[:, b, 128 * c:128 * c + 128]
                    for w in (w_hi, w_lo):
                        pe.matmul(out, st, w[:, c, 512 * n:512 * n + 512], start=(k == 0), stop=False)
                        k += 1
                for c in range(HC):
                    ins = pe.matmul(out, lo[:, b, 128 * c:128 * c + 128], w_hi[:, c, 512 * n:512 * n + 512],
                                    start=False, stop=(c == HC - 1))
                return ins

            def keys(j, i):
                pe.wait_ge(s["ct_split"], j * CH + i + 1)
                for n in range(2):
                    if not (isinstance(j, int) and j == 0 and i == 0):
                        pe.wait_ge(s["ksq_act"], 2 * (j * CH + i) + n - 1)
                    if i == 1 and not (isinstance(j, int) and j == 0):
                        pe.wait_ge(s["max_ready"], j)
                    product(pk[:, n, :], (ct_hi, ct_lo), k_hi, k_lo, BUF[i], n).then_inc(s["ksq_mm"], 1)

            def raw_scores(j, i):
                for n in range(2):
                    if not (isinstance(j, int) and j == 0 and i == 0):
                        pe.wait_ge(s["evac_a" if n else "evac_v"], j * CH + i)
                        if i == 0:
                            pe.wait_ge(s["mx_raw"], j)
                    product(ps[:, n, :], (ct_hi, ct_lo), q_hi, q_lo, BUF[i], n).then_inc(s["s_mm"], 1)

            def weighted(j, i, ctx_hi, ctx_lo, hi=p_hi, lo=p_lo, between=None):
                pe.wait_ge(s["cn_split"], j * CH + i + 1)
                if i == 0 and not (isinstance(j, int) and j == 0):
                    pe.wait_ge(s["merged"], HC * j)
                for h in range(2):
                    if h and between is not None:
                        between(j + 1)
                    pe.wait_ge(s["p_lo_ready"], 2 * (j * CH + i) + h + 1)
                    for c in range(HC):
                        out = po[:, 2 * c + h, :]
                        st = ctx_hi[:, 128 * c:128 * c + 128]
                        pe.matmul(out, st, hi[:, h, :], start=(i == 0), stop=False)
                        pe.matmul(out, st, lo[:, h, :], start=False, stop=False)
                        ins = pe.matmul(out, ctx_lo[:, 128 * c:128 * c + 128], hi[:, h, :],
                                        start=False, stop=(i == CH - 1))
                    ins.then_inc(s["pv_rh"], 1)

            def turn_max(j):
                pe.wait_ge(s["max_done"], (CH - 1) * (j + 1))
                for g in range(G):
                    ins = pe.transpose(ps[:, g // 4, ROWS * (g % 4):ROWS * (g % 4) + ROWS],
                                       run_max[:, ROWS * g:ROWS * g + ROWS], ident[:, :])
                ins.then_inc(s["rt_done"], 1)

            def spread_max(j, keys_made):
                pe.wait_ge(s["mx_ready"], j + 1)
                pe.wait_ge(s["ksq_act"], 2 * keys_made)
                for g in range(G):
                    ins = pe.transpose(pk[:, g // 4, ROWS * (g % 4):ROWS * (g % 4) + ROWS],
                                       mx[:, g:g + 1].broadcast_to([128, 128]), ident[:, :])
                ins.then_inc(s["mb_done"], 1)

            keys(0, 0)
            for i in range(CH):
                raw_scores(0, i)
                for tile in ahead(0, i, 1, False):
                    keys(*tile)
                self_attention(i)
            turn_max(0)
            spread_max(0, CH + 1)

            def pe_chunk(j, k, last=False):
                for i in range(CH):
                    raw_scores(j, i)
                    for tile in ahead(j, i, 1, last):
                        keys(*tile)
                    weighted(k, i, cn_hi[:, BUF[i], :], cn_lo[:, BUF[i], :], between=turn_max if i == CH - 1 else None)
                spread_max(j, CH * (j + 1) + (0 if last else 1))

            pe_chunk(1, 0)
            with pe.Fori(2, NCH - 1) as j:
                pe_chunk(j, j - 1)
            pe_chunk(NCH - 1, NCH - 2, last=True)
            for i in range(CH):
                weighted(NCH - 1, i, *last_tiles[i][0][1:], last_hi[i % 2], last_lo[i % 2])
            pe.wait_ge(s["psum_add"], 2 * CH * NCH)
            for g in range(G):
                ins = pe.matmul(pk[:, 0, g:g + 1], p_sum[:, ROWS * g:ROWS * g + ROWS], ones[:, 0:1], start=True, stop=True)
            ins.then_inc(s["den_done"], 1)
            pe.wait_ge(s["den_in"], 1)
            for g in range(G):
                ins = pe.transpose(pk[:, g // 4, ROWS * (g % 4):ROWS * (g % 4) + ROWS],
                                   mx[:, g:g + 1].broadcast_to([128, 128]), ident[:, :])
            ins.then_inc(s["den_spread"], 1)
            pe.wait_ge(s["merged"], HC * NCH)
            pe.wait_ge(s["wv_in"], 16)
            for g in range(G):
                for c in range(HC):
                    ins = pe.matmul(ps[:, g // 4, ROWS * (g % 4):ROWS * (g % 4) + ROWS],
                                    wv_x[:, c, D * g:D * g + D], o_acc[:, c, ROWS * g:ROWS * g + ROWS],
                                    start=(c == 0), stop=(c == HC - 1))
            ins.then_inc(s["xo_done"], 1)
            pe.wait_ge(s["wproj_in"], 16)
            for k in range(32):
                pe.wait_ge(s["catq_ready"], k // 8 + 1)
                r = HALVES[k % 2]
                ins = pe.matmul(bank[0][r, 0:H], cat_t[:, S * k:S * k + S], mid[:, H * k:H * k + H],
                                start=(k < 2), stop=(k >= 30))
            ins.then_inc(s["proj_done"], 1)
            pe.wait_ge(s["half_in"], 1)
            pe.matmul(bank[1][0:S, 0:H], fold[:, :], half, start=True, stop=True).then_inc(s["fold_done"], 1)
            second_tensor(pe, s, ph2, bank, small, ident, ones, wide, mid)


def second_memory(m, sb):
    area = sb("area", [128, 27000])

    def at(a, n, rows=128):
        return area[0:rows, a:a + n]

    m["raw"] = at(0, 4288).rearrange("p (c t) -> p c t", t=S + 3)
    m["cv"] = at(4288, 4096)
    m["tok"] = at(8384, 1024).rearrange("p (b n) -> p b n", b=2)
    m["bv"] = at(9408, 2048)
    m["yo"] = at(9408, 2048)
    m["tap0"] = at(11456, 1024).rearrange("p (b n) -> p b n", b=2)
    m["tap1"] = at(12480, 1024).rearrange("p (b n) -> p b n", b=2)
    m["u"] = at(11456, 2048)
    m["tap2"] = at(13504, 512)
    m["sq"] = at(14016, 2048)
    m["zs"] = at(16064, 2048)
    m["gam"] = at(18112, 1024)
    m["z"] = at(18112, 1024)
    m["a_t"] = at(19136, 1024)
    m["yo_t"] = at(18112, 2048)
    m["l"] = at(20160, 1024)
    m["gt"] = at(21184, 1024)
    m["lm"] = [at(21184, 1024), at(22208, 1024)]
    m["y"] = at(23232, 1024)
    m["yt"] = at(24256, 1024)
    b = 25280
    for name, n in (("lb", 256), ("tb", 256), ("tbt", 256), ("tmp", 64), ("xn", 256), ("h_t", 128), ("tri", 64),
                    ("strict", 64), ("mask", 128), ("g", 16), ("beta", 16), ("t1", 16), ("t2", 16),
                    ("t3", 16), ("cg", 16), ("ea", 16), ("rn", 16)):
        m[name] = at(b, n)
        b += n
    m["xn"] = m["xn"][0:S, :]
    m["far"] = m["lb"][:, 0:S]
    m["row"] = m["lb"][:, S:2 * S]
    m["down"] = at(0, 8192)
    m["hx"] = at(8384, 2304)
    m["hx_t"] = at(10688, 2304)
    m["half"] = at(13504, 256)
    m["route"] = at(13760, 128)
    m["base_up"] = at(20160, 2048)
    m["base_down"] = at(22208, 1024)


SECOND = """wqkv_in normed ct_half cn_half ss_eps o_scaled out_ready wz_in wout_in up_in down_in base_in hT_done
    hT_ready ba_done gates_act gates_b g_ready cg_done cg_ready gt_ready cgb_done tok_mm tok_in turn_mm
    raw_in pad_ready tap1_ready tap_ready conv_ready silu_ready z_mm z_silu sq_ready sq_mm norm_in
    norm_pow norm_diag norm_bc normed_qk vT_done bv_ready gam_diff gam_ready l_masked kk_done at_ready
    l_ready blocks_moved y_in yt_in y_zero inverse_ready lm_ready cy_mm cy_in d_mm y_new u_mm u_in o_mm o_ready
    yn_ready yoT_done yoT_in out_mm half_in fold_done x2_ready logit_done r_exp comb_ready up_mm
    gate_silu hid_ready hidT_done hidT_in down_mm""".split()
EXPERT_ORDER = [EXPERTS] + list(range(EXPERTS))
OUT_BANK = [6, 7, 0, 1]
BLK = 16


def second_loads(sp, s, t, m, wide, mid):
    sp.wait_ge(s["proj_done"], 1)
    sp.dma_start(mid[:, :], t["W_z"], max_dma_last_dim=8192).then_inc(s["wz_in"], 16)
    sp.wait_ge(s["l_ready"], 2)
    sp.dma_start(t["l_blocks"], m["l"]).then_inc(s["blocks_moved"], 16)
    sp.wait_ge(s["blocks_moved"], 16)
    rows = t["l_blocks"].rearrange("r (p c) -> r p c", c=S)
    for k in range(8):
        at, col = BLK * k, BLK * (k % 4)
        sp.dma_start(m["lb"][at:at + BLK, :].rearrange("p (r c) -> p r c", c=BLK),
                     rows[at:at + BLK, :, col:col + BLK].rearrange("r p c -> p r c")).then_inc(s["blocks_moved"], 16)
    sp.wait_ge(s["inverse_ready"], 1)
    sp.dma_start(t["inverses"][0], m["tb"]).then_inc(s["blocks_moved"], 16)
    sp.wait_ge(s["inverse_ready"], 2)
    sp.dma_start(t["inverses"][1], m["tbt"]).then_inc(s["blocks_moved"], 16)
    sp.wait_ge(s["blocks_moved"], (1 + 8 + 2) * 16)
    sp.wait_ge(s["y_zero"], 2)
    inverses_in(sp, m["y"], t["inverses"][1], s["y_in"])
    inverses_in(sp, m["yt"], t["inverses"][0], s["yt_in"])
    sp.wait_ge(s["z_mm"], 4)
    sp.dma_start(mid[:, :], t["W_out"], max_dma_last_dim=8192).then_inc(s["wout_in"], 16)
    sp.wait_ge(s["tok_mm"], 8)
    sp.dma_start(wide[:, :], t["up"], max_dma_last_dim=8192).then_inc(s["up_in"], 16)
    sp.wait_ge(s["bv_ready"], 4)
    sp.dma_start(m["down"], t["down"], max_dma_last_dim=8192).then_inc(s["down_in"], 16)
    sp.wait_ge(s["u_mm"], 4)
    sp.dma_start(m["base_up"], t["base_up"]).then_inc(s["base_in"], 16)
    sp.dma_start(m["base_down"], t["base_down"]).then_inc(s["base_in"], 16)


def inverses_in(queue, dst, src, arrived):
    for k in range(8):
        at, col = BLK * k, BLK * (k % 4)
        queue.dma_start(dst[at:at + BLK, :].rearrange("r (p c) -> r p c", c=S)[:, :, col:col + BLK],
                        src[at:at + BLK, :].rearrange("p (r c) -> r p c", c=BLK)).then_inc(arrived, 16)


def second_pool(pool, s, m, inv_root, ident, cst, small):
    pool.wait_ge(s["x1_ready"], 1)
    pool.memset(m["tri"], 1.0).then_inc(s["pool_step"], 1)
    pool.memset(m["strict"], 1.0).then_inc(s["pool_step"], 1)
    pool.memset(m["raw"][:, :, 0:3], 0.0).then_inc(s["pad_ready"], 1)
    pool.wait_ge(s["pool_step"], 5)
    pool.wait_ge(s["pad_ready"], 1)
    for k, r in enumerate(HALVES):
        for name, op, pattern, mul in (("tri", ALU.is_ge, [[1, S]], -1), ("strict", ALU.is_gt, [[-1, S]], 1)):
            pool.affine_select(out=m[name][r, :], in_=m[name][r, :], compare_op=op, fill=0.0, base=0,
                               pattern=pattern, channel_multiplier=mul).then_inc(s["pool_step"], 1)
        pool.iota(m["row"][r, :].bitcast(I32), [[0, S]], base=0, channel_multiplier=1).then_inc(s["pool_step"], 1)
        pool.wait_ge(s["pool_step"], 5 + 3 * (k + 1))
    pool.iota(m["far"].bitcast(I32), [[1, S]], base=0, channel_multiplier=0).then_inc(s["pool_step"], 1)
    pool.wait_ge(s["pool_step"], 12)
    inv_root(m["stat"][0:S, 8:9], m["stat"][0:S, 7:8], S, 1)
    w = small[:, SMALL["conv"][0]:SMALL["conv"][0] + 256].rearrange("p (c j) -> p c j", j=4)

    def first_tap(n):
        c = slice(8 * n, 8 * n + 8)
        pool.wait_ge(s["raw_in"], n + 1)
        if n >= 2:
            pool.wait_ge(s["conv_ready"], n - 1)
        pool.tensor_tensor(m["tap0"][:, n % 2, :].rearrange("p (c t) -> p c t", t=S), m["raw"][:, c, 0:S],
                           w[:, c, 0:1].broadcast_to([128, 8, S]), ALU.mult).then_inc(s["pool_step"], 1)
        pool.wait_ge(s["pool_step"], 12 + n + 1)
        pool.wait_ge(s["tap1_ready"], n + 1)
        pool.tensor_tensor(m["tap0"][:, n % 2, :], m["tap0"][:, n % 2, :], m["tap1"][:, n % 2, :],
                           ALU.add).then_inc(s["tap_ready"], 1)

    for n in range(4):
        first_tap(n)
    pool.wait_ge(s["norm_in"], 1)
    pool.tensor_tensor(m["rn"], m["rn"], cst[:, 0:1].broadcast_to([128, 16]), ALU.pow).then_inc(s["norm_pow"], 1)
    for q in range(2):
        pool.wait_ge(s["gam_ready"], q + 1)
        pool.tensor_tensor(by_head(m["l"], q), by_head(m["gam"], q), over_heads(m["strict"]),
                           ALU.mult).then_inc(s["l_masked"], 1)
    pool.memset(m["y"], 0.0).then_inc(s["y_zero"], 1)
    pool.memset(m["yt"], 0.0).then_inc(s["y_zero"], 1)
    first_tap(4)
    first_tap(5)
    pool.wait_ge(s["cgb_done"], 1)
    pool.wait_ge(s["l_ready"], 2)
    for lv in range(2):
        for q in range(2):
            pool.tensor_tensor(by_head(m["lm"][lv], q), by_head(m["l"], q), over_heads(m["mask"][:, S * lv:S * lv + S]),
                               ALU.mult).then_inc(s["lm_ready"], 1)
    first_tap(6)
    first_tap(7)
    for n in range(4):
        pool.wait_ge(s["norm_in"], 1 + n + 1)
        rn = m["rn"][:, 4 * n:4 * n + 4]
        pool.tensor_tensor(rn, rn, cst[:, 0:1].broadcast_to([128, 4]), ALU.pow).then_inc(s["norm_pow"], 1)
    inv_root(m["stat"][0:S, 8:9], m["stat"][0:S, 7:8], S, 1)


def by_head(a, q):
    return a[:, 512 * q:512 * q + 512].rearrange("p (h t) -> p h t", t=S)


def over_heads(a):
    return a.unsqueeze(1).broadcast_to([a.shape[0], 8, a.shape[1]])


def over_tokens(a, q):
    return a[:, 8 * q:8 * q + 8].unsqueeze(2).broadcast_to([a.shape[0], 8, S])


def second_scalar(act, s, m, bank, small):
    def to_rows(n):
        act.wait_ge(s["tok_mm"], n + 1)
        if n >= 2:
            act.wait_ge(s["turn_mm"], n - 1)
        act.copy(m["tok"][:, n % 2, :], bank[n % 2]).then_inc(s["tok_in"], 1)

    def to_channels(n):
        act.wait_ge(s["turn_mm"], n + 1)
        dst = m["raw"][:, 8 * n:8 * n + 8, 3:S + 3].rearrange("p (e k) t -> p e k t", e=2)
        act.copy(dst, bank[2 + n % 2].rearrange("p (k e t) -> p e k t", e=2, t=S)).then_inc(s["raw_in"], 1)

    def silu(n):
        c = m["cv"][:, 512 * n:512 * n + 512]
        act.wait_ge(s["conv_ready"], n + 1)
        act.activation(c, c, ACT.Silu).then_inc(s["silu_ready"], 1)

    act.wait_ge(s["ba_done"], 1)
    act.activation(m["t1"], bank[6][:, 0:16], ACT.Exp, scale=-1.0).then_inc(s["gates_act"], 1)
    a = SMALL["A_log"][0]
    act.activation(m["ea"], small[:, a:a + 16], ACT.Exp).then_inc(s["gates_act"], 1)
    to_rows(0)
    act.wait_ge(s["gates_b"], 1)
    act.activation(m["t3"], m["t3"], ACT.Exp, scale=-1.0).then_inc(s["gates_act"], 1)
    act.wait_ge(s["gates_act"], 3)
    act.activation(m["t3"], m["t3"], ACT.Ln, bias=m["stat"][:, 15:16]).then_inc(s["gates_act"], 1)
    act.wait_ge(s["pad_ready"], 1)
    to_rows(1)
    to_channels(0)
    to_rows(2)
    to_channels(1)
    to_rows(3)
    to_channels(2)
    to_channels(3)
    for n in range(4):
        silu(n)
        act.wait_ge(s["silu_ready"], n + 1)
        act.activation(m["sq"][:, 512 * n:512 * n + 512], m["cv"][:, 512 * n:512 * n + 512], ACT.Square)\
           .then_inc(s["sq_ready"], 1)
        if n < 3:
            to_rows(4 + n)
            if n:
                to_channels(3 + n)
    to_rows(7)
    for q in range(2):
        gq = m["gam"][:, 512 * q:512 * q + 512]
        act.wait_ge(s["gam_diff"], q + 1)
        act.activation(gq, gq, ACT.Exp, scale=-1.0).then_inc(s["gam_ready"], 1)
    to_channels(6)
    to_channels(7)
    for n in range(4):
        act.wait_ge(s["z_mm"], n + 1)
        act.activation(m["zs"][:, 512 * n:512 * n + 512], bank[4 + n % 2], ACT.Silu).then_inc(s["z_silu"], 1)
    for n in range(4, 8):
        silu(n)
    for lv in range(2):
        for q in range(2):
            act.wait_ge(s["cy_mm"], 2 * lv + q + 1)
            if lv:
                act.wait_ge(s["d_mm"], q + 1)
            act.copy(m["z"][:, 512 * q:512 * q + 512], bank[4 + q]).then_inc(s["cy_in"], 1)
    for n in range(4):
        act.wait_ge(s["u_mm"], n + 1)
        act.copy(m["u"][:, 512 * n:512 * n + 512], bank[2 + n]).then_inc(s["u_in"], 1)
    for n in range(4):
        c = slice(512 * n, 512 * n + 512)
        act.wait_ge(s["o_ready"], n + 1)
        act.activation(m["sq"][:, c], m["yo"][:, c], ACT.Square).then_inc(s["sq_ready"], 1)
    a = SMALL["norm_w"][0]
    for n in range(4):
        act.wait_ge(s["yoT_done"], n + 1)
        act.activation(m["yo_t"][:, 512 * n:512 * n + 512], bank[2 + n], ACT.Identity, scale=small[:, a:a + 1])\
           .then_inc(s["yoT_in"], 1)
    act.wait_ge(s["logit_done"], 2)
    act.activation(m["route"][:, 0:8], m["route"][:, 0:8], ACT.Exp).then_inc(s["r_exp"], 1)
    for n in range(9):
        act.wait_ge(s["up_mm"], n + 1)
        act.activation(m["hx"][:, 256 * n:256 * n + 256], bank[2 + n % 4][:, 0:256], ACT.Silu).then_inc(s["gate_silu"], 1)
        if n:
            hidden_turned(act, s, m, bank, n - 1)
    hidden_turned(act, s, m, bank, 8)


def hidden_turned(act, s, m, bank, n):
    act.wait_ge(s["hidT_done"], n + 1)
    act.copy(m["hx_t"][:, 256 * n:256 * n + 256], bank[6 + n % 2][:, 0:256]).then_inc(s["hidT_in"], 1)


def second_vector(dve, s, m, v, layernorm_rows, bank, small, x_res, ident):
    layernorm_rows(m["xn"], x_res[:, :])
    dve.wait_ge(s["hT_done"], 1)
    dve.tensor_copy(m["h_t"], bank[7][:, 0:128]).then_inc(s["hT_ready"], 1)
    v.by(dve.memset(m["stat"][:, 15:16], 1.0))
    dve.wait_ge(s["ba_done"], 1)
    dve.wait_ge(s["gates_act"], 1)
    a = SMALL["dt_bias"][0]
    v.settle(dve, dve.tensor_tensor(m["t2"], bank[6][:, 16:32], small[:, a:a + 16], ALU.add))
    dve.scalar_tensor_tensor(out=m["t3"], in0=m["t2"], scalar=-1.0, in1=m["t2"], op0=ALU.mult, op1=ALU.max)\
       .then_inc(s["gates_b"], 1)
    v.settle(dve, dve.tensor_scalar(m["t1"], m["t1"], 1.0, None, ALU.add))
    v.by(dve.reciprocal(m["beta"], m["t1"]))
    dve.wait_ge(s["pool_step"], 12)
    far, mask = m["far"], m["mask"]
    v.settle(dve, dve.tensor_tensor(far.bitcast(I32), far.bitcast(I32), m["row"].bitcast(I32), ALU.bitwise_xor))
    v.settle(dve, dve.tensor_copy(far, far.bitcast(I32)))
    v.settle(dve, dve.tensor_scalar(mask[:, 0:S], far, float(BLK), None, ALU.is_ge))
    v.by(dve.scalar_tensor_tensor(out=mask[:, 0:S], in0=far, scalar=float(2 * BLK), in1=mask[:, 0:S],
                                  op0=ALU.is_lt, op1=ALU.mult))
    v.by(dve.tensor_scalar(mask[:, S:2 * S], far, float(2 * BLK), None, ALU.is_ge))
    dve.wait_ge(s["gates_act"], 4)
    v.settle(dve, dve.scalar_tensor_tensor(out=m["t3"], in0=m["t2"], scalar=0.0, in1=m["t3"], op0=ALU.max, op1=ALU.add))
    dve.scalar_tensor_tensor(out=m["g"], in0=m["t3"], scalar=-1.0, in1=m["ea"], op0=ALU.mult, op1=ALU.mult)\
       .then_inc(s["g_ready"], 1)
    dve.wait_ge(s["g_ready"], 1)
    for q in range(2):
        dve.tensor_tensor(by_head(m["gt"], q), over_tokens(m["g"], q), over_heads(m["tri"]), ALU.mult)\
           .then_inc(s["gt_ready"], 1)
    w = small[:, SMALL["conv"][0]:SMALL["conv"][0] + 256].rearrange("p (c j) -> p c j", j=4)

    def tap(out, n, j):
        c = slice(8 * n, 8 * n + 8)
        return dve.tensor_tensor(out.rearrange("p (c t) -> p c t", t=S), m["raw"][:, c, j:S + j],
                                 w[:, c, j:j + 1].broadcast_to([128, 8, S]), ALU.mult)

    def convolve(n):
        out = m["cv"][:, 512 * n:512 * n + 512]
        dve.wait_ge(s["raw_in"], n + 1)
        if n >= 2:
            dve.wait_ge(s["tap_ready"], n - 1)
        tap(m["tap1"][:, n % 2, :], n, 1).then_inc(s["tap1_ready"], 1)
        v.by(tap(out, n, 3))
        v.settle(dve, tap(m["tap2"], n, 2))
        v.settle(dve, dve.tensor_tensor(out, out, m["tap2"], ALU.add))
        dve.wait_ge(s["tap_ready"], n + 1)
        dve.tensor_tensor(out, out, m["tap0"][:, n % 2, :], ALU.add).then_inc(s["conv_ready"], 1)

    convolve(0)
    convolve(1)
    dve.wait_ge(s["cg_done"], 1)
    dve.tensor_copy(m["cg"], bank[6][:, 32:48]).then_inc(s["cg_ready"], 1)
    dve.wait_ge(s["cg_ready"], 1)
    dve.wait_ge(s["cgb_done"], 1)
    for q in range(2):
        v.settle(dve, dve.tensor_tensor(by_head(m["gam"], q), by_head(bank[4 + q], 0), over_tokens(m["cg"], q),
                                        ALU.subtract))
        gq = m["gam"][:, 512 * q:512 * q + 512]
        dve.scalar_tensor_tensor(out=gq, in0=gq, scalar=-1.0, in1=gq, op0=ALU.mult, op1=ALU.max).then_inc(s["gam_diff"], 1)
    for n in range(2, 4):
        convolve(n)

    def diagonals(n):
        return dve.tensor_tensor(m["sq"][:, 512 * n:512 * n + 512].rearrange("p (k t) -> p k t", k=4),
                                 m["rn"][:, 4 * n:4 * n + 4].unsqueeze(2).broadcast_to([128, 4, 128]),
                                 ident[:, :].unsqueeze(1).broadcast_to([128, 4, 128]), ALU.mult)

    dve.wait_ge(s["sq_mm"], 1)
    dve.tensor_scalar(m["rn"], bank[7][:, 0:16], 1e-24, None, ALU.max).then_inc(s["norm_in"], 1)
    for q in range(2):
        dve.wait_ge(s["gam_ready"], q + 1)
        v.by(dve.tensor_tensor(by_head(m["a_t"], q), by_head(m["gam"], q), over_heads(m["tri"]), ALU.mult))
    dve.wait_ge(s["norm_pow"], 1)
    for n in range(4):
        diagonals(n).then_inc(s["norm_diag"], 1)
    for n in range(4):
        dve.wait_ge(s["norm_bc"], n + 1)
        c = m["cv"][:, 512 * n:512 * n + 512]
        dve.tensor_tensor(c, c, bank[4 + n % 2], ALU.mult).then_inc(s["normed_qk"], 1)
    for q in range(2):
        dve.wait_ge(s["l_masked"], q + 1)
        v.by(dve.tensor_tensor(by_head(m["l"], q), by_head(m["l"], q), over_tokens(m["beta"], q), ALU.mult))
    dve.wait_ge(s["kk_done"], 1)
    v.by(dve.memset(m["tb"], 0.0))
    dve.wait_ge(s["dve_step"], v.n)
    for name, b, done in (("l", 6, "l_ready"), ("a_t", 7, "at_ready")):
        for q in range(2):
            pair = m[name][:, 512 * q:512 * q + 512].rearrange("p (k e t) -> p k e t", e=2, t=S)
            prod = bank[b][:, 256 * q:256 * q + 256].rearrange("p (k t) -> p k t", t=S)
            dve.tensor_tensor(pair, pair, prod.unsqueeze(2).broadcast_to([128, 4, 2, S]), ALU.mult).then_inc(s[done], 1)
    convolve(4)
    convolve(5)
    lb = m["lb"].rearrange("p (r c) -> p r c", c=BLK)
    tb = m["tb"].rearrange("p (r c) -> p r c", c=BLK)
    v.by(dve.memset(m["tb"][:, 0:BLK * BLK:BLK + 1], 1.0))
    dve.wait_ge(s["blocks_moved"], (1 + 8) * 16)
    dve.wait_ge(s["dve_step"], v.n)
    for j in range(BLK - 1):
        below, done = BLK - 1 - j, j + 1
        tmp = m["tmp"][:, 0:below * done].rearrange("p (r c) -> p r c", c=done)
        rows = tb[:, j + 1:BLK, 0:done]
        v.settle(dve, dve.tensor_tensor(tmp, lb[:, j + 1:BLK, j:j + 1].broadcast_to([128, below, done]),
                                        tb[:, j:j + 1, 0:done].broadcast_to([128, below, done]), ALU.mult))
        ins = dve.tensor_tensor(rows, rows, tmp, ALU.subtract)
        if j < BLK - 2:
            v.settle(dve, ins)
    ins.then_inc(s["inverse_ready"], 1)
    dve.wait_ge(s["inverse_ready"], 1)
    dve.tensor_copy(m["tbt"].rearrange("p (c r) -> p r c", r=BLK), tb).then_inc(s["inverse_ready"], 1)
    convolve(6)
    convolve(7)

    def weigh_values(n):
        dve.wait_ge(s["vT_done"], n + 1)
        dve.tensor_tensor(m["bv"][:, 512 * n:512 * n + 512].rearrange("p (h d) -> p h d", d=D),
                          bank[2 + n % 2].rearrange("p (h d) -> p h d", d=D),
                          m["beta"][:, 4 * n:4 * n + 4].unsqueeze(2).broadcast_to([128, 4, D]), ALU.mult)\
           .then_inc(s["bv_ready"], 1)

    weigh_values(0)
    weigh_values(1)
    dve.wait_ge(s["y_in"], 8 * 16)
    dve.wait_ge(s["yt_in"], 8 * 16)
    for q in range(2):
        dve.wait_ge(s["d_mm"], q + 1)
        for name, b in (("y", 6 + q), ("yt", q)):
            a = m[name][:, 512 * q:512 * q + 512]
            dve.tensor_tensor(a, a, bank[b], ALU.subtract).then_inc(s["y_new"], 1)
    weigh_values(2)
    dve.wait_ge(s["y_new"], 4)
    for q in range(2):
        dve.wait_ge(s["d_mm"], 2 + q + 1)
        a = m["y"][:, 512 * q:512 * q + 512]
        dve.tensor_tensor(a, a, bank[6 + q], ALU.subtract).then_inc(s["y_new"], 1)
    weigh_values(3)
    def gate(n):
        dve.wait_ge(s["o_mm"], n + 1)
        dve.wait_ge(s["z_silu"], n + 1)
        c = slice(512 * n, 512 * n + 512)
        dve.tensor_tensor(m["yo"][:, c], bank[OUT_BANK[n]], m["zs"][:, c], ALU.mult).then_inc(s["o_ready"], 1)

    def mean_square(n):
        dve.wait_ge(s["sq_ready"], 4 + n + 1)
        rn = m["rn"][:, 4 * n:4 * n + 4]
        v.settle(dve, dve.tensor_reduce(rn, m["sq"][:, 512 * n:512 * n + 512].rearrange("p (h d) -> p h d", d=D), X, ALU.add))
        dve.tensor_scalar(rn, rn, 1.0 / D, 1e-6, ALU.mult, ALU.add).then_inc(s["norm_in"], 1)

    def normalise(n):
        dve.wait_ge(s["norm_pow"], 1 + n + 1)
        y = m["yo"][:, 512 * n:512 * n + 512].rearrange("p (h d) -> p h d", d=D)
        dve.tensor_tensor(y, y, m["rn"][:, 4 * n:4 * n + 4].unsqueeze(2).broadcast_to([128, 4, D]), ALU.mult)\
           .then_inc(s["yn_ready"], 1)

    gate(0)
    for n in range(1, 4):
        gate(n)
        mean_square(n - 1)
        if n >= 2:
            normalise(n - 2)
    normalise(2)
    mean_square(3)
    normalise(3)
    dve.wait_ge(s["out_mm"], 1)
    dve.tensor_copy(m["half"], bank[6][:, 0:H]).then_inc(s["half_in"], 1)
    dve.wait_ge(s["fold_done"], 2)
    dve.tensor_tensor(x_res[:, :], x_res[:, :], bank[7][0:S, 0:H], ALU.add).then_inc(s["x2_ready"], 1)
    dve.wait_ge(s["x2_ready"], 1)
    layernorm_rows(m["xn"], x_res[:, :])
    dve.wait_ge(s["hT_done"], 2)
    dve.tensor_copy(m["h_t"], bank[0][:, 0:128]).then_inc(s["hT_ready"], 1)
    r = m["route"]
    p, w1, w2, pos, pick, top, tot = (r[:, 8 * k:8 * k + 8] for k in range(7))

    def first_best(out, vals, best):
        v.settle(dve, dve.tensor_reduce(best, vals, X, ALU.max))
        v.settle(dve, dve.tensor_scalar(pick, vals, best, None, ALU.is_ge))
        v.settle(dve, dve.tensor_tensor(pick, pick, pos, ALU.mult))
        v.settle(dve, dve.tensor_reduce(tot[:, 7:8], pick, X, ALU.max))
        v.settle(dve, dve.tensor_scalar(out, pos, tot[:, 7:8], None, ALU.is_equal))

    for e in range(EXPERTS):
        v.by(dve.memset(pos[:, e:e + 1], float(EXPERTS - e)))
    dve.wait_ge(s["logit_done"], 1)
    lg = bank[1][:, 0:EXPERTS]
    v.settle(dve, dve.tensor_reduce(top[:, 0:1], lg, X, ALU.max))
    dve.tensor_scalar(p, lg, top[:, 0:1], None, ALU.subtract).then_inc(s["logit_done"], 1)
    dve.wait_ge(s["r_exp"], 1)
    v.settle(dve, dve.tensor_reduce(top[:, 1:2], p, X, ALU.add))
    v.settle(dve, dve.reciprocal(top[:, 1:2], top[:, 1:2]))
    v.settle(dve, dve.tensor_scalar(p, p, top[:, 1:2], None, ALU.mult))
    first_best(w1, p, top[:, 2:3])
    v.settle(dve, dve.scalar_tensor_tensor(out=w2, in0=w1, scalar=-2.0, in1=p, op0=ALU.mult, op1=ALU.add))
    v.settle(dve, dve.tensor_copy(r[:, 56:64], w2))
    first_best(w2, r[:, 56:64], top[:, 3:4])
    v.settle(dve, dve.tensor_tensor(top[:, 4:5], top[:, 2:3], top[:, 3:4], ALU.add))
    v.settle(dve, dve.reciprocal(top[:, 4:5], top[:, 4:5]))
    v.settle(dve, dve.tensor_tensor(w1, w1, w2, ALU.add))
    dve.scalar_tensor_tensor(out=p, in0=p, scalar=top[:, 4:5], in1=w1, op0=ALU.mult, op1=ALU.mult)\
       .then_inc(s["comb_ready"], 1)
    for n, e in enumerate(EXPERT_ORDER):
        dve.wait_ge(s["gate_silu"], n + 1)
        hx = m["hx"][:, 256 * n:256 * n + 256]
        up = bank[2 + n % 4][:, 256:512]
        if e == EXPERTS:
            dve.tensor_tensor(hx, hx, up, ALU.mult).then_inc(s["hid_ready"], 1)
            dve.wait_ge(s["comb_ready"], 1)
        else:
            dve.scalar_tensor_tensor(out=hx, in0=hx, scalar=p[:, e:e + 1], in1=up, op0=ALU.mult, op1=ALU.mult)\
               .then_inc(s["hid_ready"], 1)
    dve.wait_ge(s["down_mm"], 1)
    dve.tensor_copy(m["half"], bank[0][:, 0:H]).then_inc(s["half_in"], 1)
    dve.wait_ge(s["fold_done"], 3)
    dve.tensor_tensor(x_res[:, :], x_res[:, :], bank[1][0:S, 0:H], ALU.add).then_inc(s["out_ready"], 1)


def second_tensor(pe, s, m, bank, small, ident, ones, wide, mid):
    h_t = m["h_t"]

    def turn(out, done):
        for c in range(HC):
            ins = pe.transpose(out[:, c * S:c * S + S], m["xn"][:, 128 * c:128 * c + 128], ident[0:S, 0:S])
        ins.then_inc(s[done], 1)

    def fold_halves(out, n):
        pe.wait_ge(s["half_in"], n)
        pe.matmul(out, m["fold"][:, :], m["half"], start=True, stop=True).then_inc(s["fold_done"], 1)

    pe.wait_ge(s["normed"], 3)
    turn(bank[7], "hT_done")
    pe.wait_ge(s["hT_ready"], 1)
    a = SMALL["W_ba"][0]
    wba = small[:, a:a + 128].rearrange("p (c b h) -> p c b h", c=HC, b=2)
    gates = bank[6][:, 0:32].rearrange("p (b h) -> p b h", b=2)
    for c in range(HC):
        for e, r in enumerate(HALVES):
            ins = pe.matmul(gates[r], h_t[:, S * c:S * c + S], wba[:, c, :, 16 * e:16 * e + 16],
                            start=(c == 0), stop=(c == HC - 1))
    ins.then_inc(s["ba_done"], 1)
    pe.wait_ge(s["wqkv_in"], 16)
    wq = wide[:, :].rearrange("p (h n) -> p h n", h=HC)

    def rows_round(n):
        if n >= 2:
            pe.wait_ge(s["tok_in"], n - 1)
        for c in range(HC):
            for e, r in enumerate(HALVES):
                ch = 1024 * n + 512 * e
                ins = pe.matmul(bank[n % 2][r, :], h_t[:, S * c:S * c + S], wq[:, c, ch:ch + 512],
                                start=(c == 0), stop=(c == HC - 1))
        ins.then_inc(s["tok_mm"], 1)

    def turn_round(n):
        pe.wait_ge(s["tok_in"], n + 1)
        if n >= 2:
            pe.wait_ge(s["raw_in"], n - 1)
        for k in range(4):
            ins = pe.transpose(bank[2 + n % 2][:, 128 * k:128 * k + 128], m["tok"][:, n % 2, 128 * k:128 * k + 128], ident[:, :])
        ins.then_inc(s["turn_mm"], 1)

    rows_round(0)
    for n in range(1, 4):
        rows_round(n)
        turn_round(n - 1)
    turn_round(3)
    pe.wait_ge(s["g_ready"], 1)
    for r in HALVES:
        ins = pe.matmul(bank[6][r, 32:48], m["tri"][r, :], m["g"][r, :], start=True, stop=True)
    ins.then_inc(s["cg_done"], 1)
    pe.wait_ge(s["gt_ready"], 2)
    for q in range(2):
        for r in HALVES:
            ins = pe.matmul(bank[4 + q][r, :], ones[r, 0:S], m["gt"][r, 512 * q:512 * q + 512], start=True, stop=True)
    ins.then_inc(s["cgb_done"], 1)
    for n in range(4, 8):
        rows_round(n)
        if n > 4:
            turn_round(n - 1)
    for k in range(16):
        pe.wait_ge(s["sq_ready"], k // 4 + 1)
        ins = pe.matmul(bank[7][:, k:k + 1], m["sq"][:, 128 * k:128 * k + 128], ones[:, 0:1], start=True, stop=True)
    ins.then_inc(s["sq_mm"], 1)
    turn_round(7)
    pe.wait_ge(s["gam_diff"], 2)
    for n in range(4):
        pe.wait_ge(s["norm_diag"], n + 1)
        if n >= 2:
            pe.wait_ge(s["normed_qk"], n - 1)
        pe.matmul(bank[4 + n % 2], ones[:, :], m["sq"][:, 512 * n:512 * n + 512], start=True, stop=True)\
          .then_inc(s["norm_bc"], 1)
    pe.wait_ge(s["normed_qk"], 4)
    pe.wait_ge(s["cg_ready"], 1)
    for k in range(8):
        for other, b in ((NK, 6), (0, 7)):
            for e, r in enumerate(HALVES):
                h = 8 * e + k
                key = m["cv"][:, S * (NK + h):S * (NK + h) + S]
                ins = pe.matmul(bank[b][r, S * k:S * k + S], key, m["cv"][:, S * (other + h):S * (other + h) + S],
                                start=True, stop=True)
    ins.then_inc(s["kk_done"], 1)
    pe.wait_ge(s["wz_in"], 16)
    wz = mid[:, :].rearrange("p (h n) -> p h n", h=HC)
    for n in range(4):
        if n >= 2:
            pe.wait_ge(s["z_silu"], n - 1)
        for c in range(HC):
            for e, r in enumerate(HALVES):
                ch = 2048 * e + 512 * n
                ins = pe.matmul(bank[4 + n % 2][r, :], h_t[:, S * c:S * c + S], wz[:, c, ch:ch + 512],
                                start=(c == 0), stop=(c == HC - 1))
        ins.then_inc(s["z_mm"], 1)

    def turn_values(n):
        if n == 0:
            pe.wait_ge(s["raw_in"], 8)
        pe.wait_ge(s["silu_ready"], 7 + n // 2)
        if n >= 2:
            pe.wait_ge(s["bv_ready"], n - 1)
        for k in range(4):
            for e, r in enumerate(HALVES):
                at = 2048 + S * (16 * e + 4 * n + k)
                ins = pe.matmul(bank[2 + n % 2][r, D * k:D * k + D], m["cv"][:, at:at + S], ident[:, :], start=True, stop=True)
        ins.then_inc(s["vT_done"], 1)

    def pairs(out, lhs, rhs, ps, width):
        for i, p in enumerate(ps):
            for r in HALVES:
                ins = pe.matmul(out[r, width * i:width * i + width], lhs[r, S * p:S * p + S],
                                rhs[r, width * p:width * p + width], start=True, stop=True)
        return ins

    turn_values(0)
    turn_values(1)
    pe.wait_ge(s["y_in"], 8 * 16)
    pe.wait_ge(s["z_silu"], 4)
    pe.wait_ge(s["at_ready"], 2)
    for lv in range(2):
        for q in range(2):
            pe.wait_ge(s["lm_ready"], 2 * lv + q + 1)
            if lv:
                pe.wait_ge(s["y_new"], 2 * q + 1)
            pairs(bank[4 + q], m["lm"][lv], m["y"], range(8 * q, 8 * q + 8), S).then_inc(s["cy_mm"], 1)
        if lv == 0:
            pe.wait_ge(s["yt_in"], 8 * 16)
        for q in range(2):
            pe.wait_ge(s["cy_in"], 2 * lv + q + 1)
            if lv:
                pe.wait_ge(s["y_new"], 2 * q + 2)
            ps = range(8 * q, 8 * q + 8)
            ins = pairs(bank[6 + q], m["yt"], m["z"], ps, S)
            if lv == 0:
                ins = pairs(bank[q], m["z"], m["yt"], ps, S)
            ins.then_inc(s["d_mm"], 1)
        turn_values(2 + lv)
    pe.wait_ge(s["bv_ready"], 4)
    for n in range(4):
        pe.wait_ge(s["y_new"], 4 + n // 2 + 1)
        pairs(bank[2 + n], m["y"], m["bv"], range(4 * n, 4 * n + 4), D).then_inc(s["u_mm"], 1)
    pe.wait_ge(s["y_new"], 6)
    for n in range(4):
        pe.wait_ge(s["u_in"], n + 1)
        pairs(bank[OUT_BANK[n]], m["a_t"], m["u"], range(4 * n, 4 * n + 4), D).then_inc(s["o_mm"], 1)
    for n in range(4):
        pe.wait_ge(s["yn_ready"], n + 1)
        for k in range(4 * n, 4 * n + 4):
            ins = pe.transpose(bank[2 + n][:, 128 * (k % 4):128 * (k % 4) + 128], m["yo"][:, D * k:D * k + D], ident[:, :])
        ins.then_inc(s["yoT_done"], 1)
    pe.wait_ge(s["wout_in"], 16)
    for p in range(16):
        pe.wait_ge(s["yoT_in"], p // 4 + 1)
        for e, r in enumerate(HALVES):
            ins = pe.matmul(bank[6][r, 0:H], m["yo_t"][:, 128 * p + S * e:128 * p + S * e + S],
                            mid[:, H * (16 * e + p):H * (16 * e + p) + H], start=(p == 0), stop=(p == 15))
    ins.then_inc(s["out_mm"], 1)
    fold_halves(bank[7][0:S, 0:H], 2)
    pe.wait_ge(s["normed"], 4)
    turn(bank[0], "hT_done")
    pe.wait_ge(s["hT_ready"], 2)
    a = SMALL["gate"][0]
    for c in range(HC):
        for r in HALVES:
            ins = pe.matmul(bank[1][r, 0:EXPERTS], h_t[:, S * c:S * c + S], small[:, a + 8 * c:a + 8 * c + 8],
                            start=(c == 0), stop=(c == HC - 1))
    ins.then_inc(s["logit_done"], 1)
    pe.wait_ge(s["up_in"], 16)
    pe.wait_ge(s["base_in"], 32)

    def up(n):
        e = EXPERT_ORDER[n]
        w = (m["base_up"] if e == EXPERTS else wide[:, 2048 * e:2048 * e + 2048])\
            .rearrange("p (c b i) -> p c b i", c=HC, b=2)
        out = bank[2 + n % 4].rearrange("p (b i) -> p b i", b=2)
        if n >= 4:
            pe.wait_ge(s["hid_ready"], n - 3)
        for c in range(HC):
            for k, r in enumerate(HALVES):
                ins = pe.matmul(out[r], h_t[:, S * c:S * c + S], w[:, c, :, 256 * k:256 * k + 256],
                                start=(c == 0), stop=(c == HC - 1))
        ins.then_inc(s["up_mm"], 1)

    def turn_hidden(n):
        pe.wait_ge(s["hid_ready"], n + 1)
        if n >= 2:
            pe.wait_ge(s["hidT_in"], n - 1)
        for k in range(2):
            ins = pe.transpose(bank[6 + n % 2][:, 128 * k:128 * k + 128],
                               m["hx"][:, 256 * n + 128 * k:256 * n + 128 * k + 128], ident[:, :])
        ins.then_inc(s["hidT_done"], 1)

    def down(n):
        e = EXPERT_ORDER[n]
        w = m["base_down"] if e == EXPERTS else m["down"][:, 1024 * e:1024 * e + 1024]
        pe.wait_ge(s["hidT_in"], n + 1)
        if n == 1:
            pe.wait_ge(s["down_in"], 16)
        for k in range(2):
            for half, r in enumerate(HALVES):
                at, row = 256 * n + 128 * k + S * half, H * (2 * half + k)
                ins = pe.matmul(bank[0][r, 0:H], m["hx_t"][:, at:at + S], w[:, row:row + H],
                                start=(n == 0 and k == 0), stop=(n == 8 and k == 1))
        return ins

    for n in range(12):
        if n < 9:
            up(n)
        if 0 <= n - 2 < 9:
            turn_hidden(n - 2)
        if n >= 3:
            ins = down(n - 3)
    ins.then_inc(s["down_mm"], 1)
    fold_halves(bank[1][0:S, 0:H], 3)


def layout(i):
    f = lambda n: np.asarray(i[n])
    c = np.ascontiguousarray

    def by_width(w):
        return c(w.reshape(w.shape[0], HC, 128).transpose(2, 1, 0))

    def row(v):
        return np.broadcast_to(v.reshape(1, -1), (128, v.size))

    by_half = lambda v: np.repeat(v.reshape(2, NV // 2), S, axis=0)
    halves = lambda v: v.reshape(HC, 128).T
    a = "L0_xattn_"
    col = {"ln_w": halves(f(a + "ln_w")), "ln_b": halves(f(a + "ln_b")),
           "qx_in": halves(f(a + "qx_in_scale")), "q_in": halves(f(a + "q_in_scale")),
           "k_in": halves(f(a + "k_in_scale")), "v_in": halves(f(a + "v_in_scale")),
           "smooth": f(a + "proj_smooth").reshape(32, 128).T, "norm_w": f("L0_attn_norm_w").reshape(128, 1),
           "wqx_s": row(f(a + "wqx_scale")), "wq_s": row(f(a + "wq_scale")), "wk_s": row(f(a + "wk_scale")),
           "wv_s": row(f(a + "wv_scale")), "pw_s": row(f(a + "proj_w_scale")), "pin_s": row(f(a + "proj_in_scale")),
           "conv": f("L0_attn_conv_w").reshape(64, 128, 4).transpose(1, 0, 2).reshape(128, 256),
           "dt_bias": by_half(f("L0_attn_dt_bias")), "A_log": by_half(f("L0_attn_A_log")),
           "W_ba": by_width(np.concatenate([f("L0_attn_W_b"), f("L0_attn_W_a")])).reshape(128, 128),
           "gate": f("L0_ffn_gate_w").reshape(HC, 128, EXPERTS).transpose(1, 0, 2).reshape(128, 16)}
    for n in ("qxln", "qln", "kln", "kxln"):
        for e in "wb":
            col[f"{n}_{e}"] = f(f"{a}{n}_{e}").reshape(128, 1)
    ctx = f("ctx_2048").reshape(SC // 128, 128, H)
    kv = f(a + "w_kv_x")
    return {
        "x": c(f("x").reshape(S, H)),
        "small": c(np.concatenate([col[n] for n in SMALL], axis=1)),
        "wqx": by_width(f(a + "wqx")), "wq": by_width(f(a + "wq")), "wk": by_width(f(a + "wk")), "wv": by_width(f(a + "wv")),
        "kxT": by_width(kv[:1024]), "wvxT": by_width(kv[1024:]),
        "kxd": c(kv[:1024].reshape(G, D, H).transpose(1, 0, 2)),
        "ctT": c(ctx.reshape(SC // 128, 128, HC, 128).transpose(0, 3, 2, 1).reshape(SC // 128, 128, H)), "cn": c(ctx),
        "wprojT": c(f(a + "wproj").reshape(H, 32, 128).transpose(2, 1, 0).reshape(128, 8192)),
        "W_qkv": by_width(f("L0_attn_W_qkv")).reshape(128, 16384),
        "W_z": by_width(f("L0_attn_W_z")).reshape(128, 8192),
        "W_out": c(f("L0_attn_W_out").reshape(H, 32, 128).transpose(2, 1, 0).reshape(128, 8192)),
        "up": c(f("L0_ffn_expert_gate_up").reshape(EXPERTS, HC, 128, 1024).transpose(2, 0, 1, 3).reshape(128, 16384)),
        "down": c(f("L0_ffn_expert_down").reshape(EXPERTS, 4, 128, H).transpose(2, 0, 1, 3).reshape(128, 8192)),
        "base_up": c(f("L0_ffn_base_gate_up").reshape(HC, 128, 1024).transpose(1, 0, 2).reshape(128, 2048)),
        "base_down": c(f("L0_ffn_base_down").reshape(4, 128, H).transpose(1, 0, 2).reshape(128, 1024)),
    }


def kernel(**inputs):
    import concourse.bacc as bacc
    from concourse.bass_utils import run_bass_kernel_spmd

    nc = bacc.Bacc("TRN2", target_bir_lowering=False, num_devices=1)
    arrays = layout(inputs)
    t = {n: nc.dram_tensor("in_" + n, a.shape, F32, kind="ExternalInput").ap() for n, a in arrays.items()}
    t["out"] = nc.dram_tensor("out", (S, H), F32, kind="ExternalOutput").ap()
    build(nc, t)
    r = run_bass_kernel_spmd(nc, [{"in_" + n: a for n, a in arrays.items()}], core_ids=[0])
    return r.results[0]["out"].reshape(1, S, H)
```
